# Optimizing a Trainium2 kernel written in Bass

```python
import numpy as np
import jax
import jax.numpy as jnp

def _softmax(x, axis=-1):
    return jax.nn.softmax(x, axis=axis)

def _gelu(x):
    return jax.nn.gelu(x, approximate=True)

def _silu(x):
    return jax.nn.silu(x)

def _sigmoid(x):
    return jax.nn.sigmoid(x)

def _layernorm(x, axis=-1, eps=1e-05):
    m = jnp.mean(x, axis=axis, keepdims=True)
    v = jnp.var(x, axis=axis, keepdims=True)
    return (x - m) / jnp.sqrt(v + eps)

def _scatter_add(tgt, idx, src, axis=0):
    return tgt.at[idx].add(src)

def _segment_sum(src, seg, n):
    return jax.ops.segment_sum(src, seg, n)
kernel_name = 'mk_xattn_ffn_d2_seqx_r2_0893ce'

def setup_inputs(seed: int=0):
    np.random.seed(seed)
    _w = jnp.asarray

    def _rec_inputs():
        import jax
        import jax.numpy as jnp
        _rk = jax.random.key(seed)
        x = -0.0002928 + 1 * jax.random.normal(jax.random.fold_in(_rk, 1), (2, 2048, 512), jnp.float32)
        _lenS = 2048 - jax.random.randint(jax.random.fold_in(_rk, 7), (2,), 0, max(1, 2048 // 4) + 1, jnp.int32)
        _lenS2 = 154 - jax.random.randint(jax.random.fold_in(_rk, 8), (2,), 0, max(1, 154 // 4) + 1, jnp.int32)
        _ctx_1024P = jax.random.normal(jax.random.fold_in(_rk, 11), (2, 16, 512), jnp.float32)
        _ctx_1024c = jax.random.dirichlet(jax.random.fold_in(_rk, 511), 0.3 * jnp.ones((16,), jnp.float32), (2, 154))
        _ctx_1024t = jnp.einsum('bsk,bkd->bsd', _ctx_1024c, _ctx_1024P)
        _ctx_1024t = _ctx_1024t * jax.lax.rsqrt(jnp.mean(jnp.square(_ctx_1024t)) + 1e-12) * 0.953939
        ctx_1024 = -1.39393e-06 + 0.999914 * (_ctx_1024t + 0.3 * jax.random.normal(jax.random.fold_in(_rk, 611), (2, 154, 512), jnp.float32))
        _validS = jnp.arange(2048)[None, :] < _lenS[:, None]
        _validS2 = jnp.arange(154)[None, :] < _lenS2[:, None]
        _causal = jnp.tril(jnp.ones((2048, 2048), dtype=bool))
        mask_Bx1xSxS2_ff0 = jnp.where(jnp.ones((2, 1, 2048, 154), dtype=bool), 0.0, -1000000000.0).astype(jnp.float32)
        return (x, ctx_1024, mask_Bx1xSxS2_ff0)
    x, ctx_1024, mask_Bx1xSxS2_ff0 = _rec_inputs()

    def _L0_xattn_setup():
        import jax, jax.numpy as jnp
        import numpy as np
        HIDDEN = 512
        NUM_HEADS = 16
        HEAD_DIM = HIDDEN // NUM_HEADS
        B, F, T = (2, 1024, 1024)
        key = jax.random.key(seed)
        ks = jax.random.split(key, 6)
        return {'query_input': jax.random.normal(ks[0], (B, F, HIDDEN), dtype=jnp.float32), 'source_input': jax.random.normal(ks[1], (B, T, HIDDEN), dtype=jnp.float32), 'bias': jnp.zeros((B, 1, F, T), dtype=jnp.float32), 'wq': jax.random.normal(ks[2], (HIDDEN, NUM_HEADS, HEAD_DIM), dtype=jnp.float32) * (1.0 / np.sqrt(HIDDEN)), 'wk': jax.random.normal(ks[3], (HIDDEN, NUM_HEADS, HEAD_DIM), dtype=jnp.float32) * (1.0 / np.sqrt(HIDDEN)), 'wv': jax.random.normal(ks[4], (HIDDEN, NUM_HEADS, HEAD_DIM), dtype=jnp.float32) * (1.0 / np.sqrt(HIDDEN)), 'wo': jax.random.normal(ks[5], (NUM_HEADS, HEAD_DIM, HIDDEN), dtype=jnp.float32) * (1.0 / np.sqrt(HIDDEN))}
    _L0_xattn_all = _L0_xattn_setup()
    _L0_xattn_in = {k: v for k, v in _L0_xattn_all.items() if k in ('wq', 'wk', 'wv', 'wo')}
    del _L0_xattn_all

    def _L0_ffn_setup():
        import jax, jax.numpy as jnp
        import numpy as np
        B, L, C1, C2, K, K_IN = (4, 512, 512, 512, 32, 32)
        BN_EPS = 1e-05

        def _gated_bottleneck(x2d, conv_w, conv_b, gamma, beta, lin_w, lin_b):
            n = x2d.shape[0]
            g = conv_w.shape[0]
            xc = jnp.einsum('ngf,gf->ng', x2d.reshape(n, g, 4), conv_w) + conv_b
            mean = jnp.mean(xc, axis=0)
            var = jnp.mean((xc - mean) ** 2, axis=0)
            xn = (xc - mean) * jax.lax.rsqrt(var + BN_EPS) * gamma + beta
            xa = jax.nn.gelu(xn, approximate=False)
            return xa @ lin_w.T + lin_b
        key = jax.random.key(seed)
        ks = jax.random.split(key, 8)
        g = C1 // 4
        w_std = (2.0 / C2) ** 0.5
        lin_std = (1.0 / g) ** 0.5
        return {'x': jax.random.normal(ks[0], (B, L, C1), jnp.float32), 'weight': jax.random.normal(ks[1], (C1, C2), jnp.float32) * w_std, 'bias': jnp.zeros((C2,), jnp.float32), 'so_conv_w': jax.random.normal(ks[2], (g, 4), jnp.float32) * 0.5, 'so_conv_b': jnp.zeros((g,), jnp.float32), 'so_gamma': jnp.ones((g,), jnp.float32), 'so_beta': jnp.zeros((g,), jnp.float32), 'so_lin_w': jax.random.normal(ks[3], (C2, g), jnp.float32) * lin_std, 'so_lin_b': jnp.zeros((C2,), jnp.float32), 'si_conv_w': jax.random.normal(ks[4], (g, 4), jnp.float32) * 0.5, 'si_conv_b': jnp.zeros((g,), jnp.float32), 'si_gamma': jnp.ones((g,), jnp.float32), 'si_beta': jnp.zeros((g,), jnp.float32), 'si_lin_w': jax.random.normal(ks[5], (C1, g), jnp.float32) * lin_std, 'si_lin_b': jnp.zeros((C1,), jnp.float32)}
    _L0_ffn_all = _L0_ffn_setup()
    _L0_ffn_in = {k: v for k, v in _L0_ffn_all.items() if k in ('weight', 'bias', 'so_conv_w', 'so_conv_b', 'so_gamma', 'so_beta', 'so_lin_w', 'so_lin_b', 'si_conv_w', 'si_conv_b', 'si_gamma', 'si_beta', 'si_lin_w', 'si_lin_b')}
    del _L0_ffn_all

    def _L1_xattn_setup():
        import jax, jax.numpy as jnp
        import numpy as np
        D_MODEL = 512
        N_HEADS = 16
        D_K = D_MODEL // N_HEADS
        B, S = (4, 1024)
        key = jax.random.key(seed)
        ks = jax.random.split(key, 11)
        scale = 1.0 / np.sqrt(D_MODEL)
        inp = {'query': jax.random.normal(ks[0], (B, S, D_MODEL), jnp.float32), 'key_': jax.random.normal(ks[1], (B, S, D_MODEL), jnp.float32), 'value': jax.random.normal(ks[2], (B, S, D_MODEL), jnp.float32), 'W_Q': jax.random.normal(ks[3], (D_MODEL, D_MODEL), jnp.float32) * scale, 'b_Q': jnp.zeros((D_MODEL,), jnp.float32), 'W_K': jax.random.normal(ks[4], (D_MODEL, D_MODEL), jnp.float32) * scale, 'b_K': jnp.zeros((D_MODEL,), jnp.float32), 'W_V': jax.random.normal(ks[5], (D_MODEL, D_MODEL), jnp.float32) * scale, 'b_V': jnp.zeros((D_MODEL,), jnp.float32), 'W_O': jax.random.normal(ks[6], (D_MODEL, D_MODEL), jnp.float32) * scale, 'b_O': jnp.zeros((D_MODEL,), jnp.float32)}
        return inp
    _L1_xattn_all = _L1_xattn_setup()
    _L1_xattn_in = {k: v for k, v in _L1_xattn_all.items() if k in ('W_Q', 'b_Q', 'W_K', 'b_K', 'W_V', 'b_V', 'W_O', 'b_O')}
    del _L1_xattn_all

    def _L1_ffn_setup():
        import jax, jax.numpy as jnp
        import numpy as np
        B, S, H, I, E = (2, 2048, 512, 256, 8)
        key = jax.random.key(seed)
        ks = jax.random.split(key, 5)
        scale_h = 1.0 / np.sqrt(H)
        scale_i = 1.0 / np.sqrt(I)
        return {'hidden_states': jax.random.normal(ks[0], (B, S, H), dtype=jnp.float32), 'gate_w': jax.random.normal(ks[1], (E, H), dtype=jnp.float32) * scale_h, 'w_gate': jax.random.normal(ks[2], (E, I, H), dtype=jnp.float32) * scale_h, 'w_up': jax.random.normal(ks[3], (E, I, H), dtype=jnp.float32) * scale_h, 'w_down': jax.random.normal(ks[4], (E, H, I), dtype=jnp.float32) * scale_i}
    _L1_ffn_all = _L1_ffn_setup()
    _L1_ffn_in = {k: v for k, v in _L1_ffn_all.items() if k in ('gate_w', 'w_gate', 'w_up', 'w_down')}
    del _L1_ffn_all
    return {'x': x, 'ctx_1024': ctx_1024, 'mask_Bx1xSxS2_ff0': mask_Bx1xSxS2_ff0, 'L0_xattn_wq': _L0_xattn_in['wq'], 'L0_xattn_wk': _L0_xattn_in['wk'], 'L0_xattn_wv': _L0_xattn_in['wv'], 'L0_xattn_wo': _L0_xattn_in['wo'], 'L0_ffn_weight': _L0_ffn_in['weight'], 'L0_ffn_bias': _L0_ffn_in['bias'], 'L0_ffn_so_conv_w': _L0_ffn_in['so_conv_w'], 'L0_ffn_so_conv_b': _L0_ffn_in['so_conv_b'], 'L0_ffn_so_gamma': _L0_ffn_in['so_gamma'], 'L0_ffn_so_beta': _L0_ffn_in['so_beta'], 'L0_ffn_so_lin_w': _L0_ffn_in['so_lin_w'], 'L0_ffn_so_lin_b': _L0_ffn_in['so_lin_b'], 'L0_ffn_si_conv_w': _L0_ffn_in['si_conv_w'], 'L0_ffn_si_conv_b': _L0_ffn_in['si_conv_b'], 'L0_ffn_si_gamma': _L0_ffn_in['si_gamma'], 'L0_ffn_si_beta': _L0_ffn_in['si_beta'], 'L0_ffn_si_lin_w': _L0_ffn_in['si_lin_w'], 'L0_ffn_si_lin_b': _L0_ffn_in['si_lin_b'], 'L1_xattn_W_Q': _L1_xattn_in['W_Q'], 'L1_xattn_b_Q': _L1_xattn_in['b_Q'], 'L1_xattn_W_K': _L1_xattn_in['W_K'], 'L1_xattn_b_K': _L1_xattn_in['b_K'], 'L1_xattn_W_V': _L1_xattn_in['W_V'], 'L1_xattn_b_V': _L1_xattn_in['b_V'], 'L1_xattn_W_O': _L1_xattn_in['W_O'], 'L1_xattn_b_O': _L1_xattn_in['b_O'], 'L1_ffn_gate_w': _L1_ffn_in['gate_w'], 'L1_ffn_w_gate': _L1_ffn_in['w_gate'], 'L1_ffn_w_up': _L1_ffn_in['w_up'], 'L1_ffn_w_down': _L1_ffn_in['w_down']}

def reference(x, ctx_1024, mask_Bx1xSxS2_ff0, L0_xattn_wq, L0_xattn_wk, L0_xattn_wv, L0_xattn_wo, L0_ffn_weight, L0_ffn_bias, L0_ffn_so_conv_w, L0_ffn_so_conv_b, L0_ffn_so_gamma, L0_ffn_so_beta, L0_ffn_so_lin_w, L0_ffn_so_lin_b, L0_ffn_si_conv_w, L0_ffn_si_conv_b, L0_ffn_si_gamma, L0_ffn_si_beta, L0_ffn_si_lin_w, L0_ffn_si_lin_b, L1_xattn_W_Q, L1_xattn_b_Q, L1_xattn_W_K, L1_xattn_b_K, L1_xattn_W_V, L1_xattn_b_V, L1_xattn_W_O, L1_xattn_b_O, L1_ffn_gate_w, L1_ffn_w_gate, L1_ffn_w_up, L1_ffn_w_down):
    import jax
    import jax.numpy as jnp

    def _L0_xattn_ref(query_input, source_input, bias, wq, wk, wv, wo):
        import jax, jax.numpy as jnp
        import numpy as np
        HIDDEN = 512
        NUM_HEADS = 16
        HEAD_DIM = HIDDEN // NUM_HEADS
        B, F, T = (2, 1024, 1024)
        q = jnp.einsum('bfd,dnh->bfnh', query_input, wq)
        k = jnp.einsum('btd,dnh->btnh', source_input, wk)
        v = jnp.einsum('btd,dnh->btnh', source_input, wv)
        q = q * HEAD_DIM ** (-0.5)
        logits = jnp.einsum('btnh,bfnh->bnft', k, q) + bias
        weights = jax.nn.softmax(logits, axis=-1)
        attn = jnp.einsum('bnft,btnh->bfnh', weights, v)
        return jnp.einsum('bfnh,nhd->bfd', attn, wo)

    def _L0_ffn_ref(x, weight, bias, so_conv_w, so_conv_b, so_gamma, so_beta, so_lin_w, so_lin_b, si_conv_w, si_conv_b, si_gamma, si_beta, si_lin_w, si_lin_b):
        import jax, jax.numpy as jnp
        import numpy as np
        B, L, C1, C2, K, K_IN = (4, 512, 512, 512, 32, 32)
        BN_EPS = 1e-05

        def _gated_bottleneck(x2d, conv_w, conv_b, gamma, beta, lin_w, lin_b):
            n = x2d.shape[0]
            g = conv_w.shape[0]
            xc = jnp.einsum('ngf,gf->ng', x2d.reshape(n, g, 4), conv_w) + conv_b
            mean = jnp.mean(xc, axis=0)
            var = jnp.mean((xc - mean) ** 2, axis=0)
            xn = (xc - mean) * jax.lax.rsqrt(var + BN_EPS) * gamma + beta
            xa = jax.nn.gelu(xn, approximate=False)
            return xa @ lin_w.T + lin_b
        b, l, c1 = x.shape
        c2 = weight.shape[1]
        x2d = x.reshape(b * l, c1)
        bi = jnp.arange(b)[:, None, None]
        li = jnp.arange(l)[None, :, None]
        score_out = jax.nn.softmax(_gated_bottleneck(x2d, so_conv_w, so_conv_b, so_gamma, so_beta, so_lin_w, so_lin_b).reshape(b, l, c2), axis=-1)
        s_v_out, s_i_out = jax.lax.top_k(score_out, K)
        full = jnp.einsum('blc,co->blo', x, weight)
        out_k = jnp.take_along_axis(full, s_i_out, axis=-1) * s_v_out
        out_branch = jnp.zeros((b, l, c2), x.dtype).at[bi, li, s_i_out].add(out_k)
        score_in = jax.nn.softmax(_gated_bottleneck(x2d, si_conv_w, si_conv_b, si_gamma, si_beta, si_lin_w, si_lin_b).reshape(b, l, c1), axis=-1)
        s_v_in, s_i_in = jax.lax.top_k(score_in, K_IN)
        x_gated = jnp.take_along_axis(x, s_i_in, axis=-1) * s_v_in
        x_sparse = jnp.zeros((b, l, c1), x.dtype).at[bi, li, s_i_in].add(x_gated)
        in_branch = jnp.einsum('blc,co->blo', x_sparse, weight)
        return out_branch + in_branch + bias

    def _L1_xattn_ref(query, key_, value, W_Q, b_Q, W_K, b_K, W_V, b_V, W_O, b_O):
        import jax, jax.numpy as jnp
        import numpy as np
        D_MODEL = 512
        N_HEADS = 16
        D_K = D_MODEL // N_HEADS
        B, S = (4, 1024)
        b = query.shape[0]

        def split_heads(x):
            return x.reshape(b, -1, N_HEADS, D_K).transpose(0, 2, 1, 3)
        Q = split_heads(query @ W_Q.T + b_Q)
        K = split_heads(key_ @ W_K.T + b_K)
        V = split_heads(value @ W_V.T + b_V)
        scores = jnp.einsum('bhqd,bhkd->bhqk', Q, K) / jnp.sqrt(jnp.float32(D_K))
        weights = jax.nn.softmax(scores, axis=-1)
        attn = jnp.einsum('bhqk,bhkd->bhqd', weights, V)
        attn = attn.transpose(0, 2, 1, 3).reshape(b, -1, D_MODEL)
        out = attn @ W_O.T + b_O
        return out

    def _L1_ffn_ref(hidden_states, gate_w, w_gate, w_up, w_down):
        import jax, jax.numpy as jnp
        import numpy as np
        B, S, H, I, E = (2, 2048, 512, 256, 8)
        b, s, h = hidden_states.shape
        x = hidden_states.reshape(-1, h)
        logits = x @ gate_w.T
        top_v = jnp.max(logits, axis=-1)
        sel = jnp.argmax(logits, axis=-1)
        rw = jax.nn.sigmoid(top_v)
        out = jnp.zeros_like(x)
        n_exp = gate_w.shape[0]
        for e in range(n_exp):
            mask = (sel == e).astype(x.dtype)
            xs = x * (rw * mask)[:, None]
            g = xs @ w_gate[e].T
            u = xs @ w_up[e].T
            out = out + u * jax.nn.silu(g) @ w_down[e].T
        return out.reshape(b, s, h)
    x = x + _L0_xattn_ref(_layernorm(x, axis=-1), ctx_1024, mask_Bx1xSxS2_ff0, L0_xattn_wq, L0_xattn_wk, L0_xattn_wv, L0_xattn_wo)
    x = x + _L0_ffn_ref(_layernorm(x, axis=-1), L0_ffn_weight, L0_ffn_bias, L0_ffn_so_conv_w, L0_ffn_so_conv_b, L0_ffn_so_gamma, L0_ffn_so_beta, L0_ffn_so_lin_w, L0_ffn_so_lin_b, L0_ffn_si_conv_w, L0_ffn_si_conv_b, L0_ffn_si_gamma, L0_ffn_si_beta, L0_ffn_si_lin_w, L0_ffn_si_lin_b)
    x = x + _L1_xattn_ref(_layernorm(x, axis=-1), ctx_1024, ctx_1024, L1_xattn_W_Q, L1_xattn_b_Q, L1_xattn_W_K, L1_xattn_b_K, L1_xattn_W_V, L1_xattn_b_V, L1_xattn_W_O, L1_xattn_b_O)
    x = x + _L1_ffn_ref(_layernorm(x, axis=-1), L1_ffn_gate_w, L1_ffn_w_gate, L1_ffn_w_up, L1_ffn_w_down)
    return x

_drawn_inputs = setup_inputs


def setup_inputs(seed=0):
    import zlib

    import numpy as np

    out = dict(_drawn_inputs(seed))
    spreads = {'L0_ffn_bias': (0.0, 0.1),
     'L0_ffn_so_conv_b': (0.0, 0.8),
     'L0_ffn_so_gamma': (1.0, 0.6),
     'L0_ffn_so_beta': (0.0, 0.8),
     'L0_ffn_so_lin_b': (0.0, 0.65),
     'L0_ffn_si_conv_b': (0.0, 0.8),
     'L0_ffn_si_gamma': (1.0, 0.6),
     'L0_ffn_si_beta': (0.0, 0.8),
     'L0_ffn_si_lin_b': (0.0, 0.8),
     'L1_xattn_b_Q': (0.0, 0.1),
     'L1_xattn_b_K': (0.0, 0.8),
     'L1_xattn_b_V': (0.0, 0.1),
     'L1_xattn_b_O': (0.0, 0.1)}
    factors = {'L0_ffn_weight': 4.822,
     'L0_ffn_so_conv_w': 5.151,
     'L0_ffn_so_lin_w': 4.418,
     'L0_ffn_si_conv_w': 5.418,
     'L0_ffn_si_lin_w': 4.13}
    for name, (base, spread) in spreads.items():
        noise = np.random.default_rng([zlib.crc32(name.encode()), seed]).standard_normal(out[name].shape)
        drawn = base * np.exp(spread * noise) if base else spread * noise
        out[name] = jnp.asarray(drawn.astype(out[name].dtype))
    for name, factor in factors.items():
        out[name] = (out[name] * factor).astype(out[name].dtype)
    return out
```

```python
from contextlib import ExitStack

import concourse.bass as bass
from concourse import mybir

F32 = mybir.dt.float32
F32R = mybir.dt.float32r
I32 = mybir.dt.int32
U32 = mybir.dt.uint32
ACT = mybir.ActivationFunctionType
ALU = mybir.AluOpType
AX = mybir.AxisListType

P = 128
D = 512
C = D // P
B = 2
S = 2048
N = B * S
TILES = N // P
GT = 4
GW = GT * P
GROUPS = TILES // GT
GPB = GROUPS // B
H = 16
DH = D // H
QUADS = H // 4
KEYS = 154
KA = 128
KB = 32
KB0 = KEYS - KB
DUP = KA - KB0
QK = 4 * (KA + KB)
EPS = 1e-5
K_TOP = 32
E = 8
I = 256
SLOT_TILES = TILES + E - 1
GONE = -3.0e38

ATT = dict(a_bn=4, a_mv=4, a_ve=1, a_rs=1, a_xn=4, a_tp=4, a_te=4, a_qh=4, lin_done=28, lin_free=28,
           a_mm=20, a_mx=4, a_mt=1, a_mh=1, a_ml=1, sc_done=20, a_sm=20, p_done=20, pv_done=4, a_rc=4,
           a_at=4)
STAT = dict(t_bn=4, t_mv=4, t_ve=1, t_rs=1, t_xn=4, t_tp=4, t_te=4, t_xc=8, t_gs=2)
FFN = dict(f_xn=4, f_xb=1, f_tp=8, f_te=8, f_ge=2, lg_done=8, lg_free=8, f_top=64, f_nm=8, f_ex=8, f_rc=8, f_sel=8,
           f_xs=4, full_done=4, full_free=4, in_done=4, f_sum=4, f_x=4)
GATE = dict(g_bn=4, g_mv=4, g_ve=1, g_rs=1, g_xn=4, g_tp=4, g_te=4, g_lg=4, g_cp=4)


def program(nc, x, ctxT, mask, maskT, wq0, wk0, wv0, wo0, w_ffn, b_ffn, so_cw, so_cb, so_g, so_be, so_lw, so_lb,
            si_cw, si_cb, si_g, si_be, si_lw, si_lb, wq1, bq1, wk1, bk1, wv1, bv1, wo1, bo1, gate_w, w_in, w_down, out):
    xs_dram = nc.dram_tensor("sorted_tokens", (SLOT_TILES * P, D), F32, kind="Internal").ap()
    ys_dram = nc.dram_tensor("sorted_outputs", (SLOT_TILES * P, D), F32, kind="Internal").ap()
    x_tiles = x.rearrange("b (t p) d -> p (b t) d", p=P)
    out_tiles = out.rearrange("b (t p) d -> p (b t) d", p=P)

    top = ExitStack()
    with top:
        sems = {}

        def sem(name):
            if name not in sems:
                sems[name] = top.enter_context(nc.semaphore(name))
            return sems[name]

        def at(table, name, group, k):
            return group * table[name] + k

        def scope():
            stack = ExitStack()

            def sb(name, shape, dt=F32):
                return stack.enter_context(nc.sbuf_tensor(name, shape, dt))
            return stack, sb

        bank = [top.enter_context(nc.psum_tensor(f"bank{i}", [P, D], F32)) for i in range(8)]

        def sb(name, shape, dt=F32):
            return top.enter_context(nc.sbuf_tensor(name, shape, dt))

        xr = sb("x_res", [P, TILES, D])
        ident = sb("ident", [P, P])
        zero = sb("zero", [P, C])
        zero_row = sb("zero_row", [P, D])
        bn = sb("bn", [P, GT, 6])
        mv = sb("mv", [P, GT, 2])
        ve = sb("ve", [P, GT])
        expo = sb("expo", [P, TILES])
        rs = sb("rs", [P, GT])
        eps_c = sb("eps_c", [P, TILES])

        att, sb = scope()
        wq = sb("wq", [P, C, D])
        wo = sb("wo", [P, C, D])
        kh = sb("kh", [P, B, QUADS, QK], F32R)
        kl = sb("kl", [P, B, QUADS, QK], F32R)
        va = sb("va", [P, B, D])
        vb = sb("vb", [P, B, QUADS, P])
        one_a = sb("one_a", [P, DH])
        one_b = sb("one_b", [P, P])
        sel = sb("sel", [P, H], F32R)
        sel_b = sb("sel_b", [P, QUADS, 4, KB], F32R)
        neg_max = sb("neg_max", [P, GW], F32R)
        bq = sb("bq", [P, C])
        bo = sb("bo", [P, D])
        mx = sb("mx", [P, GT, H])
        mxb = sb("mxb", [P, H])
        work = ExitStack()
        xn = work.enter_context(nc.sbuf_tensor("xn", [P, 2, D], F32))
        xnT = work.enter_context(nc.sbuf_tensor("xnT", [P, C, GW], F32))
        qh = work.enter_context(nc.sbuf_tensor("qh", [P, C, GW], F32R))
        ql = work.enter_context(nc.sbuf_tensor("ql", [P, C, GW], F32R))
        pr = work.enter_context(nc.sbuf_tensor("probs", [P, 10, GW], F32))
        attnT = work.enter_context(nc.sbuf_tensor("attnT", [P, C, GW], F32))
        rc = work.enter_context(nc.sbuf_tensor("rc", [P, GW], F32))
        mtmp = work.enter_context(nc.sbuf_tensor("mtmp", [P, 2, D], F32))
        mk_t = work.enter_context(nc.sbuf_tensor("mk_t", [P, GT, KEYS], F32))
        mk_a = work.enter_context(nc.sbuf_tensor("mk_a", [P, GW], F32))
        mk_b = work.enter_context(nc.sbuf_tensor("mk_b", [P, GW], F32))
        work.close()
        ctx_sb = work.enter_context(nc.sbuf_tensor("ctxT", [P, B, C, KEYS], F32))
        ctx_b = work.enter_context(nc.sbuf_tensor("ctx_b", [P, B, C, P], F32))
        wk = work.enter_context(nc.sbuf_tensor("wk", [P, C, D], F32))
        wv = work.enter_context(nc.sbuf_tensor("wv", [P, C, D], F32))
        bk = work.enter_context(nc.sbuf_tensor("bk", [P, C], F32))
        bks = work.enter_context(nc.sbuf_tensor("bks", [P, C], F32))
        bv = work.enter_context(nc.sbuf_tensor("bv", [P, D], F32))
        kf = work.enter_context(nc.sbuf_tensor("kf", [P, 2, KEYS], F32))
        work.close()
        att.close()

        ffn, sb = scope()
        xc = [sb("xc_so", [P, N]), sb("xc_si", [P, N])]
        mv2 = sb("mv2", [P, TILES, 2])
        rs2 = sb("rs2", [P, TILES])
        nm2 = sb("nm2", [P, TILES])
        gst = sb("gst", [P, 2, GROUPS, 6])
        gmv = sb("gmv", [P, 2, 2])
        gve = sb("gve", [P, 2])
        grs = sb("grs", [P, 2])
        gsc = sb("gsc", [P, 2])
        gbi = sb("gbi", [P, 2])
        gtm = sb("gtm", [P, 2])
        cw = sb("cw", [P, 2, 4])
        cb = sb("cb", [P, 2])
        gam = sb("gam", [P, 2])
        bet = sb("bet", [P, 2])
        wf = sb("wf", [P, C, D])
        lw = sb("lw", [P, 2, D])
        lb = sb("lb", [P, 2, D])
        bf = sb("bf", [P, D])
        fxn = sb("fxn", [P, GT, D])
        fxT = sb("fxT", [P, C, GW])
        ge = sb("ge", [P, 2, GW])
        Lg = sb("Lg", [P, 2, D])
        Wk = sb("Wk", [P, 2, 1, D])
        ex = sb("ex", [P, 2, D])
        m8 = sb("m8", [P, 2, 8])
        fnm = sb("fnm", [P, 2])
        fsum = sb("fsum", [P, 2])
        frc = sb("frc", [P, 2])
        selv = sb("selv", [P, 2, D])
        fxs = sb("fxs", [P, D])
        fxsT = sb("fxsT", [P, D])
        ftmp = sb("ftmp", [P, 2, D])
        fsm = sb("fsm", [P, 2, D])
        ffn.close()

        moe, sb = scope()
        w_in_sb = sb("w_in", [P, E * C * 2 * I])
        w_dn_sb = sb("w_down", [P, E * 2 * D])
        gw = sb("gate_w", [P, C, E])
        mxn = sb("mxn", [P, 2, D])
        mxT = sb("mxT", [P, 2, D])
        below = sb("below", [P, TILES, E])
        cand = sb("cand", [P, TILES, E])
        cmp = sb("cmp", [P, SLOT_TILES, E - 1])
        tiles_f = sb("tiles_f", [P, E])
        start = sb("start", [P, E + 1])
        lgt = sb("lgt", [P, TILES, E])
        mv3 = sb("mv3", [P, TILES, 2])
        rs3 = sb("rs3", [P, TILES])
        top_v = sb("top_v", [P, TILES])
        selx = sb("selx", [P, TILES])
        iota_e = sb("iota_e", [P, E])
        onehot = sb("onehot", [P, TILES, E])
        tri = sb("tri", [P, P])
        ones = sb("ones", [P, P])
        rank = sb("rank", [P, TILES, E])
        cnt = sb("cnt", [P, 2, TILES, E])
        own = sb("own", [P, TILES, E])
        tot = sb("tot", [P, E])
        toti = sb("toti", [P, E], I32)
        prod = sb("prod", [P, TILES, E])
        posf = sb("posf", [P, TILES])
        posi = sb("posi", [P, TILES], I32)
        slot_i = sb("slot_i", [P, SLOT_TILES])
        slot_e = sb("slot_e", [P, SLOT_TILES])
        slot_ei = sb("slot_ei", [P, SLOT_TILES], I32)
        rwe = sb("rwe", [P, TILES])
        rw = sb("rw", [P, TILES])
        srs = sb("srs", [P, TILES])
        xs = sb("xs", [P, 4, D])
        tx = xs
        txT = mxT
        sg = sb("sg", [P, 2, I])
        hh = sb("hh", [P, 2, I])
        hT = sb("hT", [P, 2, I])
        yo = mxn
        yg = xs
        moe.close()

        block = top.enter_context(nc.Block())
        att_groups = [(layer, b) for layer in range(2) for b in range(B)]

        def groups(eng, layer, body):
            for b in range(B):
                with eng.Fori(0, GPB) as i:
                    body(b * GPB + i, b, layer * GROUPS + b * GPB + i)

        def pool_constants(pool):
            pool.memset(ident[:], 0.0).then_inc(sem("c_0"), 1)
            pool.memset(zero[:], 0.0).then_inc(sem("const"), 1)
            pool.memset(zero_row[:], 0.0).then_inc(sem("const"), 1)
            pool.memset(expo[:], -0.5).then_inc(sem("const"), 1)
            pool.memset(eps_c[:], EPS).then_inc(sem("const"), 1)
            pool.wait_ge(sem("c_0"), 1)
            pool.affine_select(out=ident[:], in_=ident[:], compare_op=ALU.not_equal, fill=1.0, base=0,
                               pattern=[[-1, P]], channel_multiplier=1).then_inc(sem("const"), 1)

        def pool_att_setup(pool, layer):
            if layer == 1:
                pool.wait_ge(sem("ffn_over"), 5)
            zeroed = sem("zeroed")
            pool.memset(one_b[:], 0.0).then_inc(zeroed, 1)
            pool.memset(sel[:].bitcast(F32), 0.0).then_inc(zeroed, 1)
            pool.memset(kh[:].bitcast(F32), 0.0).then_inc(zeroed, 1)
            pool.memset(kl[:].bitcast(F32), 0.0).then_inc(zeroed, 1)
            pool.memset(vb[:], 0.0).then_inc(zeroed, 1)
            pool.memset(neg_max[:].bitcast(F32), 0.0).then_inc(sem("selected"), 1)
            pool.memset(one_a[:], 1.0).then_inc(sem("selected"), 1)
            pool.wait_ge(zeroed, layer * 5 + 5)
            pool.affine_select(out=sel[:], in_=sel[:].bitcast(F32), compare_op=ALU.not_equal, fill=1.0, base=0,
                               pattern=[[-1, H]], channel_multiplier=1).then_inc(sem("selected"), 1)
            pool.wait_ge(sem("selected"), layer * 5 + 3)
            pool.affine_select(out=sel[:], in_=sel[:].bitcast(F32), compare_op=ALU.not_equal, fill=1.0, base=-32,
                               pattern=[[-1, H]], channel_multiplier=1).then_inc(sem("selected"), 1)
            pool.wait_ge(sem("selected"), layer * 5 + 4)
            pool.tensor_copy(sel_b[:].rearrange("p q h k -> p (q h) k"), sel[:].unsqueeze(2).broadcast_to([P, H, KB]))\
                .then_inc(sem("selected"), 1)
            pool.sem_inc(sem("kv_over"), 1)

        def hold(eng, name, value):
            eng.wait_ge(sem(name), value)
            eng.sem_inc(sem("held"), 1)

        def pool_att_group(pool, layer, g, b, G):
            pool.wait_ge(sem("a_mv"), at(ATT, "a_mv", G, GT))
            pool.tensor_tensor(ve[:], mv[:, :, 1], eps_c[:, 0:GT], ALU.add).then_inc(sem("a_ve"), 1)
            pool.wait_ge(sem("a_ve"), at(ATT, "a_ve", G, 1))
            pool.tensor_tensor(rs[:], ve[:], expo[:, 0:GT], ALU.pow).then_inc(sem("a_rs"), 1)
            if layer == 1:
                hold(pool, "a_xn", at(ATT, "a_xn", G, GT))
                xg = xr[:, bass.ds(g * GT, GT), :]
                pool.tensor_tensor(xg, xg, bo[:].unsqueeze(1).broadcast_to([P, GT, D]), ALU.add)\
                    .then_inc(sem("a_xb"), 1)

        def leave(eng, phase, last, value):
            eng.wait_ge(sem(last), value)
            eng.sem_inc(sem(phase), 1)

        def diagonal(u):
            for j in range(4):
                rows = slice(DH * j, DH * j + DH)
                yield rows, slice(0, KA), slice(KA * j, KA * j + KA)
                yield rows, slice(KB0, KEYS), slice(4 * KA + KB * j, 4 * KA + KB * j + KB)

        def pe_kv(pe, layer):
            pe.wait_ge(sem("kv_in"), (layer + 1) * 16 * (1 + 16 + 4))
            pe.wait_ge(sem("const"), 5)
            for b in range(B):
                for q in range(QUADS):
                    u = b * QUADS + q
                    pe.wait_ge(sem("kT_free"), layer * 8 + u + 1)
                    for c in range(C):
                        mm = pe.matmul(bank[u % 2][:, 0:KEYS], wk[:, c, P * q:P * q + P], ctx_sb[:, b, c, :],
                                       start=(c == 0), stop=(c == C - 1))
                    mm.then_inc(sem("kT_done"), 1)
            for b in range(B):
                pe.wait_ge(sem("v_free"), layer * 4 + 2 * b + 2)
                for c in range(C):
                    mm = pe.matmul(bank[4][:], ctx_sb[:, b, c, 0:KA], wv[:, c, :], start=(c == 0), stop=(c == C - 1))
                mm.then_inc(sem("v_done"), 1)
                for c in range(C):
                    mm = pe.matmul(bank[5][:], ctx_b[:, b, c, :], wv[:, c, :], start=(c == 0), stop=(c == C - 1))
                mm.then_inc(sem("v_done"), 1)
            pe.sem_inc(sem("kv_over"), 1)

        def act_kv(act, layer):
            scale = float(DH) ** -0.5
            if layer == 1:
                act.wait_ge(sem("bias_in"), 64)
                act.activation(bks[:], bk[:], ACT.Copy, scale=scale).then_inc(sem("bks"), 1)
                act.wait_ge(sem("bks"), 1)
            act.wait_ge(sem("zeroed"), layer * 5 + 5)
            for u in range(B * QUADS):
                bias = bks[:, u % QUADS:u % QUADS + 1] if layer == 1 else 0.0
                U = layer * B * QUADS + u
                act.wait_ge(sem("kT_done"), U + 1)
                act.wait_ge(sem("k_split"), U + 1)
                act.activation(kf[:, u % 2, :], bank[u % 2][:, 0:KEYS], ACT.Identity, scale=scale, bias=bias)\
                    .then_inc(sem("kT_free"), 1)
                act.wait_ge(sem("kT_free"), U + 3)
                for rows, part, cols in diagonal(u):
                    hi = act.activation(kh[rows, u // QUADS, u % QUADS, cols], kf[rows, u % 2, part], ACT.Copy)
                hi.then_inc(sem("k_hi"), 1)
            act.sem_inc(sem("kv_over"), 1)

        def dve_kv(dve, layer):
            if layer == 1:
                dve.wait_ge(sem("bias_in"), 64)
            dve.wait_ge(sem("zeroed"), layer * 5 + 5)
            for j in range(4):
                rows = slice(KB * j, KB * j + KB)
                dve.memset(one_b[rows, rows], 1.0).then_inc(sem("one_b"), 1)
            dve.wait_ge(sem("one_b"), layer * 8 + 4)
            for j in range(4):
                dve.memset(one_b[KB * j:KB * j + DUP, KB * j:KB * j + KB], 0.0).then_inc(sem("one_b"), 1)
            for u in range(B * QUADS):
                U = layer * B * QUADS + u
                dve.wait_ge(sem("k_hi"), U + 1)
                for rows, part, cols in diagonal(u):
                    lo = dve.tensor_tensor(kl[rows, u // QUADS, u % QUADS, cols], kf[rows, u % 2, part],
                                           kh[rows, u // QUADS, u % QUADS, cols], ALU.subtract)
                lo.then_inc(sem("k_split"), 1)
            for b in range(B):
                dve.wait_ge(sem("v_done"), layer * 4 + 2 * b + 1)
                if layer == 0:
                    dve.tensor_copy(va[:, b, :], bank[4][:]).then_inc(sem("v_free"), 1)
                else:
                    dve.tensor_tensor(va[:, b, :], bank[4][:], bv[:], ALU.add).then_inc(sem("v_free"), 1)
                dve.wait_ge(sem("v_done"), layer * 4 + 2 * b + 2)
                for j in range(4):
                    rows = slice(KB * j, KB * j + KB)
                    dst = vb[rows, b, :, KB * j:KB * j + KB]
                    src = bank[5][rows, :].rearrange("p (q n) -> p q n", q=QUADS)[:, :, KB * j:KB * j + KB]
                    if layer == 0:
                        cp = dve.tensor_copy(dst, src)
                    else:
                        cp = dve.tensor_tensor(dst, src, bv[rows, :].rearrange("p (q n) -> p q n", q=QUADS)
                                               [:, :, KB * j:KB * j + KB], ALU.add)
                cp.then_inc(sem("v_free"), 1)
            dve.wait_ge(sem("v_free"), 2 + 4 * (layer + 1))
            for j in range(4):
                ms = dve.memset(vb[KB * j:KB * j + DUP, :, :, :], 0.0)
            ms.then_inc(sem("vb_ready"), 1)
            dve.sem_inc(sem("kv_over"), 1)

        def enter_groups(eng, layer):
            eng.wait_ge(sem("kv_over"), 4 * (layer + 1))

        def pe_att_start(pe, layer):
            enter_groups(pe, layer)
            pe.wait_ge(sem("k_split"), (layer + 1) * B * QUADS + 2)
            pe.wait_ge(sem("vb_ready"), layer + 1)
            pe.wait_ge(sem("selected"), (layer + 1) * 5)
            pe.wait_ge(sem("one_b"), (layer + 1) * 8)
            if layer == 0:
                pe.sem_inc(sem("a_tp"), 2)
                pe.sem_inc(sem("pv_done"), 2)

        def pe_att_group(pe, layer, g, b, G):
            unit = [0]

            def lin_unit():
                u = unit[0]
                unit[0] += 1
                pe.wait_ge(sem("lin_free"), at(ATT, "lin_free", G, u + 1))
                return bank[2 + u % 2]

            for t in range(GT):
                pe.wait_ge(sem("a_xn"), at(ATT, "a_xn", G, t + 1))
                pe.wait_ge(sem("a_te"), at(ATT, "a_te", G, t + 1))
                for c in range(C):
                    mm = pe.transpose(bank[t % 2][:, P * c:P * c + P], xn[:, t % 2, c::C], ident[:])
                mm.then_inc(sem("a_tp"), 1)
            pe.wait_ge(sem("a_te"), at(ATT, "a_te", G, GT + 2))
            for m in range(C):
                o = lin_unit()
                for c in range(C):
                    mm = pe.matmul(o[:], wq[:, c, P * m:P * m + P], xnT[:, c, :], start=(c == 0), stop=(c == C - 1))
                mm.then_inc(sem("lin_done"), 1)
            pe.wait_ge(sem("a_qh"), at(ATT, "a_qh", G, C))
            for t in range(GT):
                for q in range(QUADS):
                    o = lin_unit()
                    pe.matmul(o[:], qh[:, q, P * t:P * t + P], kh[:, b, q, 0:4 * KA], start=True, stop=True)\
                        .then_inc(sem("lin_done"), 1)
                o = lin_unit()
                for q in range(QUADS):
                    mm = pe.matmul(o[:, P * q:P * q + P], qh[:, q, P * t:P * t + P], kh[:, b, q, 4 * KA:QK],
                                   start=(q == 0), stop=(q == QUADS - 1), skip_group_check=True)
                mm.then_inc(sem("lin_done"), 1)
            pe.wait_ge(sem("a_at"), at(ATT, "a_at", G, 1))
            for t in range(GT):
                pe.wait_ge(sem("a_mx"), at(ATT, "a_mx", G, t + 1))
                mm = pe.transpose(bank[7][0:H, P * t:P * t + P], mx[:, t, :], ident[:])
            mm.then_inc(sem("a_mt"), 1)
            pe.wait_ge(sem("a_ml"), at(ATT, "a_ml", G, 1))
            pe.wait_ge(sem("lin_free"), at(ATT, "lin_free", G, C + 2))

            def scores(q):
                for j in range(5):
                    u = 5 * q + j
                    o = bank[4 + u % 2]
                    if layer == 0:
                        pe.wait_ge(sem("a_sm"), at(ATT, "a_sm", G, u + 1))
                    else:
                        pe.wait_ge(sem("p_done"), at(ATT, "p_done", G, u - 1))
                    cols = slice(KA * j, KA * j + KA)
                    pe.matmul(o[:], kh[:, b, q, cols], qh[:, q, :], start=True, stop=False)
                    pe.matmul(o[:], kh[:, b, q, cols], ql[:, q, :], start=False, stop=False)
                    pe.matmul(o[:], kl[:, b, q, cols], qh[:, q, :], start=False, stop=False)
                    if j < 4:
                        pick = sel[:, 4 * q + j:4 * q + j + 1].broadcast_to([P, P])
                    else:
                        pick = sel_b[:, q, :, :].rearrange("p h k -> p (h k)")
                    pe.matmul(o[:], pick, neg_max[:], start=False, stop=True).then_inc(sem("sc_done"), 1)

            def values(q):
                pe.wait_ge(sem("a_at"), at(ATT, "a_at", G, q + 1))
                pe.wait_ge(sem("p_done"), at(ATT, "p_done", G, 5 * q + 5))
                slot = 5 * (q % 2)
                for j in range(4):
                    pe.matmul(bank[6][DH * j:DH * j + DH, :], va[:, b, P * q + DH * j:P * q + DH * j + DH],
                              pr[:, slot + j, :], start=True, stop=False, skip_group_check=True)
                for j in range(4):
                    pe.matmul(bank[7][DH * j:DH * j + DH, :], one_a[:], pr[:, slot + j, :],
                              start=True, stop=False, skip_group_check=True)
                pe.matmul(bank[6][:], vb[:, b, q, :], pr[:, slot + 4, :], start=False, stop=True, skip_group_check=True)
                pe.matmul(bank[7][:], one_b[:], pr[:, slot + 4, :], start=False, stop=True, skip_group_check=True)\
                    .then_inc(sem("pv_done"), 1)

            scores(0)
            for q in range(1, QUADS):
                scores(q)
                values(q - 1)
            values(QUADS - 1)
            for t in range(GT):
                o = lin_unit()
                for q in range(QUADS):
                    if t == 0:
                        pe.wait_ge(sem("a_at"), at(ATT, "a_at", G, q + 2))
                    mm = pe.matmul(o[:], attnT[:, q, P * t:P * t + P], wo[:, q, :], start=(q == 0),
                                   stop=(q == QUADS - 1))
                mm.then_inc(sem("lin_done"), 1)

        def act_att_group(act, layer, g, b, G):
            for t in range(GT):
                act.wait_ge(sem("a_tp"), at(ATT, "a_tp", G, t + 3))
                act.activation(xnT[:, :, P * t:P * t + P], bank[t % 2][:].rearrange("p (c n) -> p c n", c=C), ACT.Copy)\
                    .then_inc(sem("a_te"), 1)
            for m in range(C):
                act.wait_ge(sem("lin_done"), at(ATT, "lin_done", G, m + 1))
                bias = bq[:, m:m + 1] if layer == 1 else zero[:, m:m + 1]
                act.activation(qh[:, m, :], bank[2 + m % 2][:], ACT.Identity, bias=bias).then_inc(sem("a_qh"), 1)
            act.wait_ge(sem("a_mt"), at(ATT, "a_mt", G, 1))
            act.activation(neg_max[0:H, :], bank[7][0:H, :], ACT.Copy, scale=-1.0).then_inc(sem("a_mh"), 1)
            for u in range(20):
                slot = u % 10
                if layer == 0:
                    act.wait_ge(sem("a_sm"), at(ATT, "a_sm", G, u + 3))
                    act.activation(pr[:, slot, :], pr[:, slot, :], ACT.Exp).then_inc(sem("p_done"), 1)
                else:
                    act.wait_ge(sem("sc_done"), at(ATT, "sc_done", G, u + 1))
                    act.wait_ge(sem("pv_done"), at(ATT, "pv_done", G, u // 5 + 1))
                    act.activation(pr[:, slot, :], bank[4 + u % 2][:], ACT.Exp).then_inc(sem("p_done"), 1)

        def dve_att_group(dve, layer, g, b, G):
            if layer == 0:
                dve.wait_ge(sem("x_in"), 16 * g + 16)
            for t in range(GT):
                dve.bn_stats(bn[:, t, :], xr[:, bass.ds(g * GT + t, 1), :].rearrange("p a d -> p (a d)"))\
                    .then_inc(sem("a_bn"), 1)
            for t in range(GT):
                hold(dve, "a_bn", at(ATT, "a_bn", G, t + 1))
                dve.bn_aggr(mv[:, t, :], bn[:, t, :]).then_inc(sem("a_mv"), 1)
            dve.wait_ge(sem("a_rs"), at(ATT, "a_rs", G, 1))
            for t in range(GT):
                hold(dve, "a_tp", at(ATT, "a_tp", G, t + 1))
                dve.tensor_scalar(xn[:, t % 2, :], xr[:, bass.ds(g * GT + t, 1), :].rearrange("p a d -> p (a d)"),
                                  mv[:, t, 0:1], rs[:, t:t + 1], ALU.subtract, ALU.mult).then_inc(sem("a_xn"), 1)
            for m in range(C):
                dve.wait_ge(sem("a_qh"), at(ATT, "a_qh", G, m + 1))
                bias = bq[:, m:m + 1] if layer == 1 else zero[:, m:m + 1]
                dve.scalar_tensor_tensor(ql[:, m, :], bank[2 + m % 2][:], bias, qh[:, m, :], ALU.add, ALU.subtract)\
                    .then_inc(sem("lin_free"), 1)
            if layer == 0:
                dve.wait_ge(sem("mask_in"), g * 96 + 96)
            chain = [0]

            def link(ins):
                chain[0] += 1
                ins.then_inc(sem("a_mm"), 1)
                dve.wait_ge(sem("a_mm"), at(ATT, "a_mm", G, chain[0]))

            for t in range(GT):
                for q in range(5):
                    u = C + 5 * t + q
                    width, n = (KA, 4) if q < 4 else (KB, H)
                    src = bank[2 + u % 2][:].rearrange("p (h k) -> p h k", h=n)
                    dst = mx[:, t, 4 * q:4 * q + 4] if q < 4 else mxb[:]
                    dve.wait_ge(sem("lin_done"), at(ATT, "lin_done", G, u + 1))
                    if layer == 0:
                        keys = slice(0, KA) if q < 4 else slice(KB0, KEYS)
                        tmp = mtmp[:, u % 2, :].rearrange("p (h k) -> p h k", h=n)
                        dve.tensor_tensor(tmp, src, mk_t[:, t, keys].unsqueeze(1).broadcast_to([P, n, width]), ALU.add)\
                            .then_inc(sem("lin_free"), 1)
                        dve.wait_ge(sem("lin_free"), at(ATT, "lin_free", G, u + 3))
                        link(dve.tensor_reduce(dst, tmp, AX.X, ALU.max))
                    else:
                        dve.tensor_reduce(dst, src, AX.X, ALU.max).then_inc(sem("lin_free"), 1)
                if layer == 1:
                    dve.wait_ge(sem("lin_free"), at(ATT, "lin_free", G, u + 3))
                dve.tensor_tensor(mx[:, t, :], mx[:, t, :], mxb[:], ALU.max).then_inc(sem("a_mx"), 1)
                dve.wait_ge(sem("a_mx"), at(ATT, "a_mx", G, t + 1))
            dve.wait_ge(sem("a_mh"), at(ATT, "a_mh", G, 1))
            dve.scalar_tensor_tensor(neg_max[32:32 + H, :], bank[7][0:H, :], -1.0, neg_max[0:H, :],
                                     ALU.mult, ALU.subtract).then_inc(sem("a_ml"), 1)

            def normalise(q):
                dve.wait_ge(sem("pv_done"), at(ATT, "pv_done", G, q + 3))
                dve.reciprocal(rc[:], bank[7][:]).then_inc(sem("a_rc"), 1)
                dve.wait_ge(sem("a_rc"), at(ATT, "a_rc", G, q + 1))
                dve.tensor_tensor(attnT[:, q, :], bank[6][:], rc[:], ALU.mult).then_inc(sem("a_at"), 1)

            for q in range(QUADS):
                if layer == 0:
                    dve.wait_ge(sem("pv_done"), at(ATT, "pv_done", G, q + 1))
                    for j in range(5):
                        u = 5 * q + j
                        dve.wait_ge(sem("sc_done"), at(ATT, "sc_done", G, u + 1))
                        dve.tensor_tensor(pr[:, u % 10, :], bank[4 + u % 2][:], (mk_a if j < 4 else mk_b)[:], ALU.add)\
                            .then_inc(sem("a_sm"), 1)
                if q >= 1:
                    normalise(q - 1)
            if layer == 0:
                dve.wait_ge(sem("a_sm"), at(ATT, "a_sm", G, 22))
                dve.sem_inc(sem("mask_free"), 1)
            normalise(QUADS - 1)
            for t in range(GT):
                u = 24 + t
                dve.wait_ge(sem("lin_done"), at(ATT, "lin_done", G, u + 1))
                if layer == 1:
                    dve.wait_ge(sem("a_xb"), g + 1)
                xt = xr[:, bass.ds(g * GT + t, 1), :].rearrange("p a d -> p (a d)")
                dve.tensor_tensor(xt, bank[2 + u % 2][:], xt, ALU.add).then_inc(sem("lin_free"), 1)

        def tile_of(buf, g, t):
            return buf[:, bass.ds(g * GT + t, 1), :].rearrange("p a d -> p (a d)")

        def pool_stats_group(pool, g):
            hold(pool, "t_mv", at(STAT, "t_mv", g, GT))
            pool.tensor_tensor(ve[:], mv[:, :, 1], eps_c[:, 0:GT], ALU.add).then_inc(sem("t_ve"), 1)
            pool.wait_ge(sem("t_ve"), at(STAT, "t_ve", g, 1))
            pool.tensor_tensor(rs[:], ve[:], expo[:, 0:GT], ALU.pow).then_inc(sem("t_rs"), 1)

        def dve_stats_group(dve, g):
            for t in range(GT):
                dve.bn_stats(bn[:, t, :], tile_of(xr, g, t)).then_inc(sem("t_bn"), 1)
            for t in range(GT):
                hold(dve, "t_bn", at(STAT, "t_bn", g, t + 1))
                dve.bn_aggr(mv[:, t, :], bn[:, t, :]).then_inc(sem("t_mv"), 1)
            hold(dve, "t_rs", at(STAT, "t_rs", g, 1))
            dve.tensor_copy(mv2[:, bass.ds(g * GT, GT), :], mv[:]).then_inc(sem("t_keep"), 1)
            dve.tensor_copy(rs2[:, bass.ds(g * GT, GT)], rs[:]).then_inc(sem("t_keep"), 1)
            for t in range(GT):
                hold(dve, "t_tp", at(STAT, "t_tp", g, t + 1))
                dve.tensor_scalar(fxn[:, t, :], tile_of(xr, g, t), mv[:, t, 0:1], rs[:, t:t + 1],
                                  ALU.subtract, ALU.mult).then_inc(sem("t_xn"), 1)
            dve.wait_ge(sem("t_te"), at(STAT, "t_te", g, GT + 2))
            for c in range(C):
                for n in range(2):
                    xg = xc[n][:, bass.ds(g * GW, GW)]
                    if c == 0:
                        dve.tensor_scalar(xg, fxT[:, c, :], cw[:, n, c:c + 1], cb[:, n:n + 1], ALU.mult, ALU.add)\
                            .then_inc(sem("t_xc"), 1)
                    else:
                        hold(dve, "t_xc", at(STAT, "t_xc", g, 2 * c + n - 1))
                        dve.scalar_tensor_tensor(xg, fxT[:, c, :], cw[:, n, c:c + 1], xg, ALU.mult, ALU.add)\
                            .then_inc(sem("t_xc"), 1)
            for n in range(2):
                hold(dve, "t_xc", at(STAT, "t_xc", g, 7 + n))
                dve.tensor_copy(ge[:, n, :], xc[n][:, bass.ds(g * GW, GW)]).then_inc(sem("t_cp"), 1)
            for n in range(2):
                hold(dve, "t_cp", g * 2 + n + 1)
                dve.bn_stats(gst[:, n, bass.ds(g, 1), :].rearrange("p a s -> p (a s)"), ge[:, n, :])\
                    .then_inc(sem("t_gs"), 1)

        def pe_stats_group(pe, g):
            for t in range(GT):
                pe.wait_ge(sem("t_xn"), at(STAT, "t_xn", g, t + 1))
                pe.wait_ge(sem("t_te"), at(STAT, "t_te", g, t + 1))
                for c in range(C):
                    mm = pe.transpose(bank[t % 2][:, P * c:P * c + P], fxn[:, t, c::C], ident[:])
                mm.then_inc(sem("t_tp"), 1)

        def act_stats_group(act, g):
            for t in range(GT):
                act.wait_ge(sem("t_tp"), at(STAT, "t_tp", g, t + 5))
                if t == 0:
                    act.wait_ge(sem("t_gs"), at(STAT, "t_gs", g, 2))
                act.activation(fxT[:, :, P * t:P * t + P], bank[t % 2][:].rearrange("p (c n) -> p c n", c=C), ACT.Copy)\
                    .then_inc(sem("t_te"), 1)

        def dve_batch_norm(dve):
            dve.wait_ge(sem("t_gs"), 2 + 2 * GROUPS)
            for n in range(2):
                dve.bn_aggr(gmv[:, n, :], gst[:, n, :, :].rearrange("p g s -> p (g s)")).then_inc(sem("b_mv"), 1)
            dve.wait_ge(sem("b_rs"), 1)
            dve.tensor_tensor(gsc[:], grs[:], gam[:], ALU.mult).then_inc(sem("b_sc"), 1)
            dve.wait_ge(sem("b_sc"), 1)
            dve.tensor_tensor(gtm[:], gmv[:, :, 0], gsc[:], ALU.mult).then_inc(sem("b_sc"), 1)
            dve.wait_ge(sem("b_sc"), 2)
            dve.tensor_tensor(gbi[:], bet[:], gtm[:], ALU.subtract).then_inc(sem("b_sc"), 1)

        def pool_batch_norm(pool):
            pool.wait_ge(sem("b_mv"), 2)
            pool.tensor_tensor(gve[:], gmv[:, :, 1], eps_c[:, 0:2], ALU.add).then_inc(sem("b_ve"), 1)
            pool.wait_ge(sem("b_ve"), 1)
            pool.tensor_tensor(grs[:], gve[:], expo[:, 0:2], ALU.pow).then_inc(sem("b_rs"), 1)

        def pool_ffn_group(pool, g):
            hold(pool, "f_xn", at(FFN, "f_xn", g, GT))
            xg = xr[:, bass.ds(g * GT, GT), :]
            pool.tensor_tensor(xg, xg, bf[:].unsqueeze(1).broadcast_to([P, GT, D]), ALU.add).then_inc(sem("f_xb"), 1)
            pool.wait_ge(sem("f_xb"), at(FFN, "f_xb", g, 1))
            for t in range(GT):
                hold(pool, "f_sum", at(FFN, "f_sum", g, t + 3))
                pool.tensor_tensor(tile_of(xr, g, t), tile_of(xr, g, t), fsm[:, t % 2, :], ALU.add)\
                    .then_inc(sem("f_x"), 1)

        def pe_ffn_group(pe, g):
            def logits(t):
                for n in (1, 0):
                    u = 2 * t + 1 - n
                    pe.wait_ge(sem("lg_free"), at(FFN, "lg_free", g, u + 1))
                    if t == 0:
                        pe.wait_ge(sem("f_ge"), at(FFN, "f_ge", g, 2 - n))
                    pe.matmul(bank[2 + u % 2][:], ge[:, n, P * t:P * t + P], lw[:, n, :], start=True, stop=True)\
                        .then_inc(sem("lg_done"), 1)

            def full(t):
                pe.wait_ge(sem("full_free"), at(FFN, "full_free", g, t + 1))
                for c in range(C):
                    mm = pe.matmul(bank[4 + t % 2][:], fxT[:, c, P * t:P * t + P], wf[:, c, :], start=(c == 0),
                                   stop=(c == C - 1))
                mm.then_inc(sem("full_done"), 1)

            def sparse(t):
                pe.wait_ge(sem("f_xs"), at(FFN, "f_xs", g, t + 1 + GT))
                pe.wait_ge(sem("f_te"), at(FFN, "f_te", g, GT + t + 1))
                for c in range(C):
                    mm = pe.transpose(bank[t % 2][:, P * c:P * c + P], fxs[:, c::C], ident[:])
                mm.then_inc(sem("f_tp"), 1)
                pe.wait_ge(sem("f_te"), at(FFN, "f_te", g, GT + t + 3))
                pe.wait_ge(sem("f_sum"), at(FFN, "f_sum", g, t + 1))
                for c in range(C):
                    mm = pe.matmul(bank[6 + t % 2][:], fxsT[:, P * c:P * c + P], wf[:, c, :], start=(c == 0),
                                   stop=(c == C - 1))
                mm.then_inc(sem("in_done"), 1)

            logits(0)
            for t in range(GT):
                pe.wait_ge(sem("f_xn"), at(FFN, "f_xn", g, t + 1))
                pe.wait_ge(sem("f_te"), at(FFN, "f_te", g, t + 1))
                for c in range(C):
                    mm = pe.transpose(bank[t % 2][:, P * c:P * c + P], fxn[:, t, c::C], ident[:])
                mm.then_inc(sem("f_tp"), 1)
            pe.wait_ge(sem("f_te"), at(FFN, "f_te", g, GT + 2))
            for t in range(GT):
                full(t)
                if t + 1 < GT:
                    logits(t + 1)
                sparse(t)

        def act_ffn_group(act, g):
            for n in (1, 0):
                act.activation(ge[:, n, :], xc[n][:, bass.ds(g * GW, GW)], ACT.Gelu, bias=gbi[:, n:n + 1],
                               scale=gsc[:, n:n + 1]).then_inc(sem("f_ge"), 1)
            for t in range(GT):
                act.wait_ge(sem("f_tp"), at(FFN, "f_tp", g, t + 1))
                act.activation(fxT[:, :, P * t:P * t + P], bank[t % 2][:].rearrange("p (c n) -> p c n", c=C), ACT.Copy)\
                    .then_inc(sem("f_te"), 1)
            for t in range(GT):
                for n in (1, 0):
                    u = 2 * t + 1 - n
                    act.wait_ge(sem("f_nm"), at(FFN, "f_nm", g, u + 1))
                    act.activation(ex[:, n, :], Lg[:, n, :], ACT.Exp, bias=fnm[:, n:n + 1],
                                   accum_out=fsum[:, n:n + 1]).then_inc(sem("f_ex"), 1)
                act.wait_ge(sem("f_tp"), at(FFN, "f_tp", g, GT + t + 1))
                act.activation(fxsT[:], bank[t % 2][:], ACT.Copy).then_inc(sem("f_te"), 1)

        def dve_ffn_group(dve, g):
            for t in range(GT):
                hold(dve, "f_xs", at(FFN, "f_xs", g, t + 1))
                dve.tensor_scalar(fxn[:, t, :], tile_of(xr, g, t), mv2[:, bass.ds(g * GT + t, 1), 0],
                                  rs2[:, bass.ds(g * GT + t, 1)], ALU.subtract, ALU.mult).then_inc(sem("f_xn"), 1)
            chain = [0]

            def top(ins):
                chain[0] += 1
                ins.then_inc(sem("f_top"), 1)
                hold(dve, "f_top", at(FFN, "f_top", g, chain[0]))

            def combine(t):
                dve.wait_ge(sem("full_free"), at(FFN, "full_free", g, t + 3))
                dve.wait_ge(sem("in_done"), at(FFN, "in_done", g, t + 1))
                dve.wait_ge(sem("f_x"), at(FFN, "f_x", g, t + 1))
                dve.tensor_tensor(fsm[:, t % 2, :], bank[6 + t % 2][:], ftmp[:, t % 2, :], ALU.add)\
                    .then_inc(sem("f_sum"), 1)

            for t in range(GT):
                for n in (1, 0):
                    u = 2 * t + 1 - n
                    dve.wait_ge(sem("lg_done"), at(FFN, "lg_done", g, u + 1))
                    dve.tensor_tensor(Lg[:, n, :], bank[2 + u % 2][:], lb[:, n, :], ALU.add).then_inc(sem("lg_free"), 1)
                    hold(dve, "lg_free", at(FFN, "lg_free", g, u + 3))
                    src = Lg[:, n, :]
                    for k in range(K_TOP // 8):
                        top(dve.max(m8[:, n, :], src))
                        if k == 0:
                            dve.tensor_scalar(fnm[:, n:n + 1], m8[:, n, 0:1], -1.0, None, ALU.mult)\
                                .then_inc(sem("f_nm"), 1)
                        top(dve.match_replace(Wk[:, k % 2, 0, :], m8[:, n, :], src, GONE))
                        src = Wk[:, k % 2, 0, :]
                    dve.wait_ge(sem("f_ex"), at(FFN, "f_ex", g, u + 1))
                    dve.reciprocal(frc[:, n:n + 1], fsum[:, n:n + 1]).then_inc(sem("f_rc"), 1)
                    dve.scalar_tensor_tensor(selv[:, n, :], src, 0.9 * GONE, ex[:, n, :], ALU.is_le, ALU.mult)\
                        .then_inc(sem("f_sel"), 1)
                    dve.wait_ge(sem("f_rc"), at(FFN, "f_rc", g, u + 1))
                    dve.wait_ge(sem("f_sel"), at(FFN, "f_sel", g, u + 1))
                    if n == 1:
                        dve.wait_ge(sem("f_tp"), at(FFN, "f_tp", g, GT + t))
                        dve.scalar_tensor_tensor(fxs[:], selv[:, n, :], frc[:, n:n + 1], fxn[:, t, :],
                                                 ALU.mult, ALU.mult).then_inc(sem("f_xs"), 1)
                    else:
                        dve.wait_ge(sem("full_done"), at(FFN, "full_done", g, t + 1))
                        dve.scalar_tensor_tensor(ftmp[:, t % 2, :], bank[4 + t % 2][:], frc[:, n:n + 1],
                                                 selv[:, n, :], ALU.mult, ALU.mult).then_inc(sem("full_free"), 1)
                if t >= 1:
                    combine(t - 1)
            combine(GT - 1)

        def sp_experts(sp):
            sp.wait_ge(sem("att1_over"), 5)
            sp.dma_start(gw[:], gate_w.rearrange("(p c) e -> p c e", c=C)).then_inc(sem("gate_in"), 16)
            for e in range(E):
                sp.dma_start(w_in_sb[:, e * C * D:(e + 1) * C * D],
                             w_in[e].rearrange("(p c) n -> p (c n)", c=C)).then_inc(sem("w_in"), 16)
                sp.dma_start(w_dn_sb[:, e * 2 * D:(e + 1) * 2 * D].rearrange("p (i n) -> p i n", i=2),
                             w_down[e].rearrange("(i p) n -> p i n", p=P)).then_inc(sem("w_in"), 16)
            for r in range(4):
                sp.wait_ge(sem(f"scattered{r}"), 16 * TILES // 4)

            def load(k, j):
                sp.dma_start(tx[:, j, :], xs_dram[bass.ds(k * P, P), :]).then_inc(sem(f"tx_in{j}"), 16)

            def store(k, j):
                sp.wait_ge(sem("e_yo"), k + 3)
                sp.dma_start(ys_dram[bass.ds(k * P, P), :], yo[:, j, :]).then_inc(sem(f"ys_out{j}"), 16)

            for k in range(4):
                if k >= 2:
                    sp.wait_ge(sem("tx_used"), k - 1)
                load(k, k % 2)
            store(0, 0)
            with sp.Fori(2, SLOT_TILES // 2) as i:
                for j in range(2):
                    sp.wait_ge(sem("tx_used"), 2 * i + j - 1)
                    load(2 * i + j, j)
                    store(2 * i + j - 3, 1 - j)
            sp.wait_ge(sem("tx_used"), SLOT_TILES - 2)
            load(SLOT_TILES - 1, 0)
            for k in range(SLOT_TILES - 4, SLOT_TILES):
                store(k, k % 2)
            for t in range(TILES):
                sp.wait_ge(sem("final"), t + 1)
                sp.dma_start(out_tiles[:, t, :], xr[:, t, :]).then_inc(sem("out_done"), 16)
            sp.wait_ge(sem("out_done"), 16 * TILES)

        def pool_gate_group(pool, g):
            hold(pool, "g_mv", at(GATE, "g_mv", g, GT))
            pool.tensor_tensor(ve[:], mv[:, :, 1], eps_c[:, 0:GT], ALU.add).then_inc(sem("g_ve"), 1)
            pool.wait_ge(sem("g_ve"), at(GATE, "g_ve", g, 1))
            pool.tensor_tensor(rs[:], ve[:], expo[:, 0:GT], ALU.pow).then_inc(sem("g_rs"), 1)

        def dve_gate_group(dve, g):
            for t in range(GT):
                dve.bn_stats(bn[:, t, :], tile_of(xr, g, t)).then_inc(sem("g_bn"), 1)
            for t in range(GT):
                hold(dve, "g_bn", at(GATE, "g_bn", g, t + 1))
                dve.bn_aggr(mv[:, t, :], bn[:, t, :]).then_inc(sem("g_mv"), 1)
            hold(dve, "g_rs", at(GATE, "g_rs", g, 1))
            dve.tensor_copy(mv3[:, bass.ds(g * GT, GT), :], mv[:]).then_inc(sem("g_keep"), 1)
            dve.tensor_copy(rs3[:, bass.ds(g * GT, GT)], rs[:]).then_inc(sem("g_keep"), 1)
            for t in range(GT):
                hold(dve, "g_tp", at(GATE, "g_tp", g, t + 1))
                dve.tensor_scalar(mxn[:, t % 2, :], tile_of(xr, g, t), mv[:, t, 0:1], rs[:, t:t + 1],
                                  ALU.subtract, ALU.mult).then_inc(sem("g_xn"), 1)
            for t in range(GT):
                hold(dve, "g_lg", at(GATE, "g_lg", g, t + 1))
                dve.tensor_copy(lgt[:, bass.ds(g * GT + t, 1), :].rearrange("p a e -> p (a e)"),
                                bank[2 + t % 2][:, 0:E]).then_inc(sem("g_cp"), 1)

        def pe_gate_group(pe, g):
            for t in range(GT):
                pe.wait_ge(sem("g_xn"), at(GATE, "g_xn", g, t + 1))
                pe.wait_ge(sem("g_te"), at(GATE, "g_te", g, t + 1))
                for c in range(C):
                    mm = pe.transpose(bank[t % 2][:, P * c:P * c + P], mxn[:, t % 2, c::C], ident[:])
                mm.then_inc(sem("g_tp"), 1)
                pe.wait_ge(sem("g_te"), at(GATE, "g_te", g, t + 3))
                pe.wait_ge(sem("g_cp"), at(GATE, "g_cp", g, t + 1))
                for c in range(C):
                    mm = pe.matmul(bank[2 + t % 2][:, 0:E], mxT[:, t % 2, P * c:P * c + P], gw[:, c, :],
                                   start=(c == 0), stop=(c == C - 1))
                mm.then_inc(sem("g_lg"), 1)

        def act_gate_group(act, g):
            for t in range(GT):
                act.wait_ge(sem("g_tp"), at(GATE, "g_tp", g, t + 3))
                act.activation(mxT[:, t % 2, :], bank[t % 2][:], ACT.Copy).then_inc(sem("g_te"), 1)

        def bc(ap, n):
            return ap.unsqueeze(2).broadcast_to([P, ap.shape[1], n])

        def over(ap, n):
            return ap.unsqueeze(1).broadcast_to([P, n, ap.shape[1]])

        def pool_sort(pool):
            pool.iota(iota_e[:], pattern=[[1, E]], base=0, channel_multiplier=0,
                      allow_small_or_imprecise_dtypes=True).then_inc(sem("s_const"), 1)
            pool.iota(slot_i[:], pattern=[[1, SLOT_TILES]], base=0, channel_multiplier=0,
                      allow_small_or_imprecise_dtypes=True).then_inc(sem("s_const"), 1)
            pool.memset(ones[:], 1.0).then_inc(sem("s_const"), 1)
            pool.wait_ge(sem("s_const"), 3)
            pool.affine_select(out=tri[:], in_=ones[:], compare_op=ALU.is_gt, fill=0.0, base=0,
                               pattern=[[1, P]], channel_multiplier=-1).then_inc(sem("s_const"), 1)

        def dve_sort(dve):
            n = [0]

            def then(ins):
                n[0] += 1
                ins.then_inc(sem("s_step"), 1)
                dve.wait_ge(sem("s_step"), n[0])

            dve.wait_ge(sem("g_cp"), 2 + 4 * GROUPS)
            dve.wait_ge(sem("s_const"), 4)
            dve.tensor_reduce(top_v[:], lgt[:], AX.X, ALU.max).then_inc(sem("s_top"), 1)
            dve.wait_ge(sem("s_top"), 1)
            then(dve.tensor_tensor(below[:], lgt[:], bc(top_v[:], E), ALU.not_equal))
            then(dve.scalar_tensor_tensor(cand[:], below[:], float(E), over(iota_e[:], TILES), ALU.mult, ALU.add))
            then(dve.tensor_reduce(selx[:], cand[:], AX.X, ALU.min))
            dve.tensor_tensor(onehot[:], over(iota_e[:], TILES), bc(selx[:], E), ALU.is_equal)\
                .then_inc(sem("s_onehot"), 1)
            dve.wait_ge(sem("s_counts"), 1)
            then(dve.tensor_copy(own[:], bank[1][:, 0:TILES * E].rearrange("p (t e) -> p t e", e=E)))
            then(dve.tensor_copy(cnt[:, 0, :, :], own[:]))
            src = 0
            shift = 1
            while shift < TILES:
                then(dve.tensor_copy(cnt[:, 1 - src, 0:shift, :], cnt[:, src, 0:shift, :]))
                then(dve.tensor_tensor(cnt[:, 1 - src, shift:, :], cnt[:, src, shift:, :],
                                       cnt[:, src, 0:TILES - shift, :], ALU.add))
                src = 1 - src
                shift *= 2
            then(dve.tensor_scalar(tot[:], cnt[:, src, TILES - 1, :], float(P - 1), None, ALU.add))
            then(dve.tensor_copy(toti[:], tot[:]))
            then(dve.tensor_scalar(toti[:], toti[:], P.bit_length() - 1, None, ALU.arith_shift_right))
            then(dve.tensor_copy(tiles_f[:], toti[:]))
            then(dve.memset(start[:], 0.0))
            for e in range(E):
                then(dve.tensor_tensor(start[:, e + 1:e + 2], start[:, e:e + 1], tiles_f[:, e:e + 1], ALU.add))
            then(dve.tensor_tensor(cmp[:], bc(slot_i[:], E - 1), over(start[:, 1:E], SLOT_TILES), ALU.is_ge))
            then(dve.tensor_reduce(slot_e[:], cmp[:], AX.X, ALU.add))
            dve.tensor_copy(slot_ei[:], slot_e[:]).then_inc(sem("slot_expert"), 1)
            then(dve.tensor_tensor(prod[:], cnt[:, src, :, :], own[:], ALU.subtract))
            then(dve.tensor_tensor(rank[:], bank[0][:, 0:TILES * E].rearrange("p (t e) -> p t e", e=E), prod[:],
                                   ALU.add))
            then(dve.scalar_tensor_tensor(prod[:], over(start[:, 0:E], TILES), float(P), rank[:], ALU.mult, ALU.add))
            then(dve.tensor_tensor(rank[:], prod[:], onehot[:], ALU.mult))
            then(dve.tensor_reduce(posf[:], rank[:], AX.X, ALU.add))
            dve.tensor_copy(posi[:], posf[:]).then_inc(sem("places"), 1)
            dve.wait_ge(sem("s_exp"), 1)
            then(dve.tensor_scalar(rwe[:], rwe[:], 1.0, None, ALU.add))
            then(dve.reciprocal(rw[:], rwe[:]))
            then(dve.tensor_tensor(srs[:], rs3[:], rw[:], ALU.mult))
            for t in range(TILES):
                if t >= 4:
                    dve.wait_ge(sem(f"scattered{t % 4}"), 16 * (t // 4))
                dve.tensor_scalar(xs[:, t % 4, :], xr[:, t, :], mv3[:, t, 0:1], srs[:, t:t + 1], ALU.subtract,
                                  ALU.mult).then_inc(sem("s_xs"), 1)

        def pe_sort(pe):
            pe.wait_ge(sem("s_onehot"), 1)
            flat = onehot[:].rearrange("p t e -> p (t e)")
            pe.matmul(bank[0][:, 0:TILES * E], tri[:], flat, start=True, stop=True)
            pe.matmul(bank[1][:, 0:TILES * E], ones[:], flat, start=True, stop=True).then_inc(sem("s_counts"), 1)

        def pool_scatter(pool):
            pool.wait_ge(sem("places"), 1)
            pool.wait_ge(sem("slots_zeroed"), 16)
            for t in range(TILES):
                pool.wait_ge(sem("s_xs"), t + 1)
                pool.indirect_dma_start(xs_dram, bass.IndirectOffsetOnAxis(posi[:, t:t + 1], 0), xs[:, t % 4, :], None)\
                    .then_inc(sem(f"scattered{t % 4}"), 16)

        def pairs(eng, step):
            step(0, 0, True)
            with eng.Fori(0, (SLOT_TILES - 1) // 2) as i:
                step(2 * i + 1, 1, False)
                step(2 * i + 2, 0, False)

        def pe_experts(pe):
            pe.wait_ge(sem("slot_expert"), 1)
            pe.wait_ge(sem("w_in"), 16 * 2 * E)

            def turn(k, j, n):
                pe.wait_ge(sem(f"tx_in{j}"), 16 * n + 16)
                pe.wait_ge(sem("e_te"), k + 1)
                for c in range(C):
                    mm = pe.transpose(bank[j][:, P * c:P * c + P], tx[:, j, c::C], ident[:])
                mm.then_inc(sem("tx_used"), 1)

            def into(k, j):
                e = pe.value_load(slot_ei[0:1, bass.ds(k, 1)], min_val=0, max_val=E - 1)
                pe.wait_ge(sem("e_te"), k + 3)
                pe.wait_ge(sem("e_hh"), k + 1)
                for c in range(C):
                    mm = pe.matmul(bank[2 + j][:], txT[:, j, P * c:P * c + P],
                                   w_in_sb[:, bass.ds(e * (C * D) + c * D, D)], start=(c == 0), stop=(c == C - 1))
                mm.then_inc(sem("e_gu"), 1)

            def turn_h(k, j):
                pe.wait_ge(sem("e_hh"), k + 3)
                pe.wait_ge(sem("e_hT"), k + 1)
                for i in range(2):
                    mm = pe.transpose(bank[4 + j][:, P * i:P * i + P], hh[:, j, P * i:P * i + P], ident[:])
                mm.then_inc(sem("e_th"), 1)

            def down(k, j):
                e = pe.value_load(slot_ei[0:1, bass.ds(k, 1)], min_val=0, max_val=E - 1)
                pe.wait_ge(sem("e_hT"), k + 3)
                pe.wait_ge(sem("e_yo"), k + 1)
                for i in range(2):
                    mm = pe.matmul(bank[6 + j][:], hT[:, j, P * i:P * i + P],
                                   w_dn_sb[:, bass.ds(e * (2 * D) + i * D, D)], start=(i == 0), stop=(i == 1))
                mm.then_inc(sem("e_dn"), 1)

            turn(0, 0, 0)
            into(0, 0)
            turn(1, 1, 0)
            with pe.Fori(0, (SLOT_TILES - 3) // 2) as i:
                into(2 * i + 1, 1)
                turn_h(2 * i, 0)
                turn(2 * i + 2, 0, i + 1)
                down(2 * i, 0)
                into(2 * i + 2, 0)
                turn_h(2 * i + 1, 1)
                turn(2 * i + 3, 1, i + 1)
                down(2 * i + 1, 1)
            last = SLOT_TILES - 1
            into(last - 1, 1)
            turn_h(last - 2, 0)
            turn(last, 0, last // 2)
            down(last - 2, 0)
            into(last, 0)
            turn_h(last - 1, 1)
            down(last - 1, 1)
            turn_h(last, 0)
            down(last, 0)

        def act_experts(act):
            def step(k, j, first):
                act.wait_ge(sem("tx_used"), k + 1)
                act.activation(txT[:, j, :], bank[j][:], ACT.Copy).then_inc(sem("e_te"), 1)
                if not first:
                    gated(k - 1, 1 - j)

            def gated(k, j):
                act.wait_ge(sem("e_gu"), k + 1)
                act.activation(sg[:, j, :], bank[2 + j][:, 0:I], ACT.Silu).then_inc(sem("e_sg"), 1)
            pairs(act, step)
            gated(SLOT_TILES - 1, 0)

        def dve_experts(dve):
            def step(k, j, first):
                dve.wait_ge(sem("e_sg"), k + 1)
                dve.tensor_tensor(hh[:, j, :], sg[:, j, :], bank[2 + j][:, I:2 * I], ALU.mult).then_inc(sem("e_hh"), 1)
                if not first:
                    back(k - 1, 1 - j)

            def back(k, j):
                dve.wait_ge(sem("e_th"), k + 1)
                dve.tensor_copy(hT[:, j, :], bank[4 + j][:, 0:I]).then_inc(sem("e_hT"), 1)
                dve.wait_ge(sem("e_dn"), k + 1)
                dve.wait_ge(sem(f"ys_out{j}"), ys_value(k, j))
                dve.tensor_copy(yo[:, j, :], bank[6 + j][:]).then_inc(sem("e_yo"), 1)
            pairs(dve, step)
            back(SLOT_TILES - 1, 0)

        def ys_value(k, j):
            return (k - j) * 8 + 16

        def pool_gather(pool):
            pool.wait_ge(sem("ys_out0"), 16 + 16 * ((SLOT_TILES + 1) // 2))
            pool.wait_ge(sem("ys_out1"), 16 + 16 * (SLOT_TILES // 2))
            pool.wait_ge(sem("tx_used"), SLOT_TILES)
            for t in range(TILES):
                if t >= 3:
                    pool.wait_ge(sem("final"), t - 2)
                pool.indirect_dma_start(yg[:, t % 3, :], None, ys_dram, bass.IndirectOffsetOnAxis(posi[:, t:t + 1], 0))\
                    .then_inc(sem(f"gathered{t % 3}"), 16)

        def dve_final(dve):
            for t in range(TILES):
                dve.wait_ge(sem(f"gathered{t % 3}"), 16 * (t // 3 + 1))
                dve.tensor_tensor(xr[:, t, :], xr[:, t, :], yg[:, t % 3, :], ALU.add).then_inc(sem("final"), 1)

        @block.sync
        def _(sp):
            def load_weights(layer):
                if layer == 1:
                    sp.wait_ge(sem("ffn_over"), 5)
                w = (wq0, wk0, wv0, wo0) if layer == 0 else (wq1, wk1, wv1, wo1)
                sp.dma_start(ctx_sb[:], ctxT.rearrange("b (p c) k -> p b c k", c=C)).then_inc(sem("kv_in"), 16)
                for c in range(C):
                    for j in range(4):
                        sp.dma_start(ctx_b[:, :, c, KB * j:KB * j + KB],
                                     ctxT.rearrange("b (p c) k -> p b c k", c=C)[:, :, c, KB0:]).then_inc(sem("kv_in"), 16)
                sp.dma_start(wk[:], w[1].rearrange("(p c) n -> p c n", c=C)).then_inc(sem("kv_in"), 16)
                sp.dma_start(wv[:], w[2].rearrange("(p c) n -> p c n", c=C)).then_inc(sem("kv_in"), 16)
                sp.dma_start(wq[:], w[0].rearrange("(p c) n -> p c n", c=C)).then_inc(sem("kv_in"), 16)
                sp.dma_start(wo[:], w[3].rearrange("(c p) n -> p c n", c=C)).then_inc(sem("kv_in"), 16)
                if layer == 1:
                    sp.dma_start(bq[:], bq1).then_inc(sem("bias_in"), 16)
                    sp.dma_start(bk[:], bk1).then_inc(sem("bias_in"), 16)
                    sp.dma_start(bv[:], bv1.partition_broadcast(P)).then_inc(sem("bias_in"), 16)
                    sp.dma_start(bo[:], bo1.partition_broadcast(P)).then_inc(sem("bias_in"), 16)

            sp.dma_start(xr[:, 0:GT, :], x_tiles[:, 0:GT, :]).then_inc(sem("x_in"), 16)
            load_weights(0)
            sp.wait_ge(sem("const"), 5)
            sp.dma_start(xs_dram.rearrange("(t p) d -> p t d", p=P),
                         zero_row[:].unsqueeze(1).broadcast_to([P, SLOT_TILES, D])).then_inc(sem("slots_zeroed"), 16)
            sp.wait_ge(sem("kv_over"), 4)
            for b in range(B):
                with sp.Fori(0, GPB) as i:
                    g = b * GPB + i
                    sp.wait_ge(sem("mask_free"), g + 1)
                    if b == 0:
                        sp.wait_ge(sem("x_in"), 16 * g + 16)
                        sp.dma_start(xr[:, bass.ds(GT * (g + 1), GT), :], x_tiles[:, bass.ds(GT * (g + 1), GT), :])\
                            .then_inc(sem("x_in"), 16)
                    sp.dma_start(mk_t[:], mask[b, 0].rearrange("(t p) k -> p t k", p=P)[:, bass.ds(GT * i, GT), :])\
                        .then_inc(sem("mask_in"), 16)
                    sp.dma_start(mk_a[:], maskT[b, 0:KA, bass.ds(GW * i, GW)]).then_inc(sem("mask_in"), 16)
                    for j in range(4):
                        sp.dma_start(mk_b[KB * j:KB * j + KB, :], maskT[b, KB0:KEYS, bass.ds(GW * i, GW)])\
                            .then_inc(sem("mask_in"), 16)
                if b == 0:
                    for g in range(GPB + 1, GROUPS):
                        sp.wait_ge(sem("x_in"), 16 * g)
                        sp.dma_start(xr[:, GT * g:GT * g + GT, :], x_tiles[:, GT * g:GT * g + GT, :])\
                            .then_inc(sem("x_in"), 16)
            sp.sem_inc(sem("att0_over"), 1)
            sp.wait_ge(sem("att0_over"), 5)
            for n, (a, b_, g_, be_, l_, lb_) in enumerate([(so_cw, so_cb, so_g, so_be, so_lw, so_lb),
                                                           (si_cw, si_cb, si_g, si_be, si_lw, si_lb)]):
                sp.dma_start(cw[:, n, :], a).then_inc(sem("ffn_in"), 16)
                sp.dma_start(cb[:, n:n + 1], b_.rearrange("(p a) -> p a", a=1)).then_inc(sem("ffn_in"), 16)
                sp.dma_start(gam[:, n:n + 1], g_.rearrange("(p a) -> p a", a=1)).then_inc(sem("ffn_in"), 16)
                sp.dma_start(bet[:, n:n + 1], be_.rearrange("(p a) -> p a", a=1)).then_inc(sem("ffn_in"), 16)
                sp.dma_start(lw[:, n, :], l_).then_inc(sem("ffn_in"), 16)
                sp.dma_start(lb[:, n, :], lb_.partition_broadcast(P)).then_inc(sem("ffn_in"), 16)
            sp.dma_start(wf[:], w_ffn.rearrange("(p c) n -> p c n", c=C)).then_inc(sem("ffn_in"), 16)
            sp.dma_start(bf[:], b_ffn.partition_broadcast(P)).then_inc(sem("ffn_in"), 16)
            sp.sem_inc(sem("ffn_over"), 1)
            load_weights(1)
            sp.sem_inc(sem("att1_over"), 1)
            sp_experts(sp)

        @block.gpsimd
        def _(pool):
            pool_constants(pool)
            pool_att_setup(pool, 0)
            enter_groups(pool, 0)
            groups(pool, 0, lambda g, b, G: pool_att_group(pool, 0, g, b, G))
            leave(pool, "att0_over", "a_rs", 8)
            with pool.Fori(0, GROUPS) as g:
                pool_stats_group(pool, g)
            pool_batch_norm(pool)
            with pool.Fori(0, GROUPS) as g:
                pool_ffn_group(pool, g)
            leave(pool, "ffn_over", "f_x", 2 + 8 * 4)
            pool_att_setup(pool, 1)
            enter_groups(pool, 1)
            groups(pool, 1, lambda g, b, G: pool_att_group(pool, 1, g, b, G))
            leave(pool, "att1_over", "a_xb", 8)
            pool.wait_ge(sem("att1_over"), 5)
            pool_sort(pool)
            with pool.Fori(0, GROUPS) as g:
                pool_gate_group(pool, g)
            pool_scatter(pool)
            pool_gather(pool)

        @block.tensor
        def _(pe):
            pe_kv(pe, 0)
            pe_att_start(pe, 0)
            groups(pe, 0, lambda g, b, G: pe_att_group(pe, 0, g, b, G))
            leave(pe, "att0_over", "lin_done", 8 * 28)
            pe.sem_inc(sem("t_tp"), 4)
            pe.wait_ge(sem("att0_over"), 5)
            pe.wait_ge(sem("ffn_in"), 14 * 16)
            with pe.Fori(0, GROUPS) as g:
                pe_stats_group(pe, g)
            with pe.Fori(0, GROUPS) as g:
                pe_ffn_group(pe, g)
            leave(pe, "ffn_over", "in_done", 8 * 4)
            pe.wait_ge(sem("ffn_over"), 5)
            pe_kv(pe, 1)
            pe_att_start(pe, 1)
            groups(pe, 1, lambda g, b, G: pe_att_group(pe, 1, g, b, G))
            leave(pe, "att1_over", "lin_done", 16 * 28)
            pe.wait_ge(sem("att1_over"), 5)
            pe.sem_inc(sem("g_tp"), 2)
            pe.wait_ge(sem("gate_in"), 16)
            with pe.Fori(0, GROUPS) as g:
                pe_gate_group(pe, g)
            pe_sort(pe)
            pe_experts(pe)

        @block.scalar
        def _(act):
            act.sem_inc(sem("kT_free"), 2)
            act.sem_inc(sem("a_te"), 2)
            act_kv(act, 0)
            enter_groups(act, 0)
            groups(act, 0, lambda g, b, G: act_att_group(act, 0, g, b, G))
            leave(act, "att0_over", "p_done", 8 * 20)
            act.sem_inc(sem("t_te"), 2)
            act.sem_inc(sem("f_te"), 2)
            act.wait_ge(sem("att0_over"), 5)
            act.wait_ge(sem("ffn_in"), 14 * 16)
            with act.Fori(0, GROUPS) as g:
                act_stats_group(act, g)
            act.wait_ge(sem("b_sc"), 3)
            with act.Fori(0, GROUPS) as g:
                act_ffn_group(act, g)
            leave(act, "ffn_over", "f_te", 2 + 8 * 8)
            act.wait_ge(sem("ffn_over"), 5)
            act_kv(act, 1)
            enter_groups(act, 1)
            groups(act, 1, lambda g, b, G: act_att_group(act, 1, g, b, G))
            leave(act, "att1_over", "p_done", 16 * 20)
            act.sem_inc(sem("g_te"), 2)
            act.sem_inc(sem("e_te"), 2)
            act.wait_ge(sem("att1_over"), 5)
            with act.Fori(0, GROUPS) as g:
                act_gate_group(act, g)
            act.wait_ge(sem("s_top"), 1)
            act.activation(rwe[:], top_v[:], ACT.Exp, scale=-1.0).then_inc(sem("s_exp"), 1)
            act_experts(act)

        @block.vector
        def _(dve):
            dve.sem_inc(sem("k_split"), 2)
            dve.sem_inc(sem("v_free"), 2)
            dve.sem_inc(sem("lin_free"), 2)
            dve.sem_inc(sem("a_sm"), 2)
            dve.sem_inc(sem("a_at"), 1)
            dve.sem_inc(sem("mask_free"), 1)
            dve_kv(dve, 0)
            enter_groups(dve, 0)
            groups(dve, 0, lambda g, b, G: dve_att_group(dve, 0, g, b, G))
            leave(dve, "att0_over", "lin_free", 2 + 8 * 28)
            dve.sem_inc(sem("t_gs"), 2)
            dve.sem_inc(sem("lg_free"), 2)
            dve.sem_inc(sem("full_free"), 2)
            dve.sem_inc(sem("f_x"), 2)
            dve.sem_inc(sem("f_xs"), 4)
            dve.sem_inc(sem("f_sum"), 2)
            dve.wait_ge(sem("att0_over"), 5)
            dve.wait_ge(sem("ffn_in"), 14 * 16)
            with dve.Fori(0, GROUPS) as g:
                dve_stats_group(dve, g)
            dve_batch_norm(dve)
            with dve.Fori(0, GROUPS) as g:
                dve_ffn_group(dve, g)
            leave(dve, "ffn_over", "f_sum", 2 + 8 * 4)
            dve.wait_ge(sem("ffn_over"), 5)
            dve_kv(dve, 1)
            enter_groups(dve, 1)
            groups(dve, 1, lambda g, b, G: dve_att_group(dve, 1, g, b, G))
            leave(dve, "att1_over", "lin_free", 2 + 16 * 28)
            dve.sem_inc(sem("ys_out0"), 16)
            dve.sem_inc(sem("ys_out1"), 16)
            dve.sem_inc(sem("g_cp"), 2)
            dve.sem_inc(sem("e_hh"), 2)
            dve.sem_inc(sem("e_hT"), 2)
            dve.sem_inc(sem("e_yo"), 2)
            dve.wait_ge(sem("att1_over"), 5)
            with dve.Fori(0, GROUPS) as g:
                dve_gate_group(dve, g)
            dve_sort(dve)
            dve_experts(dve)
            dve_final(dve)


_INS = ["x", "ctxT", "mask", "maskT", "wq0", "wk0", "wv0", "wo0", "w_ffn", "b_ffn", "so_cw", "so_cb", "so_g", "so_be",
        "so_lw", "so_lb", "si_cw", "si_cb", "si_g", "si_be", "si_lw", "si_lb", "wq1", "bq1", "wk1", "bk1", "wv1", "bv1",
        "wo1", "bo1", "gate_w", "w_in", "w_down"]


def kernel(**inputs):
    import numpy as _np
    import concourse.bacc as _bacc
    from concourse import mybir as _mybir
    from concourse.bass_utils import run_bass_kernel_spmd as _run

    a = {k: _np.asarray(v) for k, v in inputs.items()}
    f, t = "L0_ffn_", "L1_xattn_"
    given = dict(
        x=a["x"], ctxT=a["ctx_1024"].transpose(0, 2, 1), mask=a["mask_Bx1xSxS2_ff0"],
        maskT=a["mask_Bx1xSxS2_ff0"][:, 0].transpose(0, 2, 1),
        wq0=a["L0_xattn_wq"].reshape(D, D), wk0=a["L0_xattn_wk"].reshape(D, D), wv0=a["L0_xattn_wv"].reshape(D, D),
        wo0=a["L0_xattn_wo"].reshape(D, D), w_ffn=a[f + "weight"], b_ffn=a[f + "bias"],
        so_cw=a[f + "so_conv_w"], so_cb=a[f + "so_conv_b"], so_g=a[f + "so_gamma"], so_be=a[f + "so_beta"],
        so_lw=a[f + "so_lin_w"].T, so_lb=a[f + "so_lin_b"], si_cw=a[f + "si_conv_w"], si_cb=a[f + "si_conv_b"],
        si_g=a[f + "si_gamma"], si_be=a[f + "si_beta"], si_lw=a[f + "si_lin_w"].T, si_lb=a[f + "si_lin_b"],
        wq1=a[t + "W_Q"].T, bq1=a[t + "b_Q"].reshape(C, P).T, wk1=a[t + "W_K"].T, bk1=a[t + "b_K"].reshape(C, P).T, wv1=a[t + "W_V"].T,
        bv1=a[t + "b_V"], wo1=a[t + "W_O"].T, bo1=a[t + "b_O"], gate_w=a["L1_ffn_gate_w"].T,
        w_in=_np.concatenate([a["L1_ffn_w_gate"], a["L1_ffn_w_up"]], axis=1).transpose(0, 2, 1),
        w_down=a["L1_ffn_w_down"].transpose(0, 2, 1))
    nc = _bacc.Bacc("TRN2", target_bir_lowering=False, num_devices=1)
    arrays, args = {}, []
    for name in _INS:
        v = _np.ascontiguousarray(given[name])
        arrays[f"in_{name}"] = v
        args.append(nc.dram_tensor(f"in_{name}", v.shape, _mybir.dt.from_np(v.dtype), kind="ExternalInput").ap())
    args.append(nc.dram_tensor("out_x", (B, S, D), F32, kind="ExternalOutput").ap())
    program(nc, *args)
    r = _run(nc, [arrays], core_ids=[0])
    return r.results[0]["out_x"]
```

```python
from contextlib import ExitStack

import concourse.bass as bass
from concourse import mybir

F32 = mybir.dt.float32
F32R = mybir.dt.float32r
I32 = mybir.dt.int32
U32 = mybir.dt.uint32
ACT = mybir.ActivationFunctionType
ALU = mybir.AluOpType
AX = mybir.AxisListType

P = 128
D = 512
C = D // P
B = 2
S = 2048
N = B * S
TILES = N // P
GT = 4
GW = GT * P
GROUPS = TILES // GT
GPB = GROUPS // B
H = 16
DH = D // H
QUADS = H // 4
KEYS = 154
KA = 128
KB = 32
KB0 = KEYS - KB
DUP = KA - KB0
QK = 4 * (KA + KB)
EPS = 1e-5
K_TOP = 32
E = 8
I = 256
SLOT_TILES = TILES + E - 1
GONE = -3.0e38

ATT = dict(a_bn=4, a_mv=4, a_ve=1, a_rs=1, a_xn=4, a_tp=4, a_te=4, a_qh=4, qm_done=24, qm_free=24, a_red=20, a_mx=1,
           a_mt=1, a_mh=1, a_ml=1, sc_done=20, a_sm=20, p_done=20, pv_done=4, a_raw=4, a_rc=1, a_rh=1, a_rl=1,
           spread=4, a_at=4, o_done=4, o_free=4, o_bn=4, o_mv=4)
STAT = dict(t_bn=4, t_mv=4, t_ve=1, t_rs=1, t_xn=4, t_tp=4, t_te=4, t_xc=8, t_gs=2)
FFN = dict(f_xn=4, f_xb=1, f_tp=8, f_te=8, f_ge=2, lg_done=8, lg_free=8, f_top=64, f_nm=8, f_ex=8, f_rc=8, f_sel=8,
           f_xs=4, full_done=4, full_free=4, in_done=4, f_sum=4, f_x=4)
GATE = dict(g_bn=4, g_mv=4, g_ve=1, g_rs=1, g_xn=4, g_tp=4, g_te=4, g_lg=4, g_cp=4)


def program(nc, x, ctxT, mask, maskT, wq0, wk0, wv0, wo0, w_ffn, b_ffn, so_cw, so_cb, so_g, so_be, so_lw, so_lb,
            si_cw, si_cb, si_g, si_be, si_lw, si_lb, wq1, bq1, wk1, bk1, wv1, bv1, wo1, bo1, gate_w, w_in, w_down, out):
    xs_dram = nc.dram_tensor("sorted_tokens", (SLOT_TILES * P, D), F32, kind="Internal").ap()
    ys_dram = nc.dram_tensor("sorted_outputs", (SLOT_TILES * P, D), F32, kind="Internal").ap()
    x_tiles = x.rearrange("b (t p) d -> p (b t) d", p=P)
    out_tiles = out.rearrange("b (t p) d -> p (b t) d", p=P)

    top = ExitStack()
    with top:
        sems = {}

        def sem(name):
            if name not in sems:
                sems[name] = top.enter_context(nc.semaphore(name))
            return sems[name]

        def at(table, name, group, k):
            return group * table[name] + k

        def scope():
            stack = ExitStack()

            def sb(name, shape, dt=F32):
                return stack.enter_context(nc.sbuf_tensor(name, shape, dt))
            return stack, sb

        bank = [top.enter_context(nc.psum_tensor(f"bank{i}", [P, D], F32)) for i in range(8)]

        def sb(name, shape, dt=F32):
            return top.enter_context(nc.sbuf_tensor(name, shape, dt))

        xr = sb("x_res", [P, TILES, D])
        ident = sb("ident", [P, P])
        zero = sb("zero", [P, C])
        zero_row = sb("zero_row", [P, D])
        bn = sb("bn", [P, GT, 6])
        mv = sb("mv", [P, GT, 2])
        ve = sb("ve", [P, GT])
        expo = sb("expo", [P, TILES])
        rs = sb("rs", [P, GT])
        bn_o = sb("bn_o", [P, GT, 6])
        mv_o = sb("mv_o", [P, GT, 2])
        mv_all = sb("mv_all", [P, TILES, 2])
        rs_all = sb("rs_all", [P, TILES])
        ve_all = sb("ve_all", [P, TILES])
        eps_c = sb("eps_c", [P, TILES])

        att, sb = scope()
        wq = sb("wq", [P, C, D])
        wo = sb("wo", [P, C, D])
        kh = sb("kh", [P, B, QUADS, QK], F32R)
        kl = sb("kl", [P, B, QUADS, QK], F32R)
        va = sb("va", [P, B, D])
        vb = sb("vb", [P, B, QUADS, P])
        one_a = sb("one_a", [P, QUADS, DH])
        one_b = sb("one_b", [P, QUADS, P])
        spread = sb("spread", [P, QUADS, 4, DH], F32R)
        sel = sb("sel", [P, H], F32R)
        sel_b = sb("sel_b", [P, QUADS, 4, KB], F32R)
        neg_max = sb("neg_max", [P, GW], F32R)
        bq = sb("bq", [P, C])
        bo = sb("bo", [P, D])
        mx = sb("mx", [P, GT, H])
        mxb = sb("mxb", [P, GT, H])
        work = ExitStack()
        xn = work.enter_context(nc.sbuf_tensor("xn", [P, GT, D], F32))
        xnT = work.enter_context(nc.sbuf_tensor("xnT", [P, C, GW], F32))
        qh = work.enter_context(nc.sbuf_tensor("qh", [P, C, GW], F32R))
        ql = work.enter_context(nc.sbuf_tensor("ql", [P, C, GW], F32R))
        lent = ExitStack()
        rc = lent.enter_context(nc.sbuf_tensor("rc", [P, GW], F32))
        rch = lent.enter_context(nc.sbuf_tensor("rch", [P, GW], F32R))
        rcl = lent.enter_context(nc.sbuf_tensor("rcl", [P, GW], F32R))
        lent.close()
        pr = work.enter_context(nc.sbuf_tensor("probs", [P, 10, GW], F32))
        attnT = xn
        mtmp = work.enter_context(nc.sbuf_tensor("mtmp", [P, 2, D], F32))
        mk_t = work.enter_context(nc.sbuf_tensor("mk_t", [P, GT, KEYS], F32))
        mk_a = work.enter_context(nc.sbuf_tensor("mk_a", [P, GW], F32))
        mk_b = work.enter_context(nc.sbuf_tensor("mk_b", [P, GW], F32))
        work.close()
        ctx_sb = work.enter_context(nc.sbuf_tensor("ctxT", [P, B, C, KEYS], F32))
        ctx_b = work.enter_context(nc.sbuf_tensor("ctx_b", [P, B, C, P], F32))
        wk = work.enter_context(nc.sbuf_tensor("wk", [P, C, D], F32))
        wv = work.enter_context(nc.sbuf_tensor("wv", [P, C, D], F32))
        bk = work.enter_context(nc.sbuf_tensor("bk", [P, C], F32))
        bks = work.enter_context(nc.sbuf_tensor("bks", [P, C], F32))
        bv = work.enter_context(nc.sbuf_tensor("bv", [P, D], F32))
        kf = work.enter_context(nc.sbuf_tensor("kf", [P, 2, KEYS], F32))
        work.close()
        att.close()

        ffn, sb = scope()
        xc = [sb("xc_so", [P, N]), sb("xc_si", [P, N])]
        mv2 = sb("mv2", [P, TILES, 2])
        rs2 = sb("rs2", [P, TILES])
        nm2 = sb("nm2", [P, TILES])
        gst = sb("gst", [P, 2, GROUPS, 6])
        gmv = sb("gmv", [P, 2, 2])
        gve = sb("gve", [P, 2])
        grs = sb("grs", [P, 2])
        gsc = sb("gsc", [P, 2])
        gbi = sb("gbi", [P, 2])
        gtm = sb("gtm", [P, 2])
        cw = sb("cw", [P, 2, 4])
        cb = sb("cb", [P, 2])
        gam = sb("gam", [P, 2])
        bet = sb("bet", [P, 2])
        wf = sb("wf", [P, C, D])
        lw = sb("lw", [P, 2, D])
        lb = sb("lb", [P, 2, D])
        bf = sb("bf", [P, D])
        fxn = sb("fxn", [P, GT, D])
        fxT = sb("fxT", [P, C, GW])
        ge = sb("ge", [P, 2, GW])
        Lg = sb("Lg", [P, 2, D])
        Wk = sb("Wk", [P, 2, 1, D])
        ex = sb("ex", [P, 2, D])
        m8 = sb("m8", [P, 2, 8])
        fnm = sb("fnm", [P, 2])
        fsum = sb("fsum", [P, 2])
        frc = sb("frc", [P, 2])
        selv = sb("selv", [P, 2, D])
        fxs = sb("fxs", [P, D])
        fxsT = sb("fxsT", [P, D])
        ftmp = sb("ftmp", [P, 2, D])
        fsm = sb("fsm", [P, 2, D])
        ffn.close()

        moe, sb = scope()
        w_in_sb = sb("w_in", [P, E * C * 2 * I])
        w_dn_sb = sb("w_down", [P, E * 2 * D])
        gw = sb("gate_w", [P, C, E])
        mxn = sb("mxn", [P, 2, D])
        mxT = sb("mxT", [P, 2, D])
        below = sb("below", [P, TILES, E])
        cand = sb("cand", [P, TILES, E])
        cmp = sb("cmp", [P, SLOT_TILES, E - 1])
        tiles_f = sb("tiles_f", [P, E])
        start = sb("start", [P, E + 1])
        lgt = sb("lgt", [P, TILES, E])
        mv3 = sb("mv3", [P, TILES, 2])
        rs3 = sb("rs3", [P, TILES])
        top_v = sb("top_v", [P, TILES])
        selx = sb("selx", [P, TILES])
        iota_e = sb("iota_e", [P, E])
        onehot = sb("onehot", [P, TILES, E])
        tri = sb("tri", [P, P])
        ones = sb("ones", [P, P])
        rank = sb("rank", [P, TILES, E])
        cnt = sb("cnt", [P, 2, TILES, E])
        own = sb("own", [P, TILES, E])
        tot = sb("tot", [P, E])
        toti = sb("toti", [P, E], I32)
        prod = sb("prod", [P, TILES, E])
        posf = sb("posf", [P, TILES])
        posi = sb("posi", [P, TILES], I32)
        slot_i = sb("slot_i", [P, SLOT_TILES])
        slot_e = sb("slot_e", [P, SLOT_TILES])
        slot_ei = sb("slot_ei", [P, SLOT_TILES], I32)
        rwe = sb("rwe", [P, TILES])
        rw = sb("rw", [P, TILES])
        srs = sb("srs", [P, TILES])
        xs = sb("xs", [P, 4, D])
        tx = xs
        txT = mxT
        sg = sb("sg", [P, 2, I])
        hh = sb("hh", [P, 2, I])
        hT = sb("hT", [P, 2, I])
        yo = mxn
        yg = xs
        moe.close()

        block = top.enter_context(nc.Block())

        def pipelined(eng, layer, ahead, body):
            ahead(0, 0)
            with eng.Fori(0, GPB - 1) as i:
                body(i, 0, i + 1, 0)
            body(GPB - 1, 0, GPB, 1)
            with eng.Fori(0, GPB - 1) as i:
                body(GPB + i, 1, GPB + i + 1, 1)
            body(GROUPS - 1, 1, None, None)

        def pool_constants(pool):
            pool.memset(ident[:], 0.0).then_inc(sem("c_0"), 1)
            pool.memset(zero[:], 0.0).then_inc(sem("const"), 1)
            pool.memset(zero_row[:], 0.0).then_inc(sem("const"), 1)
            pool.memset(expo[:], -0.5).then_inc(sem("const"), 1)
            pool.memset(eps_c[:], EPS).then_inc(sem("const"), 1)
            pool.wait_ge(sem("c_0"), 1)
            pool.affine_select(out=ident[:], in_=ident[:], compare_op=ALU.not_equal, fill=1.0, base=0,
                               pattern=[[-1, P]], channel_multiplier=1).then_inc(sem("const"), 1)

        def pool_att_setup(pool, layer):
            if layer == 1:
                pool.wait_ge(sem("ffn_over"), 5)
            zeroed = sem("zeroed")
            pool.memset(one_b[:], 0.0).then_inc(zeroed, 1)
            pool.memset(one_a[:], 0.0).then_inc(zeroed, 1)
            pool.memset(spread[:].bitcast(F32), 0.0).then_inc(zeroed, 1)
            pool.memset(sel[:].bitcast(F32), 0.0).then_inc(zeroed, 1)
            pool.memset(kh[:].bitcast(F32), 0.0).then_inc(zeroed, 1)
            pool.memset(kl[:].bitcast(F32), 0.0).then_inc(zeroed, 1)
            pool.memset(vb[:], 0.0).then_inc(zeroed, 1)
            pool.memset(neg_max[:].bitcast(F32), 0.0).then_inc(sem("selected"), 1)
            pool.wait_ge(zeroed, layer * 7 + 7)
            pool.affine_select(out=sel[:], in_=sel[:].bitcast(F32), compare_op=ALU.not_equal, fill=1.0, base=0,
                               pattern=[[-1, H]], channel_multiplier=1).then_inc(sem("selected"), 1)
            pool.affine_select(out=spread[:], in_=spread[:].bitcast(F32), compare_op=ALU.not_equal, fill=1.0, base=0,
                               pattern=[[-1, QUADS], [-32, 4], [0, DH]], channel_multiplier=1)\
                .then_inc(sem("selected"), 1)
            pool.affine_select(out=one_a[:], in_=one_a[:], compare_op=ALU.not_equal, fill=1.0, base=0,
                               pattern=[[-1, QUADS], [1, DH]], channel_multiplier=0).then_inc(sem("selected"), 1)
            pool.wait_ge(sem("selected"), layer * 7 + 4)
            pool.affine_select(out=sel[:], in_=sel[:].bitcast(F32), compare_op=ALU.not_equal, fill=1.0, base=-32,
                               pattern=[[-1, H]], channel_multiplier=1).then_inc(sem("selected"), 1)
            pool.memset(one_a[:, 0, QUADS:], 1.0).then_inc(sem("selected"), 1)
            pool.wait_ge(sem("selected"), layer * 7 + 6)
            pool.tensor_copy(sel_b[:].rearrange("p q h k -> p (q h) k"), sel[:].unsqueeze(2).broadcast_to([P, H, KB]))\
                .then_inc(sem("selected"), 1)
            pool.sem_inc(sem("kv_over"), 1)

        def hold(eng, name, value):
            eng.wait_ge(sem(name), value)
            eng.sem_inc(sem("held"), 1)

        def pool_att(pool, layer):
            def rstd(g, b):
                G = layer * GROUPS + g
                pool.wait_ge(sem("a_mv"), at(ATT, "a_mv", G, GT))
                pool.tensor_tensor(ve[:], mv[:, :, 1], eps_c[:, 0:GT], ALU.add).then_inc(sem("a_ve"), 1)
                pool.wait_ge(sem("a_ve"), at(ATT, "a_ve", G, 1))
                pool.tensor_tensor(rs[:], ve[:], expo[:, 0:GT], ALU.pow).then_inc(sem("a_rs"), 1)
                if layer == 1:
                    hold(pool, "a_xn", at(ATT, "a_xn", G, GT))
                    xg = xr[:, bass.ds(g * GT, GT), :]
                    pool.tensor_tensor(xg, xg, bo[:].unsqueeze(1).broadcast_to([P, GT, D]), ALU.add)\
                        .then_inc(sem("a_xb"), 1)

            def body(g, b, n, bn_):
                if n is not None:
                    rstd(n, bn_)
            pipelined(pool, layer, rstd, body)

        def tile_of(buf, g, t):
            return buf[:, bass.ds(g * GT + t, 1), :].rearrange("p a d -> p (a d)")

        def leave(eng, phase, last, value):
            eng.wait_ge(sem(last), value)
            eng.sem_inc(sem(phase), 1)

        def diagonal(u):
            for j in range(4):
                rows = slice(DH * j, DH * j + DH)
                yield rows, slice(0, KA), slice(KA * j, KA * j + KA)
                yield rows, slice(KB0, KEYS), slice(4 * KA + KB * j, 4 * KA + KB * j + KB)

        def pe_kv(pe, layer):
            pe.wait_ge(sem("kv_in"), (layer + 1) * 16 * (1 + 16 + 4))
            pe.wait_ge(sem("const"), 5)
            for b in range(B):
                for q in range(QUADS):
                    u = b * QUADS + q
                    pe.wait_ge(sem("kT_free"), layer * 8 + u + 1)
                    for c in range(C):
                        mm = pe.matmul(bank[u % 2][:, 0:KEYS], wk[:, c, P * q:P * q + P], ctx_sb[:, b, c, :],
                                       start=(c == 0), stop=(c == C - 1))
                    mm.then_inc(sem("kT_done"), 1)
            for b in range(B):
                pe.wait_ge(sem("v_free"), layer * 4 + 2 * b + 2)
                for c in range(C):
                    mm = pe.matmul(bank[4][:], ctx_sb[:, b, c, 0:KA], wv[:, c, :], start=(c == 0), stop=(c == C - 1))
                mm.then_inc(sem("v_done"), 1)
                for c in range(C):
                    mm = pe.matmul(bank[5][:], ctx_b[:, b, c, :], wv[:, c, :], start=(c == 0), stop=(c == C - 1))
                mm.then_inc(sem("v_done"), 1)
            pe.sem_inc(sem("kv_over"), 1)

        def act_kv(act, layer):
            scale = float(DH) ** -0.5
            if layer == 1:
                act.wait_ge(sem("bias_in"), 64)
                act.activation(bks[:], bk[:], ACT.Copy, scale=scale).then_inc(sem("bks"), 1)
                act.wait_ge(sem("bks"), 1)
            act.wait_ge(sem("zeroed"), layer * 7 + 7)
            for u in range(B * QUADS):
                bias = bks[:, u % QUADS:u % QUADS + 1] if layer == 1 else 0.0
                U = layer * B * QUADS + u
                act.wait_ge(sem("kT_done"), U + 1)
                act.wait_ge(sem("k_split"), U + 1)
                act.activation(kf[:, u % 2, :], bank[u % 2][:, 0:KEYS], ACT.Identity, scale=scale, bias=bias)\
                    .then_inc(sem("kT_free"), 1)
                act.wait_ge(sem("kT_free"), U + 3)
                for rows, part, cols in diagonal(u):
                    hi = act.activation(kh[rows, u // QUADS, u % QUADS, cols], kf[rows, u % 2, part], ACT.Copy)
                hi.then_inc(sem("k_hi"), 1)
            act.sem_inc(sem("kv_over"), 1)

        def dve_kv(dve, layer):
            if layer == 1:
                dve.wait_ge(sem("bias_in"), 64)
            dve.wait_ge(sem("zeroed"), layer * 7 + 7)
            flat_b = one_b[:].rearrange("p q n -> p (q n)")
            for j in range(4):
                rows = slice(KB * j, KB * j + KB)
                dve.memset(flat_b[rows, KB * j:KB * j + 3 * (P + 1) + 1:P + 1], 1.0).then_inc(sem("one_b"), 1)
                dve.memset(one_b[rows, 0, KB * j + QUADS:KB * j + KB], 1.0).then_inc(sem("one_b"), 1)
            dve.wait_ge(sem("one_b"), layer * 12 + 8)
            for j in range(4):
                dve.memset(one_b[KB * j:KB * j + DUP, :, :], 0.0).then_inc(sem("one_b"), 1)
            for u in range(B * QUADS):
                U = layer * B * QUADS + u
                dve.wait_ge(sem("k_hi"), U + 1)
                for rows, part, cols in diagonal(u):
                    lo = dve.tensor_tensor(kl[rows, u // QUADS, u % QUADS, cols], kf[rows, u % 2, part],
                                           kh[rows, u // QUADS, u % QUADS, cols], ALU.subtract)
                lo.then_inc(sem("k_split"), 1)
            for b in range(B):
                dve.wait_ge(sem("v_done"), layer * 4 + 2 * b + 1)
                if layer == 0:
                    dve.tensor_copy(va[:, b, :], bank[4][:]).then_inc(sem("v_free"), 1)
                else:
                    dve.tensor_tensor(va[:, b, :], bank[4][:], bv[:], ALU.add).then_inc(sem("v_free"), 1)
                dve.wait_ge(sem("v_done"), layer * 4 + 2 * b + 2)
                for j in range(4):
                    rows = slice(KB * j, KB * j + KB)
                    dst = vb[rows, b, :, KB * j:KB * j + KB]
                    src = bank[5][rows, :].rearrange("p (q n) -> p q n", q=QUADS)[:, :, KB * j:KB * j + KB]
                    if layer == 0:
                        cp = dve.tensor_copy(dst, src)
                    else:
                        cp = dve.tensor_tensor(dst, src, bv[rows, :].rearrange("p (q n) -> p q n", q=QUADS)
                                               [:, :, KB * j:KB * j + KB], ALU.add)
                cp.then_inc(sem("v_free"), 1)
            dve.wait_ge(sem("v_free"), 2 + 4 * (layer + 1))
            for j in range(4):
                ms = dve.memset(vb[KB * j:KB * j + DUP, :, :, :], 0.0)
            ms.then_inc(sem("vb_ready"), 1)
            dve.sem_inc(sem("kv_over"), 1)

        def enter_groups(eng, layer):
            eng.wait_ge(sem("kv_over"), 4 * (layer + 1))

        def pe_att_start(pe, layer):
            enter_groups(pe, layer)
            pe.wait_ge(sem("k_split"), (layer + 1) * B * QUADS + 2)
            pe.wait_ge(sem("vb_ready"), layer + 1)
            pe.wait_ge(sem("selected"), (layer + 1) * 7)
            pe.wait_ge(sem("one_b"), (layer + 1) * 12)
            if layer == 0:
                pe.sem_inc(sem("pv_done"), 2)

        def qm(u):
            return bank[(2, 3, 0, 1)[u % 4]]

        def pe_att(pe, layer):
            def turn(g):
                G = layer * GROUPS + g
                for t in range(GT):
                    pe.wait_ge(sem("a_xn"), at(ATT, "a_xn", G, t + 1))
                    pe.wait_ge(sem("a_te"), at(ATT, "a_te", G, t + 1))
                    if t < 2:
                        pe.wait_ge(sem("o_free"), at(ATT, "o_free", G, t + 1))
                    for c in range(C):
                        mm = pe.transpose(bank[t % 2][:, P * c:P * c + P], xn[:, t, c::C], ident[:])
                    mm.then_inc(sem("a_tp"), 1)

            def queries(g, q):
                G = layer * GROUPS + g
                if q == 0:
                    pe.wait_ge(sem("a_te"), at(ATT, "a_te", G, GT + 2))
                u = 6 * q
                pe.wait_ge(sem("qm_free"), at(ATT, "qm_free", G, u + 1))
                for c in range(C):
                    mm = pe.matmul(qm(u)[:], wq[:, c, P * q:P * q + P], xnT[:, c, :], start=(c == 0),
                                   stop=(c == C - 1))
                mm.then_inc(sem("qm_done"), 1)

            def shifts(g, b, q):
                G = layer * GROUPS + g
                pe.wait_ge(sem("a_qh"), at(ATT, "a_qh", G, q + 1))
                for t in range(GT + 1):
                    u = 6 * q + 1 + t
                    pe.wait_ge(sem("qm_free"), at(ATT, "qm_free", G, u + 1))
                    o = qm(u)
                    if t < GT:
                        mm = pe.matmul(o[:], qh[:, q, P * t:P * t + P], kh[:, b, q, 0:4 * KA], start=True, stop=True)
                    else:
                        for i in range(GT):
                            mm = pe.matmul(o[:, P * i:P * i + P], qh[:, q, P * i:P * i + P], kh[:, b, q, 4 * KA:QK],
                                           start=(i == 0), stop=(i == GT - 1), skip_group_check=True)
                    mm.then_inc(sem("qm_done"), 1)

            def turn_max(g):
                G = layer * GROUPS + g
                pe.wait_ge(sem("a_mx"), at(ATT, "a_mx", G, 1))
                pe.wait_ge(sem("a_at"), at(ATT, "a_at", G, 1))
                for t in range(GT):
                    mm = pe.transpose(bank[7][0:H, P * t:P * t + P], mx[:, t, :], ident[:])
                mm.then_inc(sem("a_mt"), 1)

            def scores(g, b, q):
                G = layer * GROUPS + g
                pe.wait_ge(sem("qm_free"), at(ATT, "qm_free", G, 6 * q + 5))
                if q == 0:
                    pe.wait_ge(sem("a_ml"), at(ATT, "a_ml", G, 1))
                for j in range(5):
                    u = 5 * q + j
                    o = bank[4 + u % 2]
                    if layer == 0:
                        pe.wait_ge(sem("a_sm"), at(ATT, "a_sm", G, u + 1))
                    else:
                        pe.wait_ge(sem("p_done"), at(ATT, "p_done", G, u - 1))
                    cols = slice(KA * j, KA * j + KA)
                    pe.matmul(o[:], kh[:, b, q, cols], qh[:, q, :], start=True, stop=False)
                    pe.matmul(o[:], kh[:, b, q, cols], ql[:, q, :], start=False, stop=False)
                    pe.matmul(o[:], kl[:, b, q, cols], qh[:, q, :], start=False, stop=False)
                    if j < 4:
                        pick = sel[:, 4 * q + j:4 * q + j + 1].broadcast_to([P, P])
                    else:
                        pick = sel_b[:, q, :, :].rearrange("p h k -> p (h k)")
                    pe.matmul(o[:], pick, neg_max[:], start=False, stop=True).then_inc(sem("sc_done"), 1)

            def values(g, b, q):
                G = layer * GROUPS + g
                pe.wait_ge(sem("a_raw"), at(ATT, "a_raw", G, q + 1))
                if q == 0:
                    pe.wait_ge(sem("a_at"), at(ATT, "a_at", G, 1))
                pe.wait_ge(sem("p_done"), at(ATT, "p_done", G, 5 * q + 5))
                slot = 5 * (q % 2)
                for j in range(4):
                    pe.matmul(bank[6][DH * j:DH * j + DH, :], va[:, b, P * q + DH * j:P * q + DH * j + DH],
                              pr[:, slot + j, :], start=True, stop=False, skip_group_check=True)
                for j in range(4):
                    pe.matmul(bank[7][DH * j:DH * j + DH, :], one_a[:, q, :], pr[:, slot + j, :],
                              start=(q == 0), stop=False, skip_group_check=True)
                pe.matmul(bank[6][:], vb[:, b, q, :], pr[:, slot + 4, :], start=False, stop=True, skip_group_check=True)
                pe.matmul(bank[7][:], one_b[:, q, :], pr[:, slot + 4, :], start=False, stop=(q == QUADS - 1),
                          skip_group_check=True).then_inc(sem("pv_done"), 1)

            def spread_sums(g):
                G = layer * GROUPS + g
                pe.wait_ge(sem("a_rl"), at(ATT, "a_rl", G, 1))
                pe.wait_ge(sem("a_raw"), at(ATT, "a_raw", G, QUADS + 1))
                for q in range(QUADS):
                    o = bank[6 + q % 2]
                    if q >= 2:
                        pe.wait_ge(sem("a_at"), at(ATT, "a_at", G, q))
                    w = spread[:, q, :, :].rearrange("p h n -> p (h n)")
                    pe.matmul(o[:], w, rch[:], start=True, stop=False)
                    pe.matmul(o[:], w, rcl[:], start=False, stop=True).then_inc(sem("spread"), 1)

            def project(g, n):
                G = layer * GROUPS + g
                for t in range(GT):
                    if t == 1 and n is not None:
                        turn_max(n)
                    pe.wait_ge(sem("o_free"), at(ATT, "o_free", G, t + 5))
                    for q in range(QUADS):
                        if t == 0:
                            pe.wait_ge(sem("a_at"), at(ATT, "a_at", G, q + 2))
                        mm = pe.matmul(bank[t % 2][:], attnT[:, q, P * t:P * t + P], wo[:, q, :], start=(q == 0),
                                       stop=(q == QUADS - 1))
                    mm.then_inc(sem("o_done"), 1)

            def ahead(g, b):
                turn(g)
                for q in range(QUADS):
                    queries(g, q)
                    shifts(g, b, q)
                turn_max(g)

            def body(g, b, n, bn_):
                scores(g, b, 0)
                scores(g, b, 1)
                values(g, b, 0)
                if n is not None:
                    turn(n)
                for q in range(2):
                    if n is not None:
                        queries(n, q)
                    scores(g, b, q + 2)
                    if n is not None:
                        shifts(n, bn_, q)
                    values(g, b, q + 1)
                if n is not None:
                    queries(n, 2)
                values(g, b, 3)
                if n is not None:
                    shifts(n, bn_, 2)
                    queries(n, 3)
                    shifts(n, bn_, 3)
                spread_sums(g)
                project(g, n)
            pipelined(pe, layer, ahead, body)

        def act_att(act, layer):
            def feature_major(g):
                G = layer * GROUPS + g
                for t in range(GT):
                    act.wait_ge(sem("a_tp"), at(ATT, "a_tp", G, t + 1))
                    act.activation(xnT[:, :, P * t:P * t + P], bank[t % 2][:].rearrange("p (c n) -> p c n", c=C),
                                   ACT.Copy).then_inc(sem("a_te"), 1)

            def high_queries(g, q):
                G = layer * GROUPS + g
                act.wait_ge(sem("qm_done"), at(ATT, "qm_done", G, 6 * q + 1))
                bias = bq[:, q:q + 1] if layer == 1 else zero[:, q:q + 1]
                act.activation(qh[:, q, :], qm(6 * q)[:], ACT.Identity, bias=bias).then_inc(sem("a_qh"), 1)

            def high_shift(g):
                G = layer * GROUPS + g
                act.wait_ge(sem("a_mt"), at(ATT, "a_mt", G, 1))
                act.activation(neg_max[0:H, :], bank[7][0:H, :], ACT.Copy, scale=-1.0).then_inc(sem("a_mh"), 1)

            def exps(g, q):
                G = layer * GROUPS + g
                for j in range(5):
                    u = 5 * q + j
                    slot = u % 10
                    if layer == 0:
                        act.wait_ge(sem("a_sm"), at(ATT, "a_sm", G, u + 3))
                        act.activation(pr[:, slot, :], pr[:, slot, :], ACT.Exp).then_inc(sem("p_done"), 1)
                    else:
                        act.wait_ge(sem("sc_done"), at(ATT, "sc_done", G, u + 1))
                        act.wait_ge(sem("pv_done"), at(ATT, "pv_done", G, q + 1))
                        act.activation(pr[:, slot, :], bank[4 + u % 2][:], ACT.Exp).then_inc(sem("p_done"), 1)

            def take_values(g, q):
                G = layer * GROUPS + g
                act.wait_ge(sem("pv_done"), at(ATT, "pv_done", G, q + 3))
                act.activation(attnT[:, q, :], bank[6][:], ACT.Copy).then_inc(sem("a_raw"), 1)

            def ahead(g, b):
                feature_major(g)
                for q in range(QUADS):
                    high_queries(g, q)
                high_shift(g)

            def body(g, b, n, bn_):
                G = layer * GROUPS + g
                exps(g, 0)
                exps(g, 1)
                if n is not None:
                    feature_major(n)
                take_values(g, 0)
                for q in range(2):
                    if n is not None:
                        high_queries(n, q)
                    exps(g, q + 2)
                    take_values(g, q + 1)
                if n is not None:
                    high_queries(n, 2)
                take_values(g, 3)
                act.wait_ge(sem("a_rc"), at(ATT, "a_rc", G, 1))
                act.activation(rch[:], rc[:], ACT.Copy).then_inc(sem("a_rh"), 1)
                if n is not None:
                    high_queries(n, 3)
                    high_shift(n)
            pipelined(act, layer, ahead, body)

        def dve_att(dve, layer):
            def stats(g):
                if layer == 0:
                    dve.wait_ge(sem("x_in"), 16 * g + 16)
                G = layer * GROUPS + g
                for t in range(GT):
                    dve.bn_stats(bn[:, t, :], tile_of(xr, g, t)).then_inc(sem("a_bn"), 1)
                for t in range(GT):
                    hold(dve, "a_bn", at(ATT, "a_bn", G, t + 1))
                    dve.bn_aggr(mv[:, t, :], bn[:, t, :]).then_inc(sem("a_mv"), 1)

            def normalise(g):
                G = layer * GROUPS + g
                hold(dve, "a_rs", at(ATT, "a_rs", G, 1))
                for t in range(GT):
                    dve.tensor_scalar(xn[:, t, :], tile_of(xr, g, t), mv[:, t, 0:1], rs[:, t:t + 1],
                                      ALU.subtract, ALU.mult).then_inc(sem("a_xn"), 1)

            def low_queries(g, q):
                G = layer * GROUPS + g
                dve.wait_ge(sem("a_qh"), at(ATT, "a_qh", G, q + 1))
                bias = bq[:, q:q + 1] if layer == 1 else zero[:, q:q + 1]
                dve.scalar_tensor_tensor(ql[:, q, :], qm(6 * q)[:], bias, qh[:, q, :], ALU.add, ALU.subtract)\
                    .then_inc(sem("qm_free"), 1)

            def maxima(g, q):
                G = layer * GROUPS + g
                if layer == 0 and q == 0:
                    dve.wait_ge(sem("mask_t_in"), g * 16 + 16)
                for t in range(GT + 1):
                    u = 6 * q + 1 + t
                    dve.wait_ge(sem("qm_done"), at(ATT, "qm_done", G, u + 1))
                    if t < GT:
                        dims, args = "p (h k) -> p h k", dict(h=4)
                        dst = mx[:, t, 4 * q:4 * q + 4]
                        mk = mk_t[:, t, 0:KA].unsqueeze(1).broadcast_to([P, 4, KA])
                    else:
                        dims, args = "p (t h k) -> p t h k", dict(t=GT, h=4)
                        dst = mxb[:, :, 4 * q:4 * q + 4]
                        mk = mk_t[:, :, KB0:KEYS].unsqueeze(2).broadcast_to([P, GT, 4, KB])
                    src = qm(u)[:].rearrange(dims, **args)
                    if layer == 0:
                        r = 5 * q + t
                        tmp = mtmp[:, r % 2, :].rearrange(dims, **args)
                        dve.wait_ge(sem("a_red"), at(ATT, "a_red", G, r + 1))
                        dve.tensor_tensor(tmp, src, mk, ALU.add).then_inc(sem("qm_free"), 1)
                        dve.wait_ge(sem("qm_free"), at(ATT, "qm_free", G, u + 5))
                        dve.tensor_reduce(dst, tmp, AX.X, ALU.max).then_inc(sem("a_red"), 1)
                    else:
                        dve.tensor_reduce(dst, src, AX.X, ALU.max).then_inc(sem("qm_free"), 1)

            def join_maxima(g):
                G = layer * GROUPS + g
                if layer == 0:
                    dve.wait_ge(sem("a_red"), at(ATT, "a_red", G, 22))
                    dve.sem_inc(sem("mask_t_free"), 1)
                else:
                    dve.wait_ge(sem("qm_free"), at(ATT, "qm_free", G, 28))
                dve.tensor_tensor(mx[:], mx[:], mxb[:], ALU.max).then_inc(sem("a_mx"), 1)

            def low_shift(g):
                G = layer * GROUPS + g
                dve.wait_ge(sem("a_mh"), at(ATT, "a_mh", G, 1))
                dve.scalar_tensor_tensor(neg_max[32:32 + H, :], bank[7][0:H, :], -1.0, neg_max[0:H, :],
                                         ALU.mult, ALU.subtract).then_inc(sem("a_ml"), 1)

            def add_mask(g, q):
                if layer == 1:
                    return
                if q == 0:
                    dve.wait_ge(sem("mask_in"), g * 80 + 80)
                G = g
                dve.wait_ge(sem("pv_done"), at(ATT, "pv_done", G, q + 1))
                for j in range(5):
                    u = 5 * q + j
                    dve.wait_ge(sem("sc_done"), at(ATT, "sc_done", G, u + 1))
                    dve.tensor_tensor(pr[:, u % 10, :], bank[4 + u % 2][:], (mk_a if j < 4 else mk_b)[:], ALU.add)\
                        .then_inc(sem("a_sm"), 1)
                if q == QUADS - 1:
                    dve.wait_ge(sem("a_sm"), at(ATT, "a_sm", G, 22))
                    dve.sem_inc(sem("mask_free"), 1)

            def ahead(g, b):
                stats(g)
                normalise(g)
                for q in range(QUADS):
                    low_queries(g, q)
                    maxima(g, q)
                join_maxima(g)
                low_shift(g)

            def body(g, b, n, bn_):
                G = layer * GROUPS + g
                add_mask(g, 0)
                add_mask(g, 1)
                if n is not None:
                    stats(n)
                    normalise(n)
                for q in range(2):
                    if n is not None:
                        low_queries(n, q)
                    add_mask(g, q + 2)
                    if n is not None:
                        maxima(n, q)
                if n is not None:
                    low_queries(n, 2)
                dve.wait_ge(sem("pv_done"), at(ATT, "pv_done", G, QUADS + 2))
                dve.reciprocal(rc[:], bank[7][:]).then_inc(sem("a_rc"), 1)
                if n is not None:
                    maxima(n, 2)
                dve.wait_ge(sem("a_rh"), at(ATT, "a_rh", G, 1))
                dve.tensor_tensor(rcl[:], rc[:], rch[:], ALU.subtract).then_inc(sem("a_rl"), 1)
                if n is not None:
                    low_queries(n, 3)
                    maxima(n, 3)
                    join_maxima(n)
                for q in range(QUADS):
                    dve.wait_ge(sem("spread"), at(ATT, "spread", G, q + 1))
                    dve.tensor_tensor(attnT[:, q, :], attnT[:, q, :], bank[6 + q % 2][:], ALU.mult)\
                        .then_inc(sem("a_at"), 1)
                if layer == 1:
                    dve.wait_ge(sem("a_xb"), g + 1)
                for t in range(GT):
                    dve.wait_ge(sem("o_done"), at(ATT, "o_done", G, t + 1))
                    dve.tensor_tensor(tile_of(xr, g, t), bank[t % 2][:], tile_of(xr, g, t), ALU.add)\
                        .then_inc(sem("o_free"), 1)
                    if t == 0 and n is not None:
                        low_shift(n)
                    if t >= 1:
                        hold(dve, "o_free", at(ATT, "o_free", G, t + 6))
                        dve.bn_stats(bn_o[:, t - 1, :], tile_of(xr, g, t - 1)).then_inc(sem("o_bn"), 1)
                hold(dve, "o_free", at(ATT, "o_free", G, GT + 6))
                dve.bn_stats(bn_o[:, GT - 1, :], tile_of(xr, g, GT - 1)).then_inc(sem("o_bn"), 1)
                for t in range(GT):
                    hold(dve, "o_bn", at(ATT, "o_bn", G, t + 1))
                    dve.bn_aggr(mv_o[:, t, :], bn_o[:, t, :]).then_inc(sem("o_mv"), 1)
                hold(dve, "o_mv", at(ATT, "o_mv", G, GT))
                dve.tensor_copy(mv_all[:, bass.ds(g * GT, GT), :], mv_o[:]).then_inc(sem("kept"), 1)
            pipelined(dve, layer, ahead, body)

        def pool_stats_group(pool, g):
            hold(pool, "t_mv", at(STAT, "t_mv", g, GT))
            pool.tensor_tensor(ve[:], mv[:, :, 1], eps_c[:, 0:GT], ALU.add).then_inc(sem("t_ve"), 1)
            pool.wait_ge(sem("t_ve"), at(STAT, "t_ve", g, 1))
            pool.tensor_tensor(rs[:], ve[:], expo[:, 0:GT], ALU.pow).then_inc(sem("t_rs"), 1)

        def dve_stats_group(dve, g):
            for t in range(GT):
                dve.bn_stats(bn[:, t, :], tile_of(xr, g, t)).then_inc(sem("t_bn"), 1)
            for t in range(GT):
                hold(dve, "t_bn", at(STAT, "t_bn", g, t + 1))
                dve.bn_aggr(mv[:, t, :], bn[:, t, :]).then_inc(sem("t_mv"), 1)
            hold(dve, "t_rs", at(STAT, "t_rs", g, 1))
            dve.tensor_copy(mv2[:, bass.ds(g * GT, GT), :], mv[:]).then_inc(sem("t_keep"), 1)
            dve.tensor_copy(rs2[:, bass.ds(g * GT, GT)], rs[:]).then_inc(sem("t_keep"), 1)
            for t in range(GT):
                hold(dve, "t_tp", at(STAT, "t_tp", g, t + 1))
                dve.tensor_scalar(fxn[:, t, :], tile_of(xr, g, t), mv[:, t, 0:1], rs[:, t:t + 1],
                                  ALU.subtract, ALU.mult).then_inc(sem("t_xn"), 1)
            dve.wait_ge(sem("t_te"), at(STAT, "t_te", g, GT + 2))
            for c in range(C):
                for n in range(2):
                    xg = xc[n][:, bass.ds(g * GW, GW)]
                    if c == 0:
                        dve.tensor_scalar(xg, fxT[:, c, :], cw[:, n, c:c + 1], cb[:, n:n + 1], ALU.mult, ALU.add)\
                            .then_inc(sem("t_xc"), 1)
                    else:
                        hold(dve, "t_xc", at(STAT, "t_xc", g, 2 * c + n - 1))
                        dve.scalar_tensor_tensor(xg, fxT[:, c, :], cw[:, n, c:c + 1], xg, ALU.mult, ALU.add)\
                            .then_inc(sem("t_xc"), 1)
            for n in range(2):
                hold(dve, "t_xc", at(STAT, "t_xc", g, 7 + n))
                dve.tensor_copy(ge[:, n, :], xc[n][:, bass.ds(g * GW, GW)]).then_inc(sem("t_cp"), 1)
            for n in range(2):
                hold(dve, "t_cp", g * 2 + n + 1)
                dve.bn_stats(gst[:, n, bass.ds(g, 1), :].rearrange("p a s -> p (a s)"), ge[:, n, :])\
                    .then_inc(sem("t_gs"), 1)

        def pe_stats_group(pe, g):
            for t in range(GT):
                pe.wait_ge(sem("t_xn"), at(STAT, "t_xn", g, t + 1))
                pe.wait_ge(sem("t_te"), at(STAT, "t_te", g, t + 1))
                for c in range(C):
                    mm = pe.transpose(bank[t % 2][:, P * c:P * c + P], fxn[:, t, c::C], ident[:])
                mm.then_inc(sem("t_tp"), 1)

        def act_stats_group(act, g):
            for t in range(GT):
                act.wait_ge(sem("t_tp"), at(STAT, "t_tp", g, t + 5))
                if t == 0:
                    act.wait_ge(sem("t_gs"), at(STAT, "t_gs", g, 2))
                act.activation(fxT[:, :, P * t:P * t + P], bank[t % 2][:].rearrange("p (c n) -> p c n", c=C), ACT.Copy)\
                    .then_inc(sem("t_te"), 1)

        def dve_batch_norm(dve):
            dve.wait_ge(sem("t_gs"), 2 + 2 * GROUPS)
            for n in range(2):
                dve.bn_aggr(gmv[:, n, :], gst[:, n, :, :].rearrange("p g s -> p (g s)")).then_inc(sem("b_mv"), 1)
            dve.wait_ge(sem("b_rs"), 1)
            dve.tensor_tensor(gsc[:], grs[:], gam[:], ALU.mult).then_inc(sem("b_sc"), 1)
            dve.wait_ge(sem("b_sc"), 1)
            dve.tensor_tensor(gtm[:], gmv[:, :, 0], gsc[:], ALU.mult).then_inc(sem("b_sc"), 1)
            dve.wait_ge(sem("b_sc"), 2)
            dve.tensor_tensor(gbi[:], bet[:], gtm[:], ALU.subtract).then_inc(sem("b_sc"), 1)

        def pool_batch_norm(pool):
            pool.wait_ge(sem("b_mv"), 2)
            pool.tensor_tensor(gve[:], gmv[:, :, 1], eps_c[:, 0:2], ALU.add).then_inc(sem("b_ve"), 1)
            pool.wait_ge(sem("b_ve"), 1)
            pool.tensor_tensor(grs[:], gve[:], expo[:, 0:2], ALU.pow).then_inc(sem("b_rs"), 1)

        def pool_ffn_group(pool, g):
            hold(pool, "f_xn", at(FFN, "f_xn", g, GT))
            xg = xr[:, bass.ds(g * GT, GT), :]
            pool.tensor_tensor(xg, xg, bf[:].unsqueeze(1).broadcast_to([P, GT, D]), ALU.add).then_inc(sem("f_xb"), 1)
            pool.wait_ge(sem("f_xb"), at(FFN, "f_xb", g, 1))
            for t in range(GT):
                hold(pool, "f_sum", at(FFN, "f_sum", g, t + 3))
                pool.tensor_tensor(tile_of(xr, g, t), tile_of(xr, g, t), fsm[:, t % 2, :], ALU.add)\
                    .then_inc(sem("f_x"), 1)

        def pe_ffn_group(pe, g):
            def logits(t):
                for n in (1, 0):
                    u = 2 * t + 1 - n
                    pe.wait_ge(sem("lg_free"), at(FFN, "lg_free", g, u + 1))
                    if t == 0:
                        pe.wait_ge(sem("f_ge"), at(FFN, "f_ge", g, 2 - n))
                    pe.matmul(bank[2 + u % 2][:], ge[:, n, P * t:P * t + P], lw[:, n, :], start=True, stop=True)\
                        .then_inc(sem("lg_done"), 1)

            def full(t):
                pe.wait_ge(sem("full_free"), at(FFN, "full_free", g, t + 1))
                for c in range(C):
                    mm = pe.matmul(bank[4 + t % 2][:], fxT[:, c, P * t:P * t + P], wf[:, c, :], start=(c == 0),
                                   stop=(c == C - 1))
                mm.then_inc(sem("full_done"), 1)

            def sparse(t):
                pe.wait_ge(sem("f_xs"), at(FFN, "f_xs", g, t + 1 + GT))
                pe.wait_ge(sem("f_te"), at(FFN, "f_te", g, GT + t + 1))
                for c in range(C):
                    mm = pe.transpose(bank[t % 2][:, P * c:P * c + P], fxs[:, c::C], ident[:])
                mm.then_inc(sem("f_tp"), 1)
                pe.wait_ge(sem("f_te"), at(FFN, "f_te", g, GT + t + 3))
                pe.wait_ge(sem("f_sum"), at(FFN, "f_sum", g, t + 1))
                for c in range(C):
                    mm = pe.matmul(bank[6 + t % 2][:], fxsT[:, P * c:P * c + P], wf[:, c, :], start=(c == 0),
                                   stop=(c == C - 1))
                mm.then_inc(sem("in_done"), 1)

            logits(0)
            for t in range(GT):
                pe.wait_ge(sem("f_xn"), at(FFN, "f_xn", g, t + 1))
                pe.wait_ge(sem("f_te"), at(FFN, "f_te", g, t + 1))
                for c in range(C):
                    mm = pe.transpose(bank[t % 2][:, P * c:P * c + P], fxn[:, t, c::C], ident[:])
                mm.then_inc(sem("f_tp"), 1)
            pe.wait_ge(sem("f_te"), at(FFN, "f_te", g, GT + 2))
            for t in range(GT):
                full(t)
                if t + 1 < GT:
                    logits(t + 1)
                sparse(t)

        def act_ffn_group(act, g):
            for n in (1, 0):
                act.activation(ge[:, n, :], xc[n][:, bass.ds(g * GW, GW)], ACT.Gelu, bias=gbi[:, n:n + 1],
                               scale=gsc[:, n:n + 1]).then_inc(sem("f_ge"), 1)
            for t in range(GT):
                act.wait_ge(sem("f_tp"), at(FFN, "f_tp", g, t + 1))
                act.activation(fxT[:, :, P * t:P * t + P], bank[t % 2][:].rearrange("p (c n) -> p c n", c=C), ACT.Copy)\
                    .then_inc(sem("f_te"), 1)
            for t in range(GT):
                for n in (1, 0):
                    u = 2 * t + 1 - n
                    act.wait_ge(sem("f_nm"), at(FFN, "f_nm", g, u + 1))
                    act.activation(ex[:, n, :], Lg[:, n, :], ACT.Exp, bias=fnm[:, n:n + 1],
                                   accum_out=fsum[:, n:n + 1]).then_inc(sem("f_ex"), 1)
                act.wait_ge(sem("f_tp"), at(FFN, "f_tp", g, GT + t + 1))
                act.activation(fxsT[:], bank[t % 2][:], ACT.Copy).then_inc(sem("f_te"), 1)

        def dve_ffn_group(dve, g):
            for t in range(GT):
                hold(dve, "f_xs", at(FFN, "f_xs", g, t + 1))
                dve.tensor_scalar(fxn[:, t, :], tile_of(xr, g, t), mv2[:, bass.ds(g * GT + t, 1), 0],
                                  rs2[:, bass.ds(g * GT + t, 1)], ALU.subtract, ALU.mult).then_inc(sem("f_xn"), 1)
            chain = [0]

            def top(ins):
                chain[0] += 1
                ins.then_inc(sem("f_top"), 1)
                hold(dve, "f_top", at(FFN, "f_top", g, chain[0]))

            def combine(t):
                dve.wait_ge(sem("full_free"), at(FFN, "full_free", g, t + 3))
                dve.wait_ge(sem("in_done"), at(FFN, "in_done", g, t + 1))
                dve.wait_ge(sem("f_x"), at(FFN, "f_x", g, t + 1))
                dve.tensor_tensor(fsm[:, t % 2, :], bank[6 + t % 2][:], ftmp[:, t % 2, :], ALU.add)\
                    .then_inc(sem("f_sum"), 1)

            for t in range(GT):
                for n in (1, 0):
                    u = 2 * t + 1 - n
                    dve.wait_ge(sem("lg_done"), at(FFN, "lg_done", g, u + 1))
                    dve.tensor_tensor(Lg[:, n, :], bank[2 + u % 2][:], lb[:, n, :], ALU.add).then_inc(sem("lg_free"), 1)
                    hold(dve, "lg_free", at(FFN, "lg_free", g, u + 3))
                    src = Lg[:, n, :]
                    for k in range(K_TOP // 8):
                        top(dve.max(m8[:, n, :], src))
                        if k == 0:
                            dve.tensor_scalar(fnm[:, n:n + 1], m8[:, n, 0:1], -1.0, None, ALU.mult)\
                                .then_inc(sem("f_nm"), 1)
                        top(dve.match_replace(Wk[:, k % 2, 0, :], m8[:, n, :], src, GONE))
                        src = Wk[:, k % 2, 0, :]
                    dve.wait_ge(sem("f_ex"), at(FFN, "f_ex", g, u + 1))
                    dve.reciprocal(frc[:, n:n + 1], fsum[:, n:n + 1]).then_inc(sem("f_rc"), 1)
                    dve.scalar_tensor_tensor(selv[:, n, :], src, 0.9 * GONE, ex[:, n, :], ALU.is_le, ALU.mult)\
                        .then_inc(sem("f_sel"), 1)
                    dve.wait_ge(sem("f_rc"), at(FFN, "f_rc", g, u + 1))
                    dve.wait_ge(sem("f_sel"), at(FFN, "f_sel", g, u + 1))
                    if n == 1:
                        dve.wait_ge(sem("f_tp"), at(FFN, "f_tp", g, GT + t))
                        dve.scalar_tensor_tensor(fxs[:], selv[:, n, :], frc[:, n:n + 1], fxn[:, t, :],
                                                 ALU.mult, ALU.mult).then_inc(sem("f_xs"), 1)
                    else:
                        dve.wait_ge(sem("full_done"), at(FFN, "full_done", g, t + 1))
                        dve.scalar_tensor_tensor(ftmp[:, t % 2, :], bank[4 + t % 2][:], frc[:, n:n + 1],
                                                 selv[:, n, :], ALU.mult, ALU.mult).then_inc(sem("full_free"), 1)
                if t >= 1:
                    combine(t - 1)
            combine(GT - 1)

        def sp_experts(sp):
            sp.wait_ge(sem("att1_over"), 5)
            sp.dma_start(gw[:], gate_w.rearrange("(p c) e -> p c e", c=C)).then_inc(sem("gate_in"), 16)
            for e in range(E):
                sp.dma_start(w_in_sb[:, e * C * D:(e + 1) * C * D],
                             w_in[e].rearrange("(p c) n -> p (c n)", c=C)).then_inc(sem("w_in"), 16)
                sp.dma_start(w_dn_sb[:, e * 2 * D:(e + 1) * 2 * D].rearrange("p (i n) -> p i n", i=2),
                             w_down[e].rearrange("(i p) n -> p i n", p=P)).then_inc(sem("w_in"), 16)
            for r in range(4):
                sp.wait_ge(sem(f"scattered{r}"), 16 * TILES // 4)

            def load(k, j):
                sp.dma_start(tx[:, j, :], xs_dram[bass.ds(k * P, P), :]).then_inc(sem(f"tx_in{j}"), 16)

            def store(k, j):
                sp.wait_ge(sem("e_yo"), k + 3)
                sp.dma_start(ys_dram[bass.ds(k * P, P), :], yo[:, j, :]).then_inc(sem(f"ys_out{j}"), 16)

            for k in range(4):
                if k >= 2:
                    sp.wait_ge(sem("tx_used"), k - 1)
                load(k, k % 2)
            store(0, 0)
            with sp.Fori(2, SLOT_TILES // 2) as i:
                for j in range(2):
                    sp.wait_ge(sem("tx_used"), 2 * i + j - 1)
                    load(2 * i + j, j)
                    store(2 * i + j - 3, 1 - j)
            sp.wait_ge(sem("tx_used"), SLOT_TILES - 2)
            load(SLOT_TILES - 1, 0)
            for k in range(SLOT_TILES - 4, SLOT_TILES):
                store(k, k % 2)
            for t in range(TILES):
                sp.wait_ge(sem("final"), t + 1)
                sp.dma_start(out_tiles[:, t, :], xr[:, t, :]).then_inc(sem("out_done"), 16)
            sp.wait_ge(sem("out_done"), 16 * TILES)

        def pool_gate_group(pool, g):
            hold(pool, "g_mv", at(GATE, "g_mv", g, GT))
            pool.tensor_tensor(ve[:], mv[:, :, 1], eps_c[:, 0:GT], ALU.add).then_inc(sem("g_ve"), 1)
            pool.wait_ge(sem("g_ve"), at(GATE, "g_ve", g, 1))
            pool.tensor_tensor(rs[:], ve[:], expo[:, 0:GT], ALU.pow).then_inc(sem("g_rs"), 1)

        def dve_gate_group(dve, g):
            for t in range(GT):
                dve.bn_stats(bn[:, t, :], tile_of(xr, g, t)).then_inc(sem("g_bn"), 1)
            for t in range(GT):
                hold(dve, "g_bn", at(GATE, "g_bn", g, t + 1))
                dve.bn_aggr(mv[:, t, :], bn[:, t, :]).then_inc(sem("g_mv"), 1)
            hold(dve, "g_rs", at(GATE, "g_rs", g, 1))
            dve.tensor_copy(mv3[:, bass.ds(g * GT, GT), :], mv[:]).then_inc(sem("g_keep"), 1)
            dve.tensor_copy(rs3[:, bass.ds(g * GT, GT)], rs[:]).then_inc(sem("g_keep"), 1)
            for t in range(GT):
                hold(dve, "g_tp", at(GATE, "g_tp", g, t + 1))
                dve.tensor_scalar(mxn[:, t % 2, :], tile_of(xr, g, t), mv[:, t, 0:1], rs[:, t:t + 1],
                                  ALU.subtract, ALU.mult).then_inc(sem("g_xn"), 1)
            for t in range(GT):
                hold(dve, "g_lg", at(GATE, "g_lg", g, t + 1))
                dve.tensor_copy(lgt[:, bass.ds(g * GT + t, 1), :].rearrange("p a e -> p (a e)"),
                                bank[2 + t % 2][:, 0:E]).then_inc(sem("g_cp"), 1)

        def pe_gate_group(pe, g):
            for t in range(GT):
                pe.wait_ge(sem("g_xn"), at(GATE, "g_xn", g, t + 1))
                pe.wait_ge(sem("g_te"), at(GATE, "g_te", g, t + 1))
                for c in range(C):
                    mm = pe.transpose(bank[t % 2][:, P * c:P * c + P], mxn[:, t % 2, c::C], ident[:])
                mm.then_inc(sem("g_tp"), 1)
                pe.wait_ge(sem("g_te"), at(GATE, "g_te", g, t + 3))
                pe.wait_ge(sem("g_cp"), at(GATE, "g_cp", g, t + 1))
                for c in range(C):
                    mm = pe.matmul(bank[2 + t % 2][:, 0:E], mxT[:, t % 2, P * c:P * c + P], gw[:, c, :],
                                   start=(c == 0), stop=(c == C - 1))
                mm.then_inc(sem("g_lg"), 1)

        def act_gate_group(act, g):
            for t in range(GT):
                act.wait_ge(sem("g_tp"), at(GATE, "g_tp", g, t + 3))
                act.activation(mxT[:, t % 2, :], bank[t % 2][:], ACT.Copy).then_inc(sem("g_te"), 1)

        def bc(ap, n):
            return ap.unsqueeze(2).broadcast_to([P, ap.shape[1], n])

        def over(ap, n):
            return ap.unsqueeze(1).broadcast_to([P, n, ap.shape[1]])

        def pool_sort(pool):
            pool.iota(iota_e[:], pattern=[[1, E]], base=0, channel_multiplier=0,
                      allow_small_or_imprecise_dtypes=True).then_inc(sem("s_const"), 1)
            pool.iota(slot_i[:], pattern=[[1, SLOT_TILES]], base=0, channel_multiplier=0,
                      allow_small_or_imprecise_dtypes=True).then_inc(sem("s_const"), 1)
            pool.memset(ones[:], 1.0).then_inc(sem("s_const"), 1)
            pool.wait_ge(sem("s_const"), 3)
            pool.affine_select(out=tri[:], in_=ones[:], compare_op=ALU.is_gt, fill=0.0, base=0,
                               pattern=[[1, P]], channel_multiplier=-1).then_inc(sem("s_const"), 1)

        def dve_sort(dve):
            n = [0]

            def then(ins):
                n[0] += 1
                ins.then_inc(sem("s_step"), 1)
                dve.wait_ge(sem("s_step"), n[0])

            dve.wait_ge(sem("g_cp"), 2 + 4 * GROUPS)
            dve.wait_ge(sem("s_const"), 4)
            dve.tensor_reduce(top_v[:], lgt[:], AX.X, ALU.max).then_inc(sem("s_top"), 1)
            dve.wait_ge(sem("s_top"), 1)
            then(dve.tensor_tensor(below[:], lgt[:], bc(top_v[:], E), ALU.not_equal))
            then(dve.scalar_tensor_tensor(cand[:], below[:], float(E), over(iota_e[:], TILES), ALU.mult, ALU.add))
            then(dve.tensor_reduce(selx[:], cand[:], AX.X, ALU.min))
            dve.tensor_tensor(onehot[:], over(iota_e[:], TILES), bc(selx[:], E), ALU.is_equal)\
                .then_inc(sem("s_onehot"), 1)
            dve.wait_ge(sem("s_counts"), 1)
            then(dve.tensor_copy(own[:], bank[1][:, 0:TILES * E].rearrange("p (t e) -> p t e", e=E)))
            then(dve.tensor_copy(cnt[:, 0, :, :], own[:]))
            src = 0
            shift = 1
            while shift < TILES:
                then(dve.tensor_copy(cnt[:, 1 - src, 0:shift, :], cnt[:, src, 0:shift, :]))
                then(dve.tensor_tensor(cnt[:, 1 - src, shift:, :], cnt[:, src, shift:, :],
                                       cnt[:, src, 0:TILES - shift, :], ALU.add))
                src = 1 - src
                shift *= 2
            then(dve.tensor_scalar(tot[:], cnt[:, src, TILES - 1, :], float(P - 1), None, ALU.add))
            then(dve.tensor_copy(toti[:], tot[:]))
            then(dve.tensor_scalar(toti[:], toti[:], P.bit_length() - 1, None, ALU.arith_shift_right))
            then(dve.tensor_copy(tiles_f[:], toti[:]))
            then(dve.memset(start[:], 0.0))
            for e in range(E):
                then(dve.tensor_tensor(start[:, e + 1:e + 2], start[:, e:e + 1], tiles_f[:, e:e + 1], ALU.add))
            then(dve.tensor_tensor(cmp[:], bc(slot_i[:], E - 1), over(start[:, 1:E], SLOT_TILES), ALU.is_ge))
            then(dve.tensor_reduce(slot_e[:], cmp[:], AX.X, ALU.add))
            dve.tensor_copy(slot_ei[:], slot_e[:]).then_inc(sem("slot_expert"), 1)
            then(dve.tensor_tensor(prod[:], cnt[:, src, :, :], own[:], ALU.subtract))
            then(dve.tensor_tensor(rank[:], bank[0][:, 0:TILES * E].rearrange("p (t e) -> p t e", e=E), prod[:],
                                   ALU.add))
            then(dve.scalar_tensor_tensor(prod[:], over(start[:, 0:E], TILES), float(P), rank[:], ALU.mult, ALU.add))
            then(dve.tensor_tensor(rank[:], prod[:], onehot[:], ALU.mult))
            then(dve.tensor_reduce(posf[:], rank[:], AX.X, ALU.add))
            dve.tensor_copy(posi[:], posf[:]).then_inc(sem("places"), 1)
            dve.wait_ge(sem("s_exp"), 1)
            then(dve.tensor_scalar(rwe[:], rwe[:], 1.0, None, ALU.add))
            then(dve.reciprocal(rw[:], rwe[:]))
            then(dve.tensor_tensor(srs[:], rs3[:], rw[:], ALU.mult))
            for t in range(TILES):
                if t >= 4:
                    dve.wait_ge(sem(f"scattered{t % 4}"), 16 * (t // 4))
                dve.tensor_scalar(xs[:, t % 4, :], xr[:, t, :], mv3[:, t, 0:1], srs[:, t:t + 1], ALU.subtract,
                                  ALU.mult).then_inc(sem("s_xs"), 1)

        def pe_sort(pe):
            pe.wait_ge(sem("s_onehot"), 1)
            flat = onehot[:].rearrange("p t e -> p (t e)")
            pe.matmul(bank[0][:, 0:TILES * E], tri[:], flat, start=True, stop=True)
            pe.matmul(bank[1][:, 0:TILES * E], ones[:], flat, start=True, stop=True).then_inc(sem("s_counts"), 1)

        def pool_scatter(pool):
            pool.wait_ge(sem("places"), 1)
            pool.wait_ge(sem("slots_zeroed"), 16)
            for t in range(TILES):
                pool.wait_ge(sem("s_xs"), t + 1)
                pool.indirect_dma_start(xs_dram, bass.IndirectOffsetOnAxis(posi[:, t:t + 1], 0), xs[:, t % 4, :], None)\
                    .then_inc(sem(f"scattered{t % 4}"), 16)

        def pairs(eng, step):
            step(0, 0, True)
            with eng.Fori(0, (SLOT_TILES - 1) // 2) as i:
                step(2 * i + 1, 1, False)
                step(2 * i + 2, 0, False)

        def pe_experts(pe):
            pe.wait_ge(sem("slot_expert"), 1)
            pe.wait_ge(sem("w_in"), 16 * 2 * E)

            def turn(k, j, n):
                pe.wait_ge(sem(f"tx_in{j}"), 16 * n + 16)
                pe.wait_ge(sem("e_te"), k + 1)
                for c in range(C):
                    mm = pe.transpose(bank[j][:, P * c:P * c + P], tx[:, j, c::C], ident[:])
                mm.then_inc(sem("tx_used"), 1)

            def into(k, j):
                e = pe.value_load(slot_ei[0:1, bass.ds(k, 1)], min_val=0, max_val=E - 1)
                pe.wait_ge(sem("e_te"), k + 3)
                pe.wait_ge(sem("e_hh"), k + 1)
                for c in range(C):
                    mm = pe.matmul(bank[2 + j][:], txT[:, j, P * c:P * c + P],
                                   w_in_sb[:, bass.ds(e * (C * D) + c * D, D)], start=(c == 0), stop=(c == C - 1))
                mm.then_inc(sem("e_gu"), 1)

            def turn_h(k, j):
                pe.wait_ge(sem("e_hh"), k + 3)
                pe.wait_ge(sem("e_hT"), k + 1)
                for i in range(2):
                    mm = pe.transpose(bank[4 + j][:, P * i:P * i + P], hh[:, j, P * i:P * i + P], ident[:])
                mm.then_inc(sem("e_th"), 1)

            def down(k, j):
                e = pe.value_load(slot_ei[0:1, bass.ds(k, 1)], min_val=0, max_val=E - 1)
                pe.wait_ge(sem("e_hT"), k + 3)
                pe.wait_ge(sem("e_yo"), k + 1)
                for i in range(2):
                    mm = pe.matmul(bank[6 + j][:], hT[:, j, P * i:P * i + P],
                                   w_dn_sb[:, bass.ds(e * (2 * D) + i * D, D)], start=(i == 0), stop=(i == 1))
                mm.then_inc(sem("e_dn"), 1)

            turn(0, 0, 0)
            into(0, 0)
            turn(1, 1, 0)
            with pe.Fori(0, (SLOT_TILES - 3) // 2) as i:
                into(2 * i + 1, 1)
                turn_h(2 * i, 0)
                turn(2 * i + 2, 0, i + 1)
                down(2 * i, 0)
                into(2 * i + 2, 0)
                turn_h(2 * i + 1, 1)
                turn(2 * i + 3, 1, i + 1)
                down(2 * i + 1, 1)
            last = SLOT_TILES - 1
            into(last - 1, 1)
            turn_h(last - 2, 0)
            turn(last, 0, last // 2)
            down(last - 2, 0)
            into(last, 0)
            turn_h(last - 1, 1)
            down(last - 1, 1)
            turn_h(last, 0)
            down(last, 0)

        def act_experts(act):
            def step(k, j, first):
                act.wait_ge(sem("tx_used"), k + 1)
                act.activation(txT[:, j, :], bank[j][:], ACT.Copy).then_inc(sem("e_te"), 1)
                if not first:
                    gated(k - 1, 1 - j)

            def gated(k, j):
                act.wait_ge(sem("e_gu"), k + 1)
                act.activation(sg[:, j, :], bank[2 + j][:, 0:I], ACT.Silu).then_inc(sem("e_sg"), 1)
            pairs(act, step)
            gated(SLOT_TILES - 1, 0)

        def dve_experts(dve):
            def step(k, j, first):
                dve.wait_ge(sem("e_sg"), k + 1)
                dve.tensor_tensor(hh[:, j, :], sg[:, j, :], bank[2 + j][:, I:2 * I], ALU.mult).then_inc(sem("e_hh"), 1)
                if not first:
                    back(k - 1, 1 - j)

            def back(k, j):
                dve.wait_ge(sem("e_th"), k + 1)
                dve.tensor_copy(hT[:, j, :], bank[4 + j][:, 0:I]).then_inc(sem("e_hT"), 1)
                dve.wait_ge(sem("e_dn"), k + 1)
                dve.wait_ge(sem(f"ys_out{j}"), ys_value(k, j))
                dve.tensor_copy(yo[:, j, :], bank[6 + j][:]).then_inc(sem("e_yo"), 1)
            pairs(dve, step)
            back(SLOT_TILES - 1, 0)

        def ys_value(k, j):
            return (k - j) * 8 + 16

        def pool_gather(pool):
            pool.wait_ge(sem("ys_out0"), 16 + 16 * ((SLOT_TILES + 1) // 2))
            pool.wait_ge(sem("ys_out1"), 16 + 16 * (SLOT_TILES // 2))
            pool.wait_ge(sem("tx_used"), SLOT_TILES)
            for t in range(TILES):
                if t >= 3:
                    pool.wait_ge(sem("final"), t - 2)
                pool.indirect_dma_start(yg[:, t % 3, :], None, ys_dram, bass.IndirectOffsetOnAxis(posi[:, t:t + 1], 0))\
                    .then_inc(sem(f"gathered{t % 3}"), 16)

        def dve_final(dve):
            for t in range(TILES):
                dve.wait_ge(sem(f"gathered{t % 3}"), 16 * (t // 3 + 1))
                dve.tensor_tensor(xr[:, t, :], xr[:, t, :], yg[:, t % 3, :], ALU.add).then_inc(sem("final"), 1)

        @block.sync
        def _(sp):
            def load_weights(layer):
                if layer == 1:
                    sp.wait_ge(sem("ffn_over"), 5)
                w = (wq0, wk0, wv0, wo0) if layer == 0 else (wq1, wk1, wv1, wo1)
                sp.dma_start(ctx_sb[:], ctxT.rearrange("b (p c) k -> p b c k", c=C)).then_inc(sem("kv_in"), 16)
                for c in range(C):
                    for j in range(4):
                        sp.dma_start(ctx_b[:, :, c, KB * j:KB * j + KB],
                                     ctxT.rearrange("b (p c) k -> p b c k", c=C)[:, :, c, KB0:]).then_inc(sem("kv_in"), 16)
                sp.dma_start(wk[:], w[1].rearrange("(p c) n -> p c n", c=C)).then_inc(sem("kv_in"), 16)
                sp.dma_start(wv[:], w[2].rearrange("(p c) n -> p c n", c=C)).then_inc(sem("kv_in"), 16)
                sp.dma_start(wq[:], w[0].rearrange("(p c) n -> p c n", c=C)).then_inc(sem("kv_in"), 16)
                sp.dma_start(wo[:], w[3].rearrange("(c p) n -> p c n", c=C)).then_inc(sem("kv_in"), 16)
                if layer == 1:
                    sp.dma_start(bq[:], bq1).then_inc(sem("bias_in"), 16)
                    sp.dma_start(bk[:], bk1).then_inc(sem("bias_in"), 16)
                    sp.dma_start(bv[:], bv1.partition_broadcast(P)).then_inc(sem("bias_in"), 16)
                    sp.dma_start(bo[:], bo1.partition_broadcast(P)).then_inc(sem("bias_in"), 16)

            sp.dma_start(xr[:, 0:GT, :], x_tiles[:, 0:GT, :]).then_inc(sem("x_in"), 16)
            load_weights(0)
            sp.wait_ge(sem("const"), 5)
            sp.dma_start(xs_dram.rearrange("(t p) d -> p t d", p=P),
                         zero_row[:].unsqueeze(1).broadcast_to([P, SLOT_TILES, D])).then_inc(sem("slots_zeroed"), 16)
            sp.wait_ge(sem("kv_over"), 4)
            def load_x(g):
                sp.wait_ge(sem("x_in"), 16 * g)
                sp.dma_start(xr[:, bass.ds(GT * g, GT), :], x_tiles[:, bass.ds(GT * g, GT), :])\
                    .then_inc(sem("x_in"), 16)

            def load_masks(b, i):
                g = b * GPB + i
                sp.wait_ge(sem("mask_t_free"), g + 1)
                sp.dma_start(mk_t[:], mask[b, 0].rearrange("(t p) k -> p t k", p=P)[:, bass.ds(GT * i, GT), :])\
                    .then_inc(sem("mask_t_in"), 16)
                sp.wait_ge(sem("mask_free"), g + 1)
                sp.dma_start(mk_a[:], maskT[b, 0:KA, bass.ds(GW * i, GW)]).then_inc(sem("mask_in"), 16)
                for j in range(4):
                    sp.dma_start(mk_b[KB * j:KB * j + KB, :], maskT[b, KB0:KEYS, bass.ds(GW * i, GW)])\
                        .then_inc(sem("mask_in"), 16)

            load_masks(0, 0)
            load_x(1)
            with sp.Fori(1, GPB) as i:
                load_x(i + 1)
                load_masks(0, i)
            with sp.Fori(0, GPB - 1) as i:
                load_x(GPB + 1 + i)
                load_masks(1, i)
            load_masks(1, GPB - 1)
            sp.sem_inc(sem("att0_over"), 1)
            sp.wait_ge(sem("att0_over"), 5)
            for n, (a, b_, g_, be_, l_, lb_) in enumerate([(so_cw, so_cb, so_g, so_be, so_lw, so_lb),
                                                           (si_cw, si_cb, si_g, si_be, si_lw, si_lb)]):
                sp.dma_start(cw[:, n, :], a).then_inc(sem("ffn_in"), 16)
                sp.dma_start(cb[:, n:n + 1], b_.rearrange("(p a) -> p a", a=1)).then_inc(sem("ffn_in"), 16)
                sp.dma_start(gam[:, n:n + 1], g_.rearrange("(p a) -> p a", a=1)).then_inc(sem("ffn_in"), 16)
                sp.dma_start(bet[:, n:n + 1], be_.rearrange("(p a) -> p a", a=1)).then_inc(sem("ffn_in"), 16)
                sp.dma_start(lw[:, n, :], l_).then_inc(sem("ffn_in"), 16)
                sp.dma_start(lb[:, n, :], lb_.partition_broadcast(P)).then_inc(sem("ffn_in"), 16)
            sp.dma_start(wf[:], w_ffn.rearrange("(p c) n -> p c n", c=C)).then_inc(sem("ffn_in"), 16)
            sp.dma_start(bf[:], b_ffn.partition_broadcast(P)).then_inc(sem("ffn_in"), 16)
            sp.sem_inc(sem("ffn_over"), 1)
            load_weights(1)
            sp.sem_inc(sem("att1_over"), 1)
            sp_experts(sp)

        @block.gpsimd
        def _(pool):
            pool_constants(pool)
            pool_att_setup(pool, 0)
            enter_groups(pool, 0)
            pool_att(pool, 0)
            leave(pool, "att0_over", "a_rs", 8)
            with pool.Fori(0, GROUPS) as g:
                pool_stats_group(pool, g)
            pool_batch_norm(pool)
            with pool.Fori(0, GROUPS) as g:
                pool_ffn_group(pool, g)
            leave(pool, "ffn_over", "f_x", 2 + 8 * 4)
            pool_att_setup(pool, 1)
            enter_groups(pool, 1)
            pool_att(pool, 1)
            leave(pool, "att1_over", "a_xb", 8)
            pool.wait_ge(sem("att1_over"), 5)
            pool_sort(pool)
            with pool.Fori(0, GROUPS) as g:
                pool_gate_group(pool, g)
            pool_scatter(pool)
            pool_gather(pool)

        @block.tensor
        def _(pe):
            pe_kv(pe, 0)
            pe_att_start(pe, 0)
            pe_att(pe, 0)
            leave(pe, "att0_over", "o_done", GROUPS * GT)
            pe.sem_inc(sem("t_tp"), 4)
            pe.wait_ge(sem("att0_over"), 5)
            pe.wait_ge(sem("ffn_in"), 14 * 16)
            with pe.Fori(0, GROUPS) as g:
                pe_stats_group(pe, g)
            with pe.Fori(0, GROUPS) as g:
                pe_ffn_group(pe, g)
            leave(pe, "ffn_over", "in_done", 8 * 4)
            pe.wait_ge(sem("ffn_over"), 5)
            pe_kv(pe, 1)
            pe_att_start(pe, 1)
            pe_att(pe, 1)
            leave(pe, "att1_over", "o_done", 2 * GROUPS * GT)
            pe.wait_ge(sem("att1_over"), 5)
            pe.sem_inc(sem("g_tp"), 2)
            pe.wait_ge(sem("gate_in"), 16)
            with pe.Fori(0, GROUPS) as g:
                pe_gate_group(pe, g)
            pe_sort(pe)
            pe_experts(pe)

        @block.scalar
        def _(act):
            act.sem_inc(sem("kT_free"), 2)
            act.sem_inc(sem("a_te"), 2)
            act_kv(act, 0)
            enter_groups(act, 0)
            act_att(act, 0)
            leave(act, "att0_over", "a_rh", GROUPS)
            act.sem_inc(sem("t_te"), 2)
            act.sem_inc(sem("f_te"), 2)
            act.wait_ge(sem("att0_over"), 5)
            act.wait_ge(sem("ffn_in"), 14 * 16)
            with act.Fori(0, GROUPS) as g:
                act_stats_group(act, g)
            act.wait_ge(sem("b_sc"), 3)
            with act.Fori(0, GROUPS) as g:
                act_ffn_group(act, g)
            leave(act, "ffn_over", "f_te", 2 + 8 * 8)
            act.wait_ge(sem("ffn_over"), 5)
            act_kv(act, 1)
            enter_groups(act, 1)
            act_att(act, 1)
            leave(act, "att1_over", "a_rh", 2 * GROUPS)
            act.sem_inc(sem("g_te"), 2)
            act.sem_inc(sem("e_te"), 2)
            act.wait_ge(sem("att1_over"), 5)
            with act.Fori(0, GROUPS) as g:
                act_gate_group(act, g)
            act.wait_ge(sem("s_top"), 1)
            act.activation(rwe[:], top_v[:], ACT.Exp, scale=-1.0).then_inc(sem("s_exp"), 1)
            act_experts(act)

        @block.vector
        def _(dve):
            dve.sem_inc(sem("k_split"), 2)
            dve.sem_inc(sem("v_free"), 2)
            dve.sem_inc(sem("qm_free"), 4)
            dve.sem_inc(sem("o_free"), 6)
            dve.sem_inc(sem("a_raw"), 1)
            dve.sem_inc(sem("mask_t_free"), 1)
            dve.sem_inc(sem("a_sm"), 2)
            dve.sem_inc(sem("a_red"), 2)
            dve.sem_inc(sem("a_at"), 1)
            dve.sem_inc(sem("mask_free"), 1)
            dve_kv(dve, 0)
            enter_groups(dve, 0)
            dve_att(dve, 0)
            leave(dve, "att0_over", "kept", GROUPS)
            dve.sem_inc(sem("t_gs"), 2)
            dve.sem_inc(sem("lg_free"), 2)
            dve.sem_inc(sem("full_free"), 2)
            dve.sem_inc(sem("f_x"), 2)
            dve.sem_inc(sem("f_xs"), 4)
            dve.sem_inc(sem("f_sum"), 2)
            dve.wait_ge(sem("att0_over"), 5)
            dve.wait_ge(sem("ffn_in"), 14 * 16)
            with dve.Fori(0, GROUPS) as g:
                dve_stats_group(dve, g)
            dve_batch_norm(dve)
            with dve.Fori(0, GROUPS) as g:
                dve_ffn_group(dve, g)
            leave(dve, "ffn_over", "f_sum", 2 + 8 * 4)
            dve.wait_ge(sem("ffn_over"), 5)
            dve_kv(dve, 1)
            enter_groups(dve, 1)
            dve_att(dve, 1)
            leave(dve, "att1_over", "kept", 2 * GROUPS)
            dve.sem_inc(sem("ys_out0"), 16)
            dve.sem_inc(sem("ys_out1"), 16)
            dve.sem_inc(sem("g_cp"), 2)
            dve.sem_inc(sem("e_hh"), 2)
            dve.sem_inc(sem("e_hT"), 2)
            dve.sem_inc(sem("e_yo"), 2)
            dve.wait_ge(sem("att1_over"), 5)
            with dve.Fori(0, GROUPS) as g:
                dve_gate_group(dve, g)
            dve_sort(dve)
            dve_experts(dve)
            dve_final(dve)


_INS = ["x", "ctxT", "mask", "maskT", "wq0", "wk0", "wv0", "wo0", "w_ffn", "b_ffn", "so_cw", "so_cb", "so_g", "so_be",
        "so_lw", "so_lb", "si_cw", "si_cb", "si_g", "si_be", "si_lw", "si_lb", "wq1", "bq1", "wk1", "bk1", "wv1", "bv1",
        "wo1", "bo1", "gate_w", "w_in", "w_down"]


def kernel(**inputs):
    import numpy as _np
    import concourse.bacc as _bacc
    from concourse import mybir as _mybir
    from concourse.bass_utils import run_bass_kernel_spmd as _run

    a = {k: _np.asarray(v) for k, v in inputs.items()}
    f, t = "L0_ffn_", "L1_xattn_"
    given = dict(
        x=a["x"], ctxT=a["ctx_1024"].transpose(0, 2, 1), mask=a["mask_Bx1xSxS2_ff0"],
        maskT=a["mask_Bx1xSxS2_ff0"][:, 0].transpose(0, 2, 1),
        wq0=a["L0_xattn_wq"].reshape(D, D), wk0=a["L0_xattn_wk"].reshape(D, D), wv0=a["L0_xattn_wv"].reshape(D, D),
        wo0=a["L0_xattn_wo"].reshape(D, D), w_ffn=a[f + "weight"], b_ffn=a[f + "bias"],
        so_cw=a[f + "so_conv_w"], so_cb=a[f + "so_conv_b"], so_g=a[f + "so_gamma"], so_be=a[f + "so_beta"],
        so_lw=a[f + "so_lin_w"].T, so_lb=a[f + "so_lin_b"], si_cw=a[f + "si_conv_w"], si_cb=a[f + "si_conv_b"],
        si_g=a[f + "si_gamma"], si_be=a[f + "si_beta"], si_lw=a[f + "si_lin_w"].T, si_lb=a[f + "si_lin_b"],
        wq1=a[t + "W_Q"].T, bq1=a[t + "b_Q"].reshape(C, P).T, wk1=a[t + "W_K"].T, bk1=a[t + "b_K"].reshape(C, P).T, wv1=a[t + "W_V"].T,
        bv1=a[t + "b_V"], wo1=a[t + "W_O"].T, bo1=a[t + "b_O"], gate_w=a["L1_ffn_gate_w"].T,
        w_in=_np.concatenate([a["L1_ffn_w_gate"], a["L1_ffn_w_up"]], axis=1).transpose(0, 2, 1),
        w_down=a["L1_ffn_w_down"].transpose(0, 2, 1))
    nc = _bacc.Bacc("TRN2", target_bir_lowering=False, num_devices=1)
    arrays, args = {}, []
    for name in _INS:
        v = _np.ascontiguousarray(given[name])
        arrays[f"in_{name}"] = v
        args.append(nc.dram_tensor(f"in_{name}", v.shape, _mybir.dt.from_np(v.dtype), kind="ExternalInput").ap())
    args.append(nc.dram_tensor("out_x", (B, S, D), F32, kind="ExternalOutput").ap())
    program(nc, *args)
    r = _run(nc, [arrays], core_ids=[0])
    return r.results[0]["out_x"]
```

```python
from contextlib import ExitStack

import concourse.bass as bass
from concourse import mybir

F32 = mybir.dt.float32
F32R = mybir.dt.float32r
I32 = mybir.dt.int32
U32 = mybir.dt.uint32
ACT = mybir.ActivationFunctionType
ALU = mybir.AluOpType
AX = mybir.AxisListType

P = 128
D = 512
C = D // P
B = 2
S = 2048
N = B * S
TILES = N // P
GT = 4
GW = GT * P
GROUPS = TILES // GT
GPB = GROUPS // B
H = 16
DH = D // H
QUADS = H // 4
KEYS = 154
KA = 128
KB = 32
KB0 = KEYS - KB
DUP = KA - KB0
QK = 4 * (KA + KB)
EPS = 1e-5
K_TOP = 32
E = 8
I = 256
SLOT_TILES = TILES + E - 1
GONE = -3.0e38

ATT = dict(a_bn=4, a_mv=4, a_ve=1, a_rs=1, a_xn=4, a_tp=4, a_te=4, a_qh=4, qm_done=24, qm_free=24, a_red=20, a_mx=1,
           a_mt=1, a_mh=1, a_ml=1, sc_done=20, a_sm=20, p_done=20, pv_done=4, a_raw=4, a_rc=1, a_rh=1, a_rl=1,
           spread=4, a_at=4, o_done=4, o_free=4, o_bn=4, o_mv=4)
STAT = dict(t_xn=4, t_tp=4, t_te=4, t_xc=8, t_cp=2, t_gs=2)
FFN = dict(f_xn=4, f_xb=1, f_tp=8, f_te=8, f_ge=2, lg_done=8, f_top=64, f_nm=8, f_ex=8, f_rc=8, f_sel=8,
           f_xs=4, full_done=4, full_free=4, in_done=4, f_sum=4, f_x=4)
GATE = dict(g_xn=4, g_tp=4, g_te=4, g_lg=1, g_cp=1)


def program(nc, x, ctxT, mask, maskT, wq0, wk0, wv0, wo0, w_ffn, b_ffn, so_cw, so_cb, so_g, so_be, so_lw, so_lb,
            si_cw, si_cb, si_g, si_be, si_lw, si_lb, wq1, bq1, wk1, bk1, wv1, bv1, wo1, bo1, gate_w, w_in, w_down, out):
    xs_dram = nc.dram_tensor("sorted_tokens", (SLOT_TILES * P, D), F32, kind="Internal").ap()
    ys_dram = nc.dram_tensor("sorted_outputs", (SLOT_TILES * P, D), F32, kind="Internal").ap()
    x_tiles = x.rearrange("b (t p) d -> p (b t) d", p=P)
    out_tiles = out.rearrange("b (t p) d -> p (b t) d", p=P)

    top = ExitStack()
    with top:
        sems = {}

        def sem(name):
            if name not in sems:
                sems[name] = top.enter_context(nc.semaphore(name))
            return sems[name]

        def at(table, name, group, k):
            return group * table[name] + k

        def scope():
            stack = ExitStack()

            def sb(name, shape, dt=F32):
                return stack.enter_context(nc.sbuf_tensor(name, shape, dt))
            return stack, sb

        bank = [top.enter_context(nc.psum_tensor(f"bank{i}", [P, D], F32)) for i in range(8)]

        def sb(name, shape, dt=F32):
            return top.enter_context(nc.sbuf_tensor(name, shape, dt))

        xr = sb("x_res", [P, TILES, D])
        ident = sb("ident", [P, P])
        zero = sb("zero", [P, C])
        zero_row = sb("zero_row", [P, D])
        bn = sb("bn", [P, GT, 6])
        mv = sb("mv", [P, GT, 2])
        ve = sb("ve", [P, GT])
        expo = sb("expo", [P, TILES])
        rs = sb("rs", [P, GT])
        bn_o = sb("bn_o", [P, GT, 6])
        mv_o = sb("mv_o", [P, GT, 2])
        mv_all = sb("mv_all", [P, TILES, 2])
        rs_all = sb("rs_all", [P, TILES])
        ve_all = sb("ve_all", [P, TILES])
        eps_c = sb("eps_c", [P, TILES])

        att, sb = scope()
        wq = sb("wq", [P, C, D])
        wo = sb("wo", [P, C, D])
        kh = sb("kh", [P, B, QUADS, QK], F32R)
        kl = sb("kl", [P, B, QUADS, QK], F32R)
        va = sb("va", [P, B, D])
        vb = sb("vb", [P, B, QUADS, P])
        one_a = sb("one_a", [P, QUADS, DH])
        one_b = sb("one_b", [P, QUADS, P])
        spread = sb("spread", [P, QUADS, 4, DH], F32R)
        sel = sb("sel", [P, H], F32R)
        sel_b = sb("sel_b", [P, QUADS, 4, KB], F32R)
        neg_max = sb("neg_max", [P, GW], F32R)
        bq = sb("bq", [P, C])
        bo = sb("bo", [P, D])
        mx = sb("mx", [P, GT, H])
        mxb = sb("mxb", [P, GT, H])
        work = ExitStack()
        xn = work.enter_context(nc.sbuf_tensor("xn", [P, GT, D], F32))
        xnT = work.enter_context(nc.sbuf_tensor("xnT", [P, C, GW], F32))
        qh = work.enter_context(nc.sbuf_tensor("qh", [P, C, GW], F32R))
        ql = work.enter_context(nc.sbuf_tensor("ql", [P, C, GW], F32R))
        lent = ExitStack()
        rc = lent.enter_context(nc.sbuf_tensor("rc", [P, GW], F32))
        rch = lent.enter_context(nc.sbuf_tensor("rch", [P, GW], F32R))
        rcl = lent.enter_context(nc.sbuf_tensor("rcl", [P, GW], F32R))
        lent.close()
        pr = work.enter_context(nc.sbuf_tensor("probs", [P, 10, GW], F32))
        attnT = xn
        mtmp = work.enter_context(nc.sbuf_tensor("mtmp", [P, 2, D], F32))
        mk_t = work.enter_context(nc.sbuf_tensor("mk_t", [P, GT, KEYS], F32))
        mk_a = work.enter_context(nc.sbuf_tensor("mk_a", [P, GW], F32))
        mk_b = work.enter_context(nc.sbuf_tensor("mk_b", [P, GW], F32))
        work.close()
        work.enter_context(nc.sbuf_tensor("beyond", [P, 9440], F32))
        ctx_sb = work.enter_context(nc.sbuf_tensor("ctxT", [P, B, C, KEYS], F32))
        ctx_b = work.enter_context(nc.sbuf_tensor("ctx_b", [P, B, C, P], F32))
        wk = work.enter_context(nc.sbuf_tensor("wk", [P, C, D], F32))
        wv = work.enter_context(nc.sbuf_tensor("wv", [P, C, D], F32))
        bk = work.enter_context(nc.sbuf_tensor("bk", [P, C], F32))
        bks = work.enter_context(nc.sbuf_tensor("bks", [P, C], F32))
        bv = work.enter_context(nc.sbuf_tensor("bv", [P, D], F32))
        kf = work.enter_context(nc.sbuf_tensor("kf", [P, 2, KEYS], F32))
        work.close()
        att.close()

        ffn, sb = scope()
        xc = [sb("xc_so", [P, N]), sb("xc_si", [P, N])]
        gst = sb("gst", [P, 2, GROUPS, 6])
        gmv = sb("gmv", [P, 2, 2])
        gve = sb("gve", [P, 2])
        grs = sb("grs", [P, 2])
        gsc = sb("gsc", [P, 2])
        gbi = sb("gbi", [P, 2])
        gtm = sb("gtm", [P, 2])
        cw = sb("cw", [P, 2, 4])
        cb = sb("cb", [P, 2])
        gam = sb("gam", [P, 2])
        bet = sb("bet", [P, 2])
        wf = sb("wf", [P, C, D])
        lw = sb("lw", [P, 2, D])
        lb = sb("lb", [P, 2, D])
        lbr = sb("lbr", [P, 2, D], F32R)
        one_r = sb("one_r", [P, P], F32R)
        bf = sb("bf", [P, D])
        fxn = sb("fxn", [P, GT, D])
        fxT = sb("fxT", [P, C, GW])
        ge = sb("ge", [P, 2, GW])
        Wk = sb("Wk", [P, 2, 2, D])
        ex = sb("ex", [P, 2, D])
        m8 = sb("m8", [P, 2, 8])
        fnm = sb("fnm", [P, 2])
        fsum = sb("fsum", [P, 2])
        frc = sb("frc", [P, 2])
        selv = sb("selv", [P, 2, D])
        fxs = sb("fxs", [P, D])
        fxsT = sb("fxsT", [P, D])
        ftmp = sb("ftmp", [P, 2, D])
        fsm = sb("fsm", [P, 2, D])
        sxT = [fxT, sb("sxT", [P, C, GW])]
        ffn.close()

        moe, sb = scope()
        w_in_sb = sb("w_in", [P, E * C * 2 * I])
        w_dn_sb = sb("w_down", [P, E * 2 * D])
        gw = sb("gate_w", [P, C, E])
        mxn = sb("mxn", [P, GT, D])
        mxT = sb("mxT", [P, GT, D])
        below = sb("below", [P, TILES, E])
        cand = sb("cand", [P, TILES, E])
        cmp = sb("cmp", [P, SLOT_TILES, E - 1])
        tiles_f = sb("tiles_f", [P, E])
        start = sb("start", [P, E + 1])
        lgt = sb("lgt", [P, TILES, E])
        top_v = sb("top_v", [P, TILES])
        selx = sb("selx", [P, TILES])
        iota_e = sb("iota_e", [P, E])
        onehot = sb("onehot", [P, TILES, E])
        tri = sb("tri", [P, P])
        ones = sb("ones", [P, P])
        rank = sb("rank", [P, TILES, E])
        cnt = sb("cnt", [P, 2, TILES, E])
        own = sb("own", [P, TILES, E])
        tot = sb("tot", [P, E])
        toti = sb("toti", [P, E], I32)
        prod = sb("prod", [P, TILES, E])
        posf = sb("posf", [P, TILES])
        posi = sb("posi", [P, TILES], I32)
        slot_i = sb("slot_i", [P, SLOT_TILES])
        slot_e = sb("slot_e", [P, SLOT_TILES])
        slot_ei = sb("slot_ei", [P, SLOT_TILES], I32)
        rwe = sb("rwe", [P, TILES])
        rw = sb("rw", [P, TILES])
        srs = sb("srs", [P, TILES])
        xs = sb("xs", [P, 4, D])
        tx = xs
        txT = mxT
        sg = sb("sg", [P, 2, I])
        hh = sb("hh", [P, 2, I])
        hT = sb("hT", [P, 2, I])
        yo = mxn
        yg = xs
        moe.close()

        block = top.enter_context(nc.Block())

        def pipelined(eng, layer, ahead, body):
            ahead(0, 0)
            body(0, 0, 1, 0)
            with eng.Fori(1, GPB - 1) as i:
                body(i, 0, i + 1, 0)
            body(GPB - 1, 0, GPB, 1)
            with eng.Fori(0, GPB - 1) as i:
                body(GPB + i, 1, GPB + i + 1, 1)
            body(GROUPS - 1, 1, None, None)

        def pool_constants(pool):
            pool.memset(ident[:], 0.0).then_inc(sem("c_0"), 1)
            pool.memset(zero[:], 0.0).then_inc(sem("const"), 1)
            pool.memset(zero_row[:], 0.0).then_inc(sem("const"), 1)
            pool.memset(expo[:], -0.5).then_inc(sem("const"), 1)
            pool.memset(eps_c[:], EPS).then_inc(sem("const"), 1)
            pool.wait_ge(sem("c_0"), 1)
            pool.affine_select(out=ident[:], in_=ident[:], compare_op=ALU.not_equal, fill=1.0, base=0,
                               pattern=[[-1, P]], channel_multiplier=1).then_inc(sem("const"), 1)

        def pool_att_setup(pool, layer):
            if layer == 1:
                pool.wait_ge(sem("ffn_over"), 5)
            zeroed = sem("zeroed")
            pool.memset(kh[:].bitcast(F32), 0.0).then_inc(zeroed, 1)
            pool.memset(one_b[:], 0.0).then_inc(zeroed, 1)
            pool.memset(one_a[:], 0.0).then_inc(zeroed, 1)
            pool.memset(spread[:].bitcast(F32), 0.0).then_inc(zeroed, 1)
            pool.memset(sel[:].bitcast(F32), 0.0).then_inc(zeroed, 1)
            pool.memset(neg_max[:].bitcast(F32), 0.0).then_inc(sem("selected"), 1)
            pool.wait_ge(zeroed, layer * 7 + 7)
            pool.affine_select(out=sel[:], in_=sel[:].bitcast(F32), compare_op=ALU.not_equal, fill=1.0, base=0,
                               pattern=[[-1, H]], channel_multiplier=1).then_inc(sem("selected"), 1)
            pool.affine_select(out=spread[:], in_=spread[:].bitcast(F32), compare_op=ALU.not_equal, fill=1.0, base=0,
                               pattern=[[-1, QUADS], [-32, 4], [0, DH]], channel_multiplier=1)\
                .then_inc(sem("selected"), 1)
            pool.affine_select(out=one_a[:], in_=one_a[:], compare_op=ALU.not_equal, fill=1.0, base=0,
                               pattern=[[-1, QUADS], [1, DH]], channel_multiplier=0).then_inc(sem("selected"), 1)
            pool.wait_ge(sem("selected"), layer * 7 + 4)
            pool.affine_select(out=sel[:], in_=sel[:].bitcast(F32), compare_op=ALU.not_equal, fill=1.0, base=-32,
                               pattern=[[-1, H]], channel_multiplier=1).then_inc(sem("selected"), 1)
            pool.memset(one_a[:, 0, QUADS:], 1.0).then_inc(sem("selected"), 1)
            pool.wait_ge(sem("selected"), layer * 7 + 6)
            pool.tensor_copy(sel_b[:].rearrange("p q h k -> p (q h) k"), sel[:].unsqueeze(2).broadcast_to([P, H, KB]))\
                .then_inc(sem("selected"), 1)
            pool.sem_inc(sem("kv_over"), 1)

        def hold(eng, name, value):
            eng.wait_ge(sem(name), value)
            eng.sem_inc(sem("held"), 1)

        def pool_att(pool, layer):
            def rstd(g, b):
                G = layer * GROUPS + g
                pool.wait_ge(sem("a_mv"), at(ATT, "a_mv", G, GT))
                pool.tensor_tensor(ve[:], mv[:, :, 1], eps_c[:, 0:GT], ALU.add).then_inc(sem("a_ve"), 1)
                pool.wait_ge(sem("a_ve"), at(ATT, "a_ve", G, 1))
                pool.tensor_tensor(rs[:], ve[:], expo[:, 0:GT], ALU.pow).then_inc(sem("a_rs"), 1)
                if layer == 1:
                    hold(pool, "a_xn", at(ATT, "a_xn", G, GT))
                    xg = xr[:, bass.ds(g * GT, GT), :]
                    pool.tensor_tensor(xg, xg, bo[:].unsqueeze(1).broadcast_to([P, GT, D]), ALU.add)\
                        .then_inc(sem("a_xb"), 1)

            def body(g, b, n, bn_):
                if n is not None:
                    rstd(n, bn_)
                G = layer * GROUPS + g
                pool.wait_ge(sem("a_rh"), at(ATT, "a_rh", G, 1))
                pool.tensor_tensor(rcl[:], rc[:], rch[:], ALU.subtract).then_inc(sem("a_rl"), 1)
            pipelined(pool, layer, rstd, body)

        def tile_of(buf, g, t):
            return buf[:, bass.ds(g * GT + t, 1), :].rearrange("p a d -> p (a d)")

        def leave(eng, phase, last, value):
            eng.wait_ge(sem(last), value)
            eng.sem_inc(sem(phase), 1)

        def diagonal(u):
            for j in range(4):
                rows = slice(DH * j, DH * j + DH)
                yield rows, slice(0, KA), slice(KA * j, KA * j + KA)
                yield rows, slice(KB0, KEYS), slice(4 * KA + KB * j, 4 * KA + KB * j + KB)

        def pe_kv(pe, layer):
            pe.wait_ge(sem("k_in"), (layer + 1) * 32)
            pe.wait_ge(sem("const"), 5)
            for b in range(B):
                for q in range(QUADS):
                    u = b * QUADS + q
                    pe.wait_ge(sem("kT_free"), layer * 8 + u + 1)
                    for c in range(C):
                        mm = pe.matmul(bank[u % 2][:, 0:KEYS], wk[:, c, P * q:P * q + P], ctx_sb[:, b, c, :],
                                       start=(c == 0), stop=(c == C - 1))
                    mm.then_inc(sem("kT_done"), 1)
            pe.wait_ge(sem("v_in"), (layer + 1) * 16 * (1 + 4 * C))
            for b in range(B):
                pe.wait_ge(sem("v_free"), layer * 4 + 2 * b + 2)
                for c in range(C):
                    mm = pe.matmul(bank[4][:], ctx_sb[:, b, c, 0:KA], wv[:, c, :], start=(c == 0), stop=(c == C - 1))
                mm.then_inc(sem("v_done"), 1)
                for c in range(C):
                    mm = pe.matmul(bank[5][:], ctx_b[:, b, c, :], wv[:, c, :], start=(c == 0), stop=(c == C - 1))
                mm.then_inc(sem("v_done"), 1)
            pe.sem_inc(sem("kv_over"), 1)

        def act_kv(act, layer):
            scale = float(DH) ** -0.5
            if layer == 1:
                act.wait_ge(sem("kv_bias_in"), 32)
                act.activation(bks[:], bk[:], ACT.Copy, scale=scale).then_inc(sem("bks"), 1)
                act.wait_ge(sem("bks"), 1)
            act.wait_ge(sem("zeroed"), layer * 7 + 7)
            for u in range(B * QUADS):
                bias = bks[:, u % QUADS:u % QUADS + 1] if layer == 1 else 0.0
                U = layer * B * QUADS + u
                act.wait_ge(sem("kT_done"), U + 1)
                act.wait_ge(sem("k_split"), U + 1)
                act.activation(kf[:, u % 2, :], bank[u % 2][:, 0:KEYS], ACT.Identity, scale=scale, bias=bias)\
                    .then_inc(sem("kT_free"), 1)
                act.wait_ge(sem("kT_free"), U + 3)
                for rows, part, cols in diagonal(u):
                    hi = act.activation(kh[rows, u // QUADS, u % QUADS, cols], kf[rows, u % 2, part], ACT.Copy)
                hi.then_inc(sem("k_hi"), 1)
            act.sem_inc(sem("kv_over"), 1)

        def dve_kv(dve, layer):
            if layer == 1:
                dve.wait_ge(sem("kv_bias_in"), 32)
            dve.memset(kl[:].bitcast(F32), 0.0).then_inc(sem("zeroed"), 1)
            dve.memset(vb[:], 0.0).then_inc(sem("zeroed"), 1)
            dve.wait_ge(sem("zeroed"), layer * 7 + 7)
            flat_b = one_b[:].rearrange("p q n -> p (q n)")
            for j in range(4):
                rows = slice(KB * j, KB * j + KB)
                dve.memset(flat_b[rows, KB * j:KB * j + 3 * (P + 1) + 1:P + 1], 1.0).then_inc(sem("one_b"), 1)
                dve.memset(one_b[rows, 0, KB * j + QUADS:KB * j + KB], 1.0).then_inc(sem("one_b"), 1)
            dve.wait_ge(sem("one_b"), layer * 12 + 8)
            for j in range(4):
                dve.memset(one_b[KB * j:KB * j + DUP, :, :], 0.0).then_inc(sem("one_b"), 1)
            for u in range(B * QUADS):
                U = layer * B * QUADS + u
                dve.wait_ge(sem("k_hi"), U + 1)
                for rows, part, cols in diagonal(u):
                    lo = dve.tensor_tensor(kl[rows, u // QUADS, u % QUADS, cols], kf[rows, u % 2, part],
                                           kh[rows, u // QUADS, u % QUADS, cols], ALU.subtract)
                lo.then_inc(sem("k_split"), 1)
            for b in range(B):
                dve.wait_ge(sem("v_done"), layer * 4 + 2 * b + 1)
                if layer == 0:
                    dve.tensor_copy(va[:, b, :], bank[4][:]).then_inc(sem("v_free"), 1)
                else:
                    dve.tensor_tensor(va[:, b, :], bank[4][:], bv[:], ALU.add).then_inc(sem("v_free"), 1)
                dve.wait_ge(sem("v_done"), layer * 4 + 2 * b + 2)
                for j in range(4):
                    rows = slice(KB * j, KB * j + KB)
                    dst = vb[rows, b, :, KB * j:KB * j + KB]
                    src = bank[5][rows, :].rearrange("p (q n) -> p q n", q=QUADS)[:, :, KB * j:KB * j + KB]
                    if layer == 0:
                        cp = dve.tensor_copy(dst, src)
                    else:
                        cp = dve.tensor_tensor(dst, src, bv[rows, :].rearrange("p (q n) -> p q n", q=QUADS)
                                               [:, :, KB * j:KB * j + KB], ALU.add)
                cp.then_inc(sem("v_free"), 1)
            dve.wait_ge(sem("v_free"), 2 + 4 * (layer + 1))
            for j in range(4):
                ms = dve.memset(vb[KB * j:KB * j + DUP, :, :, :], 0.0)
            ms.then_inc(sem("vb_ready"), 1)
            dve.sem_inc(sem("kv_over"), 1)

        def enter_groups(eng, layer):
            eng.wait_ge(sem("kv_over"), 4 * (layer + 1))
            eng.wait_ge(sem("qo_in"), 32 * (layer + 1))
            if layer == 1:
                eng.wait_ge(sem("qo_bias_in"), 32)

        def pe_att_start(pe, layer):
            enter_groups(pe, layer)
            pe.wait_ge(sem("k_split"), (layer + 1) * B * QUADS + 2)
            pe.wait_ge(sem("vb_ready"), layer + 1)
            pe.wait_ge(sem("selected"), (layer + 1) * 7)
            pe.wait_ge(sem("one_b"), (layer + 1) * 12)
            if layer == 0:
                pe.sem_inc(sem("pv_done"), 2)

        def qm(u):
            return bank[(2, 3, 0, 1)[u % 4]]

        def out_bank(t):
            return bank[(6, 7, 0, 1)[t]]

        def pe_att(pe, layer):
            def turn(g):
                G = layer * GROUPS + g
                for t in range(GT):
                    pe.wait_ge(sem("a_xn"), at(ATT, "a_xn", G, t + 1))
                    pe.wait_ge(sem("a_te"), at(ATT, "a_te", G, t + 1))
                    if t < 2:
                        pe.wait_ge(sem("o_free"), at(ATT, "o_free", G, t + 1))
                    for c in range(C):
                        mm = pe.transpose(bank[t % 2][:, P * c:P * c + P], xn[:, t, c::C], ident[:])
                    mm.then_inc(sem("a_tp"), 1)

            def queries(g, q):
                G = layer * GROUPS + g
                if q == 0:
                    pe.wait_ge(sem("a_te"), at(ATT, "a_te", G, GT + 2))
                u = 6 * q
                pe.wait_ge(sem("qm_free"), at(ATT, "qm_free", G, u + 1))
                for c in range(C):
                    mm = pe.matmul(qm(u)[:], wq[:, c, P * q:P * q + P], xnT[:, c, :], start=(c == 0),
                                   stop=(c == C - 1))
                mm.then_inc(sem("qm_done"), 1)

            def shifts(g, b, q):
                G = layer * GROUPS + g
                pe.wait_ge(sem("a_qh"), at(ATT, "a_qh", G, q + 1))
                for t in range(GT + 1):
                    u = 6 * q + 1 + t
                    pe.wait_ge(sem("qm_free"), at(ATT, "qm_free", G, u + 1))
                    o = qm(u)
                    if t < GT:
                        mm = pe.matmul(o[:], qh[:, q, P * t:P * t + P], kh[:, b, q, 0:4 * KA], start=True, stop=True)
                    else:
                        for i in range(GT):
                            mm = pe.matmul(o[:, P * i:P * i + P], qh[:, q, P * i:P * i + P], kh[:, b, q, 4 * KA:QK],
                                           start=(i == 0), stop=(i == GT - 1), skip_group_check=True)
                    mm.then_inc(sem("qm_done"), 1)

            def turn_max(g):
                G = layer * GROUPS + g
                pe.wait_ge(sem("a_mx"), at(ATT, "a_mx", G, 1))
                for t in range(GT):
                    mm = pe.transpose(bank[4][0:H, P * t:P * t + P], mx[:, t, :], ident[:])
                mm.then_inc(sem("a_mt"), 1)

            def scores(g, b, q):
                G = layer * GROUPS + g
                pe.wait_ge(sem("qm_free"), at(ATT, "qm_free", G, 6 * q + 5))
                if q == 0:
                    pe.wait_ge(sem("a_ml"), at(ATT, "a_ml", G, 1))
                for j in range(5):
                    u = 5 * q + j
                    o = bank[4 + u % 2]
                    if layer == 0:
                        pe.wait_ge(sem("a_sm"), at(ATT, "a_sm", G, u + 1))
                    else:
                        pe.wait_ge(sem("p_done"), at(ATT, "p_done", G, u - 1))
                    cols = slice(KA * j, KA * j + KA)
                    pe.matmul(o[:], kh[:, b, q, cols], qh[:, q, :], start=True, stop=False)
                    pe.matmul(o[:], kh[:, b, q, cols], ql[:, q, :], start=False, stop=False)
                    pe.matmul(o[:], kl[:, b, q, cols], qh[:, q, :], start=False, stop=False)
                    if j < 4:
                        pick = sel[:, 4 * q + j:4 * q + j + 1].broadcast_to([P, P])
                    else:
                        pick = sel_b[:, q, :, :].rearrange("p h k -> p (h k)")
                    pe.matmul(o[:], pick, neg_max[:], start=False, stop=True).then_inc(sem("sc_done"), 1)

            def values(g, b, q):
                G = layer * GROUPS + g
                pe.wait_ge(sem("a_raw"), at(ATT, "a_raw", G, q + 1))
                if q == 0:
                    pe.wait_ge(sem("a_at"), at(ATT, "a_at", G, 1))
                    pe.wait_ge(sem("o_free"), at(ATT, "o_free", G, 4))
                pe.wait_ge(sem("p_done"), at(ATT, "p_done", G, 5 * q + 5))
                slot = 5 * (q % 2)
                for j in range(4):
                    pe.matmul(bank[6][DH * j:DH * j + DH, :], va[:, b, P * q + DH * j:P * q + DH * j + DH],
                              pr[:, slot + j, :], start=True, stop=False, skip_group_check=True)
                for j in range(4):
                    pe.matmul(bank[7][DH * j:DH * j + DH, :], one_a[:, q, :], pr[:, slot + j, :],
                              start=(q == 0), stop=False, skip_group_check=True)
                pe.matmul(bank[6][:], vb[:, b, q, :], pr[:, slot + 4, :], start=False, stop=True, skip_group_check=True)
                pe.matmul(bank[7][:], one_b[:, q, :], pr[:, slot + 4, :], start=False, stop=(q == QUADS - 1),
                          skip_group_check=True).then_inc(sem("pv_done"), 1)

            def spread_sums(g):
                G = layer * GROUPS + g
                pe.wait_ge(sem("a_rl"), at(ATT, "a_rl", G, 1))
                pe.wait_ge(sem("a_raw"), at(ATT, "a_raw", G, QUADS + 1))
                for q in range(QUADS):
                    o = bank[6 + q % 2]
                    if q >= 2:
                        pe.wait_ge(sem("a_at"), at(ATT, "a_at", G, q))
                    w = spread[:, q, :, :].rearrange("p h n -> p (h n)")
                    pe.matmul(o[:], w, rch[:], start=True, stop=False)
                    pe.matmul(o[:], w, rcl[:], start=False, stop=True).then_inc(sem("spread"), 1)

            def project(g, tiles):
                G = layer * GROUPS + g
                for t in tiles:
                    pe.wait_ge(sem("o_free"), at(ATT, "o_free", G, t + 3))
                    if t == 0:
                        pe.wait_ge(sem("a_at"), at(ATT, "a_at", G, QUADS + 1))
                    for q in range(QUADS):
                        mm = pe.matmul(out_bank(t)[:], attnT[:, q, P * t:P * t + P], wo[:, q, :], start=(q == 0),
                                       stop=(q == QUADS - 1))
                    mm.then_inc(sem("o_done"), 1)

            def ahead(g, b):
                turn(g)
                for q in range(QUADS):
                    queries(g, q)
                    shifts(g, b, q)
                turn_max(g)

            def body(g, b, n, bn_):
                scores(g, b, 0)
                scores(g, b, 1)
                values(g, b, 0)
                if n is not None:
                    turn(n)
                for q in range(2):
                    if n is not None:
                        queries(n, q)
                    scores(g, b, q + 2)
                    if n is not None:
                        shifts(n, bn_, q)
                    values(g, b, q + 1)
                if n is not None:
                    queries(n, 2)
                    shifts(n, bn_, 2)
                values(g, b, 3)
                if n is not None:
                    queries(n, 3)
                spread_sums(g)
                if n is not None:
                    shifts(n, bn_, 3)
                project(g, (0, 1))
                if n is not None:
                    turn_max(n)
                project(g, (2, 3))
            pipelined(pe, layer, ahead, body)

        def act_att(act, layer):
            def feature_major(g):
                G = layer * GROUPS + g
                for t in range(GT):
                    act.wait_ge(sem("a_tp"), at(ATT, "a_tp", G, t + 1))
                    act.activation(xnT[:, :, P * t:P * t + P], bank[t % 2][:].rearrange("p (c n) -> p c n", c=C),
                                   ACT.Copy).then_inc(sem("a_te"), 1)

            def high_queries(g, q):
                G = layer * GROUPS + g
                act.wait_ge(sem("qm_done"), at(ATT, "qm_done", G, 6 * q + 1))
                bias = bq[:, q:q + 1] if layer == 1 else zero[:, q:q + 1]
                act.activation(qh[:, q, :], qm(6 * q)[:], ACT.Identity, bias=bias).then_inc(sem("a_qh"), 1)

            def high_shift(g):
                G = layer * GROUPS + g
                act.wait_ge(sem("a_mt"), at(ATT, "a_mt", G, 1))
                act.activation(neg_max[0:H, :], bank[4][0:H, :], ACT.Copy, scale=-1.0).then_inc(sem("a_mh"), 1)

            def exps(g, q):
                G = layer * GROUPS + g
                for j in range(5):
                    u = 5 * q + j
                    slot = u % 10
                    if layer == 0:
                        act.wait_ge(sem("a_sm"), at(ATT, "a_sm", G, u + 3))
                        act.activation(pr[:, slot, :], pr[:, slot, :], ACT.Exp).then_inc(sem("p_done"), 1)
                    else:
                        act.wait_ge(sem("sc_done"), at(ATT, "sc_done", G, u + 1))
                        act.wait_ge(sem("pv_done"), at(ATT, "pv_done", G, q + 1))
                        act.activation(pr[:, slot, :], bank[4 + u % 2][:], ACT.Exp).then_inc(sem("p_done"), 1)

            def take_values(g, q):
                G = layer * GROUPS + g
                act.wait_ge(sem("pv_done"), at(ATT, "pv_done", G, q + 3))
                act.activation(attnT[:, q, :], bank[6][:], ACT.Copy).then_inc(sem("a_raw"), 1)

            def ahead(g, b):
                feature_major(g)
                for q in range(QUADS):
                    high_queries(g, q)
                high_shift(g)

            def body(g, b, n, bn_):
                G = layer * GROUPS + g
                exps(g, 0)
                exps(g, 1)
                if n is not None:
                    feature_major(n)
                take_values(g, 0)
                for q in range(2):
                    if n is not None:
                        high_queries(n, q)
                    exps(g, q + 2)
                    take_values(g, q + 1)
                if n is not None:
                    high_queries(n, 2)
                take_values(g, 3)
                act.wait_ge(sem("a_rc"), at(ATT, "a_rc", G, 1))
                act.activation(rch[:], rc[:], ACT.Copy).then_inc(sem("a_rh"), 1)
                if n is not None:
                    high_queries(n, 3)
                    high_shift(n)
            pipelined(act, layer, ahead, body)

        def dve_att(dve, layer):
            def stats(g):
                if layer == 0:
                    dve.wait_ge(sem("x_in"), 16 * g + 16)
                G = layer * GROUPS + g
                for t in range(GT):
                    dve.bn_stats(bn[:, t, :], tile_of(xr, g, t)).then_inc(sem("a_bn"), 1)
                for t in range(GT):
                    hold(dve, "a_bn", at(ATT, "a_bn", G, t + 1))
                    dve.bn_aggr(mv[:, t, :], bn[:, t, :]).then_inc(sem("a_mv"), 1)

            def normalise(g):
                G = layer * GROUPS + g
                hold(dve, "a_rs", at(ATT, "a_rs", G, 1))
                for t in range(GT):
                    dve.tensor_scalar(xn[:, t, :], tile_of(xr, g, t), mv[:, t, 0:1], rs[:, t:t + 1],
                                      ALU.subtract, ALU.mult).then_inc(sem("a_xn"), 1)

            def low_queries(g, q):
                G = layer * GROUPS + g
                dve.wait_ge(sem("a_qh"), at(ATT, "a_qh", G, q + 1))
                bias = bq[:, q:q + 1] if layer == 1 else zero[:, q:q + 1]
                dve.scalar_tensor_tensor(ql[:, q, :], qm(6 * q)[:], bias, qh[:, q, :], ALU.add, ALU.subtract)\
                    .then_inc(sem("qm_free"), 1)

            def maxima(g, q):
                G = layer * GROUPS + g
                if layer == 0 and q == 0:
                    dve.wait_ge(sem("mask_t_in"), g * 16 + 16)
                for t in range(GT + 1):
                    u = 6 * q + 1 + t
                    dve.wait_ge(sem("qm_done"), at(ATT, "qm_done", G, u + 1))
                    if t < GT:
                        dims, args = "p (h k) -> p h k", dict(h=4)
                        dst = mx[:, t, 4 * q:4 * q + 4]
                        mk = mk_t[:, t, 0:KA].unsqueeze(1).broadcast_to([P, 4, KA])
                    else:
                        dims, args = "p (t h k) -> p t h k", dict(t=GT, h=4)
                        dst = mxb[:, :, 4 * q:4 * q + 4]
                        mk = mk_t[:, :, KB0:KEYS].unsqueeze(2).broadcast_to([P, GT, 4, KB])
                    src = qm(u)[:].rearrange(dims, **args)
                    if layer == 0:
                        r = 5 * q + t
                        tmp = mtmp[:, r % 2, :].rearrange(dims, **args)
                        dve.wait_ge(sem("a_red"), at(ATT, "a_red", G, r + 1))
                        dve.tensor_tensor(tmp, src, mk, ALU.add).then_inc(sem("qm_free"), 1)
                        dve.wait_ge(sem("qm_free"), at(ATT, "qm_free", G, u + 5))
                        dve.tensor_reduce(dst, tmp, AX.X, ALU.max).then_inc(sem("a_red"), 1)
                    else:
                        dve.tensor_reduce(dst, src, AX.X, ALU.max).then_inc(sem("qm_free"), 1)

            def join_maxima(g):
                G = layer * GROUPS + g
                if layer == 0:
                    dve.wait_ge(sem("a_red"), at(ATT, "a_red", G, 22))
                    dve.sem_inc(sem("mask_t_free"), 1)
                else:
                    dve.wait_ge(sem("qm_free"), at(ATT, "qm_free", G, 28))
                dve.tensor_tensor(mx[:], mx[:], mxb[:], ALU.max).then_inc(sem("a_mx"), 1)

            def low_shift(g):
                G = layer * GROUPS + g
                dve.wait_ge(sem("a_mh"), at(ATT, "a_mh", G, 1))
                dve.scalar_tensor_tensor(neg_max[32:32 + H, :], bank[4][0:H, :], -1.0, neg_max[0:H, :],
                                         ALU.mult, ALU.subtract).then_inc(sem("a_ml"), 1)

            def add_mask(g, q):
                if layer == 1:
                    return
                if q == 0:
                    dve.wait_ge(sem("mask_in"), g * 80 + 80)
                G = g
                dve.wait_ge(sem("pv_done"), at(ATT, "pv_done", G, q + 1))
                for j in range(5):
                    u = 5 * q + j
                    dve.wait_ge(sem("sc_done"), at(ATT, "sc_done", G, u + 1))
                    dve.tensor_tensor(pr[:, u % 10, :], bank[4 + u % 2][:], (mk_a if j < 4 else mk_b)[:], ALU.add)\
                        .then_inc(sem("a_sm"), 1)
                if q == QUADS - 1:
                    dve.wait_ge(sem("a_sm"), at(ATT, "a_sm", G, 22))
                    dve.sem_inc(sem("mask_free"), 1)

            def ahead(g, b):
                stats(g)
                normalise(g)
                for q in range(QUADS):
                    low_queries(g, q)
                    maxima(g, q)
                join_maxima(g)
                low_shift(g)

            def output_stats(g, t):
                hold(dve, "o_free", at(ATT, "o_free", layer * GROUPS + g, t + 7))
                dve.bn_stats(bn_o[:, t, :], tile_of(xr, g, t)).then_inc(sem("o_bn"), 1)

            def aggregate(g, t):
                hold(dve, "o_bn", at(ATT, "o_bn", layer * GROUPS + g, t + 1))
                dve.bn_aggr(mv_o[:, t, :], bn_o[:, t, :]).then_inc(sem("o_mv"), 1)

            def keep(g):
                output_stats(g, GT - 1)
                aggregate(g, GT - 2)
                aggregate(g, GT - 1)
                hold(dve, "o_mv", at(ATT, "o_mv", layer * GROUPS + g, GT))
                dve.tensor_copy(mv_all[:, bass.ds(g * GT, GT), :], mv_o[:]).then_inc(sem("kept"), 1)

            def body(g, b, n, bn_):
                G = layer * GROUPS + g
                add_mask(g, 0)
                add_mask(g, 1)
                if n is not None:
                    stats(n)
                    normalise(n)
                for q in range(2):
                    if n is not None:
                        low_queries(n, q)
                    add_mask(g, q + 2)
                    if n is not None:
                        maxima(n, q)
                if not (isinstance(g, int) and g == 0):
                    keep(g - 1)
                if n is not None:
                    low_queries(n, 2)
                if n is not None:
                    maxima(n, 2)
                dve.wait_ge(sem("pv_done"), at(ATT, "pv_done", G, QUADS + 2))
                dve.reciprocal(rc[:], bank[7][:]).then_inc(sem("a_rc"), 1)
                if n is not None:
                    low_queries(n, 3)
                for q in range(QUADS):
                    dve.wait_ge(sem("spread"), at(ATT, "spread", G, q + 1))
                    dve.tensor_tensor(attnT[:, q, :], attnT[:, q, :], bank[6 + q % 2][:], ALU.mult)\
                        .then_inc(sem("a_at"), 1)
                if n is not None:
                    maxima(n, 3)
                    join_maxima(n)
                if layer == 1:
                    dve.wait_ge(sem("a_xb"), g + 1)
                for t in range(GT):
                    dve.wait_ge(sem("o_done"), at(ATT, "o_done", G, t + 1))
                    dve.tensor_tensor(tile_of(xr, g, t), out_bank(t)[:], tile_of(xr, g, t), ALU.add)\
                        .then_inc(sem("o_free"), 1)
                    if t == 1 and n is not None:
                        low_shift(n)
                    if t >= 1:
                        output_stats(g, t - 1)
                    if t >= 2:
                        aggregate(g, t - 2)
                if n is None:
                    keep(g)
            pipelined(dve, layer, ahead, body)

        def pool_all_rstd(pool, layer):
            pool.wait_ge(sem("kept"), (layer + 1) * GROUPS)
            pool.tensor_tensor(ve_all[:], mv_all[:, :, 1], eps_c[:], ALU.add).then_inc(sem("all_ve"), 1)
            pool.wait_ge(sem("all_ve"), layer + 1)
            pool.tensor_tensor(rs_all[:], ve_all[:], expo[:], ALU.pow).then_inc(sem("all_rs"), 1)

        def doubled(eng, ahead, body):
            ahead(0, 0)
            with eng.Fori(0, GROUPS // 2 - 1) as i:
                ahead(2 * i + 1, 1)
                body(2 * i, 0)
                ahead(2 * i + 2, 0)
                body(2 * i + 1, 1)
            ahead(GROUPS - 1, 1)
            body(GROUPS - 2, 0)
            body(GROUPS - 1, 1)

        def dve_stats(dve):
            def normalise(g, par):
                for t in range(GT):
                    hold(dve, "t_tp", at(STAT, "t_tp", g, t + 1))
                    dve.tensor_scalar(fxn[:, t, :], tile_of(xr, g, t), mv_all[:, bass.ds(g * GT + t, 1), 0],
                                      rs_all[:, bass.ds(g * GT + t, 1)], ALU.subtract, ALU.mult)\
                        .then_inc(sem("t_xn"), 1)

            def convolve(g, par):
                hold(dve, "t_te", at(STAT, "t_te", g, 2 * GT))
                hold(dve, "t_cp", at(STAT, "t_cp", g, 2))
                hold(dve, "t_gs", at(STAT, "t_gs", g, 2))
                for c in range(C):
                    for n in range(2):
                        src = sxT[par][:, c, :]
                        if c == 0:
                            dve.tensor_scalar(ge[:, n, :], src, cw[:, n, c:c + 1], cb[:, n:n + 1], ALU.mult, ALU.add)\
                                .then_inc(sem("t_xc"), 1)
                        else:
                            hold(dve, "t_xc", at(STAT, "t_xc", g, 2 * c + n - 1))
                            dve.scalar_tensor_tensor(ge[:, n, :], src, cw[:, n, c:c + 1], ge[:, n, :], ALU.mult,
                                                     ALU.add).then_inc(sem("t_xc"), 1)
                for n in range(2):
                    hold(dve, "t_xc", at(STAT, "t_xc", g, 7 + n))
                    dve.bn_stats(gst[:, n, bass.ds(g, 1), :].rearrange("p a s -> p (a s)"), ge[:, n, :])\
                        .then_inc(sem("t_gs"), 1)
            dve.wait_ge(sem("all_rs"), 1)
            doubled(dve, normalise, convolve)

        def pe_stats_group(pe, g):
            for t in range(GT):
                pe.wait_ge(sem("t_xn"), at(STAT, "t_xn", g, t + 1))
                pe.wait_ge(sem("t_te"), at(STAT, "t_te", g, t + 1))
                for c in range(C):
                    mm = pe.transpose(bank[t][:, P * c:P * c + P], fxn[:, t, c::C], ident[:])
                mm.then_inc(sem("t_tp"), 1)

        def act_stats(act):
            def feature_major(g, par):
                for t in range(GT):
                    act.wait_ge(sem("t_tp"), at(STAT, "t_tp", g, t + 5))
                    act.activation(sxT[par][:, :, P * t:P * t + P], bank[t][:].rearrange("p (c n) -> p c n", c=C),
                                   ACT.Copy).then_inc(sem("t_te"), 1)

            def keep(g, par):
                for n in range(2):
                    act.wait_ge(sem("t_xc"), at(STAT, "t_xc", g, 7 + n))
                    act.activation(xc[n][:, bass.ds(g * GW, GW)], ge[:, n, :], ACT.Copy).then_inc(sem("t_cp"), 1)
            doubled(act, feature_major, keep)

        def dve_batch_norm(dve):
            dve.wait_ge(sem("t_gs"), 2 + 2 * GROUPS)
            for n in range(2):
                dve.bn_aggr(gmv[:, n, :], gst[:, n, :, :].rearrange("p g s -> p (g s)")).then_inc(sem("b_mv"), 1)
            dve.wait_ge(sem("b_rs"), 1)
            dve.tensor_tensor(gsc[:], grs[:], gam[:], ALU.mult).then_inc(sem("b_sc"), 1)
            dve.wait_ge(sem("b_sc"), 1)
            dve.tensor_tensor(gtm[:], gmv[:, :, 0], gsc[:], ALU.mult).then_inc(sem("b_sc"), 1)
            dve.wait_ge(sem("b_sc"), 2)
            dve.tensor_tensor(gbi[:], bet[:], gtm[:], ALU.subtract).then_inc(sem("b_sc"), 1)

        def pool_batch_norm(pool):
            pool.wait_ge(sem("b_mv"), 2)
            pool.tensor_tensor(gve[:], gmv[:, :, 1], eps_c[:, 0:2], ALU.add).then_inc(sem("b_ve"), 1)
            pool.wait_ge(sem("b_ve"), 1)
            pool.tensor_tensor(grs[:], gve[:], expo[:, 0:2], ALU.pow).then_inc(sem("b_rs"), 1)

        def pool_ffn_group(pool, g):
            hold(pool, "f_xn", at(FFN, "f_xn", g, GT))
            xg = xr[:, bass.ds(g * GT, GT), :]
            pool.tensor_tensor(xg, xg, bf[:].unsqueeze(1).broadcast_to([P, GT, D]), ALU.add).then_inc(sem("f_xb"), 1)
            pool.wait_ge(sem("f_xb"), at(FFN, "f_xb", g, 1))
            for t in range(GT):
                hold(pool, "f_sum", at(FFN, "f_sum", g, t + 3))
                pool.tensor_tensor(tile_of(xr, g, t), tile_of(xr, g, t), fsm[:, t % 2, :], ALU.add)\
                    .then_inc(sem("f_x"), 1)

        def pe_logits(pe, g, t):
            for n in (1, 0):
                pe.wait_ge(sem("f_top"), at(FFN, "f_top", g, 16 * t + 4 - n))
                pe.wait_ge(sem("f_ex"), at(FFN, "f_ex", g, 2 * t + 2 - n))
                if t == 0:
                    pe.wait_ge(sem("f_ge"), at(FFN, "f_ge", g, 2 - n))
                pe.matmul(bank[3 - n][:], ge[:, n, P * t:P * t + P], lw[:, n, :], start=True, stop=False)
                pe.matmul(bank[3 - n][:], one_r[0:64, :], lbr[0:64, n, :], start=False, stop=True)\
                    .then_inc(sem("lg_done"), 1)

        def pe_ffn_group(pe, g, following):
            def full(t):
                pe.wait_ge(sem("full_free"), at(FFN, "full_free", g, t + 1))
                for c in range(C):
                    mm = pe.matmul(bank[4 + t % 2][:], fxT[:, c, P * t:P * t + P], wf[:, c, :], start=(c == 0),
                                   stop=(c == C - 1))
                mm.then_inc(sem("full_done"), 1)

            def sparse(t):
                pe.wait_ge(sem("f_xs"), at(FFN, "f_xs", g, t + 1 + GT))
                pe.wait_ge(sem("f_te"), at(FFN, "f_te", g, GT + t + 1))
                for c in range(C):
                    mm = pe.transpose(bank[t % 2][:, P * c:P * c + P], fxs[:, c::C], ident[:])
                mm.then_inc(sem("f_tp"), 1)
                pe.wait_ge(sem("f_te"), at(FFN, "f_te", g, GT + t + 3))
                pe.wait_ge(sem("f_sum"), at(FFN, "f_sum", g, t + 1))
                for c in range(C):
                    mm = pe.matmul(bank[6 + t % 2][:], fxsT[:, P * c:P * c + P], wf[:, c, :], start=(c == 0),
                                   stop=(c == C - 1))
                mm.then_inc(sem("in_done"), 1)

            for t in range(GT):
                pe.wait_ge(sem("f_xn"), at(FFN, "f_xn", g, t + 1))
                pe.wait_ge(sem("f_te"), at(FFN, "f_te", g, t + 1))
                for c in range(C):
                    mm = pe.transpose(bank[t % 2][:, P * c:P * c + P], fxn[:, t, c::C], ident[:])
                mm.then_inc(sem("f_tp"), 1)
            pe.wait_ge(sem("f_te"), at(FFN, "f_te", g, GT + 2))
            for t in range(GT):
                full(t)
                if t + 1 < GT:
                    pe_logits(pe, g, t + 1)
                elif following is not None:
                    pe_logits(pe, following, 0)
                sparse(t)

        def act_gelu(act, g):
            for n in (1, 0):
                act.activation(ge[:, n, :], xc[n][:, bass.ds(g * GW, GW)], ACT.Gelu, bias=gbi[:, n:n + 1],
                               scale=gsc[:, n:n + 1]).then_inc(sem("f_ge"), 1)

        def act_ffn_group(act, g, following):
            for t in range(GT):
                act.wait_ge(sem("f_tp"), at(FFN, "f_tp", g, t + 1))
                act.activation(fxT[:, :, P * t:P * t + P], bank[t % 2][:].rearrange("p (c n) -> p c n", c=C), ACT.Copy)\
                    .then_inc(sem("f_te"), 1)
            for t in range(GT):
                for n in (1, 0):
                    u = 2 * t + 1 - n
                    act.wait_ge(sem("f_nm"), at(FFN, "f_nm", g, u + 1))
                    act.wait_ge(sem("f_top"), at(FFN, "f_top", g, 16 * t + 20 - n))
                    act.activation(ex[:, n, :], bank[3 - n][:], ACT.Exp, bias=fnm[:, n:n + 1],
                                   accum_out=fsum[:, n:n + 1]).then_inc(sem("f_ex"), 1)
                if t == GT - 1 and following is not None:
                    act_gelu(act, following)
                act.wait_ge(sem("f_tp"), at(FFN, "f_tp", g, GT + t + 1))
                act.activation(fxsT[:], bank[t % 2][:], ACT.Copy).then_inc(sem("f_te"), 1)

        def act_bias_rows(act):
            act.wait_ge(sem("bias_zero"), 2)
            act.activation(lbr[0:1, :, :], lb[0:1, :, :], ACT.Copy).then_inc(sem("bias_hi"), 1)

        def dve_bias_rows(dve):
            dve.memset(lbr[:].bitcast(F32), 0.0).then_inc(sem("bias_zero"), 1)
            dve.memset(one_r[:].bitcast(F32), 1.0).then_inc(sem("bias_zero"), 1)
            dve.wait_ge(sem("bias_hi"), 1)
            dve.tensor_tensor(lbr[32:33, :, :], lb[0:1, :, :], lbr[0:1, :, :], ALU.subtract)\
                .then_inc(sem("bias_lo"), 1)

        def dve_ffn(dve):
            def normalise(g):
                for t in range(GT):
                    hold(dve, "f_xs", at(FFN, "f_xs", g, t + 1))
                    dve.tensor_scalar(fxn[:, t, :], tile_of(xr, g, t), mv_all[:, bass.ds(g * GT + t, 1), 0],
                                      rs_all[:, bass.ds(g * GT + t, 1)], ALU.subtract, ALU.mult)\
                        .then_inc(sem("f_xn"), 1)

            def combine(g, t):
                dve.wait_ge(sem("full_free"), at(FFN, "full_free", g, t + 3))
                dve.wait_ge(sem("in_done"), at(FFN, "in_done", g, t + 1))
                dve.wait_ge(sem("f_x"), at(FFN, "f_x", g, t + 1))
                dve.tensor_tensor(fsm[:, t % 2, :], bank[6 + t % 2][:], ftmp[:, t % 2, :], ALU.add)\
                    .then_inc(sem("f_sum"), 1)

            def top(g, t, earlier):
                last = [0, 0]

                def then(n, ins):
                    steps[0] += 1
                    last[n] = steps[0]
                    ins.then_inc(sem("f_top"), 1)

                for k in range(K_TOP // 8):
                    for n in (1, 0):
                        if k == 0:
                            hold(dve, "lg_done", at(FFN, "lg_done", g, 2 * t + 2 - n))
                        else:
                            hold(dve, "f_top", at(FFN, "f_top", g, 16 + last[n]))
                        src = bank[3 - n][:] if k == 0 else Wk[:, n, 1 - k % 2, :]
                        then(n, dve.max(m8[:, n, :], src))
                    for n in (1, 0):
                        hold(dve, "f_top", at(FFN, "f_top", g, 16 + last[n]))
                        if k == 0:
                            dve.tensor_scalar(fnm[:, n:n + 1], m8[:, n, 0:1], -1.0, None, ALU.mult)\
                                .then_inc(sem("f_nm"), 1)
                        src = bank[3 - n][:] if k == 0 else Wk[:, n, 1 - k % 2, :]
                        then(n, dve.match_replace(Wk[:, n, k % 2, :], m8[:, n, :], src, GONE))
                    if k == 2 and earlier:
                        combine(*earlier)
                for n in (1, 0):
                    u = 2 * t + 1 - n
                    dve.wait_ge(sem("f_ex"), at(FFN, "f_ex", g, u + 3))
                    dve.reciprocal(frc[:, n:n + 1], fsum[:, n:n + 1]).then_inc(sem("f_rc"), 1)
                    dve.wait_ge(sem("f_top"), at(FFN, "f_top", g, 16 + last[n]))
                    dve.scalar_tensor_tensor(selv[:, n, :], Wk[:, n, 1, :], 0.9 * GONE, ex[:, n, :], ALU.is_le,
                                             ALU.mult).then_inc(sem("f_sel"), 1)
                dve.wait_ge(sem("f_rc"), at(FFN, "f_rc", g, 2 * t + 1))
                dve.wait_ge(sem("f_sel"), at(FFN, "f_sel", g, 2 * t + 1))
                dve.wait_ge(sem("f_tp"), at(FFN, "f_tp", g, GT + t))
                dve.scalar_tensor_tensor(fxs[:], selv[:, 1, :], frc[:, 1:2], fxn[:, t, :], ALU.mult, ALU.mult)\
                    .then_inc(sem("f_xs"), 1)
                dve.wait_ge(sem("f_rc"), at(FFN, "f_rc", g, 2 * t + 2))
                dve.wait_ge(sem("f_sel"), at(FFN, "f_sel", g, 2 * t + 2))
                dve.wait_ge(sem("full_done"), at(FFN, "full_done", g, t + 1))
                dve.scalar_tensor_tensor(ftmp[:, t % 2, :], bank[4 + t % 2][:], frc[:, 0:1], selv[:, 0, :],
                                         ALU.mult, ALU.mult).then_inc(sem("full_free"), 1)

            def group(g, before):
                steps[0] = 0
                normalise(g)
                top(g, 0, before)
                for t in range(1, GT):
                    top(g, t, (g, t - 1))

            steps = [0]
            group(0, None)
            with dve.Fori(1, GROUPS) as g:
                group(g, (g - 1, GT - 1))
            combine(GROUPS - 1, GT - 1)

        def sp_experts(sp):
            sp.wait_ge(sem("att1_over"), 5)
            sp.dma_start(gw[:], gate_w.rearrange("(p c) e -> p c e", c=C)).then_inc(sem("gate_in"), 16)
            for e in range(E):
                sp.dma_start(w_in_sb[:, e * C * D:(e + 1) * C * D],
                             w_in[e].rearrange("(p c) n -> p (c n)", c=C)).then_inc(sem("w_in"), 16)
                sp.dma_start(w_dn_sb[:, e * 2 * D:(e + 1) * 2 * D].rearrange("p (i n) -> p i n", i=2),
                             w_down[e].rearrange("(i p) n -> p i n", p=P)).then_inc(sem("w_in"), 16)
            for r in range(4):
                sp.wait_ge(sem(f"scattered{r}"), 16 * TILES // 4)

            def load(k, j):
                sp.dma_start(tx[:, j, :], xs_dram[bass.ds(k * P, P), :]).then_inc(sem(f"tx_in{j}"), 16)

            def store(k, j):
                sp.wait_ge(sem("e_yo"), k + 3)
                sp.dma_start(ys_dram[bass.ds(k * P, P), :], yo[:, j, :]).then_inc(sem(f"ys_out{j}"), 16)

            for k in range(4):
                if k >= 2:
                    sp.wait_ge(sem("tx_used"), k - 1)
                load(k, k % 2)
            store(0, 0)
            with sp.Fori(2, SLOT_TILES // 2) as i:
                for j in range(2):
                    sp.wait_ge(sem("tx_used"), 2 * i + j - 1)
                    load(2 * i + j, j)
                    store(2 * i + j - 3, 1 - j)
            sp.wait_ge(sem("tx_used"), SLOT_TILES - 2)
            load(SLOT_TILES - 1, 0)
            for k in range(SLOT_TILES - 4, SLOT_TILES):
                store(k, k % 2)
            for t in range(TILES):
                sp.wait_ge(sem("final"), t + 1)
                sp.dma_start(out_tiles[:, t, :], xr[:, t, :]).then_inc(sem("out_done"), 16)
            sp.wait_ge(sem("out_done"), 16 * TILES)

        def dve_gate_apply(dve, g):
            for t in range(GT):
                hold(dve, "g_tp", at(GATE, "g_tp", g, t + 1))
                dve.tensor_scalar(mxn[:, t, :], tile_of(xr, g, t), mv_all[:, bass.ds(g * GT + t, 1), 0],
                                  rs_all[:, bass.ds(g * GT + t, 1)], ALU.subtract, ALU.mult).then_inc(sem("g_xn"), 1)

        def dve_gate_keep(dve, g):
            hold(dve, "g_lg", at(GATE, "g_lg", g, 2))
            dve.tensor_copy(lgt[:, bass.ds(g * GT, GT), :], bank[4][:, 0:GT * E].rearrange("p (t e) -> p t e", e=E))\
                .then_inc(sem("g_cp"), 1)

        def dve_gate(dve):
            dve.wait_ge(sem("all_rs"), 2)
            dve_gate_apply(dve, 0)
            with dve.Fori(1, GROUPS) as g:
                dve_gate_apply(dve, g)
                dve_gate_keep(dve, g - 1)
            dve_gate_keep(dve, GROUPS - 1)

        def pe_gate_group(pe, g):
            def turn(t):
                pe.wait_ge(sem("g_xn"), at(GATE, "g_xn", g, t + 1))
                pe.wait_ge(sem("g_te"), at(GATE, "g_te", g, t + 1))
                for c in range(C):
                    mm = pe.transpose(bank[t][:, P * c:P * c + P], mxn[:, t, c::C], ident[:])
                mm.then_inc(sem("g_tp"), 1)

            turn(0)
            for t in range(GT):
                if t + 1 < GT:
                    turn(t + 1)
                pe.wait_ge(sem("g_te"), at(GATE, "g_te", g, t + 5))
                if t == 0:
                    pe.wait_ge(sem("g_cp"), at(GATE, "g_cp", g, 1))
                for c in range(C):
                    mm = pe.matmul(bank[4][:, E * t:E * t + E], mxT[:, t, P * c:P * c + P], gw[:, c, :],
                                   start=(c == 0), stop=(c == C - 1))
            mm.then_inc(sem("g_lg"), 1)

        def act_gate_group(act, g):
            for t in range(GT):
                act.wait_ge(sem("g_tp"), at(GATE, "g_tp", g, t + 5))
                if t == 0:
                    act.wait_ge(sem("g_lg"), at(GATE, "g_lg", g, 1))
                act.activation(mxT[:, t, :], bank[t][:], ACT.Copy).then_inc(sem("g_te"), 1)

        def bc(ap, n):
            return ap.unsqueeze(2).broadcast_to([P, ap.shape[1], n])

        def over(ap, n):
            return ap.unsqueeze(1).broadcast_to([P, n, ap.shape[1]])

        def pool_sort(pool):
            pool.iota(iota_e[:], pattern=[[1, E]], base=0, channel_multiplier=0,
                      allow_small_or_imprecise_dtypes=True).then_inc(sem("s_const"), 1)
            pool.iota(slot_i[:], pattern=[[1, SLOT_TILES]], base=0, channel_multiplier=0,
                      allow_small_or_imprecise_dtypes=True).then_inc(sem("s_const"), 1)
            pool.memset(ones[:], 1.0).then_inc(sem("s_const"), 1)
            pool.wait_ge(sem("s_const"), 3)
            pool.affine_select(out=tri[:], in_=ones[:], compare_op=ALU.is_gt, fill=0.0, base=0,
                               pattern=[[1, P]], channel_multiplier=-1).then_inc(sem("s_const"), 1)

        def dve_sort(dve):
            n = [0]

            def then(ins):
                n[0] += 1
                ins.then_inc(sem("s_step"), 1)
                dve.wait_ge(sem("s_step"), n[0])

            dve.wait_ge(sem("g_cp"), 1 + GROUPS)
            dve.wait_ge(sem("s_const"), 4)
            dve.tensor_reduce(top_v[:], lgt[:], AX.X, ALU.max).then_inc(sem("s_top"), 1)
            dve.wait_ge(sem("s_top"), 1)
            then(dve.tensor_tensor(below[:], lgt[:], bc(top_v[:], E), ALU.not_equal))
            then(dve.scalar_tensor_tensor(cand[:], below[:], float(E), over(iota_e[:], TILES), ALU.mult, ALU.add))
            then(dve.tensor_reduce(selx[:], cand[:], AX.X, ALU.min))
            dve.tensor_tensor(onehot[:], over(iota_e[:], TILES), bc(selx[:], E), ALU.is_equal)\
                .then_inc(sem("s_onehot"), 1)
            dve.wait_ge(sem("s_counts"), 1)
            then(dve.tensor_copy(own[:], bank[1][:, 0:TILES * E].rearrange("p (t e) -> p t e", e=E)))
            then(dve.tensor_copy(cnt[:, 0, :, :], own[:]))
            src = 0
            shift = 1
            while shift < TILES:
                then(dve.tensor_copy(cnt[:, 1 - src, 0:shift, :], cnt[:, src, 0:shift, :]))
                then(dve.tensor_tensor(cnt[:, 1 - src, shift:, :], cnt[:, src, shift:, :],
                                       cnt[:, src, 0:TILES - shift, :], ALU.add))
                src = 1 - src
                shift *= 2
            then(dve.tensor_scalar(tot[:], cnt[:, src, TILES - 1, :], float(P - 1), None, ALU.add))
            then(dve.tensor_copy(toti[:], tot[:]))
            then(dve.tensor_scalar(toti[:], toti[:], P.bit_length() - 1, None, ALU.arith_shift_right))
            then(dve.tensor_copy(tiles_f[:], toti[:]))
            then(dve.memset(start[:], 0.0))
            for e in range(E):
                then(dve.tensor_tensor(start[:, e + 1:e + 2], start[:, e:e + 1], tiles_f[:, e:e + 1], ALU.add))
            then(dve.tensor_tensor(cmp[:], bc(slot_i[:], E - 1), over(start[:, 1:E], SLOT_TILES), ALU.is_ge))
            then(dve.tensor_reduce(slot_e[:], cmp[:], AX.X, ALU.add))
            dve.tensor_copy(slot_ei[:], slot_e[:]).then_inc(sem("slot_expert"), 1)
            then(dve.tensor_tensor(prod[:], cnt[:, src, :, :], own[:], ALU.subtract))
            then(dve.tensor_tensor(rank[:], bank[0][:, 0:TILES * E].rearrange("p (t e) -> p t e", e=E), prod[:],
                                   ALU.add))
            then(dve.scalar_tensor_tensor(prod[:], over(start[:, 0:E], TILES), float(P), rank[:], ALU.mult, ALU.add))
            then(dve.tensor_tensor(rank[:], prod[:], onehot[:], ALU.mult))
            then(dve.tensor_reduce(posf[:], rank[:], AX.X, ALU.add))
            dve.tensor_copy(posi[:], posf[:]).then_inc(sem("places"), 1)
            dve.wait_ge(sem("s_exp"), 1)
            then(dve.tensor_scalar(rwe[:], rwe[:], 1.0, None, ALU.add))
            then(dve.reciprocal(rw[:], rwe[:]))
            then(dve.tensor_tensor(srs[:], rs_all[:], rw[:], ALU.mult))
            for t in range(TILES):
                if t >= 4:
                    dve.wait_ge(sem(f"scattered{t % 4}"), 16 * (t // 4))
                dve.tensor_scalar(xs[:, t % 4, :], xr[:, t, :], mv_all[:, t, 0:1], srs[:, t:t + 1], ALU.subtract,
                                  ALU.mult).then_inc(sem("s_xs"), 1)

        def pe_sort(pe):
            pe.wait_ge(sem("s_onehot"), 1)
            flat = onehot[:].rearrange("p t e -> p (t e)")
            pe.matmul(bank[0][:, 0:TILES * E], tri[:], flat, start=True, stop=True)
            pe.matmul(bank[1][:, 0:TILES * E], ones[:], flat, start=True, stop=True).then_inc(sem("s_counts"), 1)

        def pool_scatter(pool):
            pool.wait_ge(sem("places"), 1)
            pool.wait_ge(sem("slots_zeroed"), 16)
            for t in range(TILES):
                pool.wait_ge(sem("s_xs"), t + 1)
                pool.indirect_dma_start(xs_dram, bass.IndirectOffsetOnAxis(posi[:, t:t + 1], 0), xs[:, t % 4, :], None)\
                    .then_inc(sem(f"scattered{t % 4}"), 16)

        def pe_experts(pe):
            pe.wait_ge(sem("slot_expert"), 1)
            pe.wait_ge(sem("w_in"), 16 * 2 * E)

            def turn(k, j, n):
                pe.wait_ge(sem(f"tx_in{j}"), 16 * n + 16)
                pe.wait_ge(sem("e_te"), k + 1)
                for c in range(C):
                    mm = pe.transpose(bank[j][:, P * c:P * c + P], tx[:, j, c::C], ident[:])
                mm.then_inc(sem("tx_used"), 1)

            def into(k, j):
                e = pe.value_load(slot_ei[0:1, bass.ds(k, 1)], min_val=0, max_val=E - 1)
                pe.wait_ge(sem("e_te"), k + 3)
                pe.wait_ge(sem("e_hh"), k + 1)
                for c in range(C):
                    mm = pe.matmul(bank[2 + j][:], txT[:, j, P * c:P * c + P],
                                   w_in_sb[:, bass.ds(e * (C * D) + c * D, D)], start=(c == 0), stop=(c == C - 1))
                mm.then_inc(sem("e_gu"), 1)

            def turn_h(k, j):
                pe.wait_ge(sem("e_hh"), k + 3)
                pe.wait_ge(sem("e_hT"), k + 1)
                for i in range(2):
                    mm = pe.transpose(bank[4 + j][:, P * i:P * i + P], hh[:, j, P * i:P * i + P], ident[:])
                mm.then_inc(sem("e_th"), 1)

            def down(k, j):
                e = pe.value_load(slot_ei[0:1, bass.ds(k, 1)], min_val=0, max_val=E - 1)
                pe.wait_ge(sem("e_hT"), k + 3)
                pe.wait_ge(sem("e_yo"), k + 1)
                for i in range(2):
                    mm = pe.matmul(bank[6 + j][:], hT[:, j, P * i:P * i + P],
                                   w_dn_sb[:, bass.ds(e * (2 * D) + i * D, D)], start=(i == 0), stop=(i == 1))
                mm.then_inc(sem("e_dn"), 1)

            turn(0, 0, 0)
            into(0, 0)
            turn(1, 1, 0)
            with pe.Fori(0, (SLOT_TILES - 3) // 2) as i:
                into(2 * i + 1, 1)
                turn_h(2 * i, 0)
                turn(2 * i + 2, 0, i + 1)
                down(2 * i, 0)
                into(2 * i + 2, 0)
                turn_h(2 * i + 1, 1)
                turn(2 * i + 3, 1, i + 1)
                down(2 * i + 1, 1)
            last = SLOT_TILES - 1
            into(last - 1, 1)
            turn_h(last - 2, 0)
            turn(last, 0, last // 2)
            down(last - 2, 0)
            into(last, 0)
            turn_h(last - 1, 1)
            down(last - 1, 1)
            turn_h(last, 0)
            down(last, 0)

        def act_experts(act):
            def gated(k, j):
                act.wait_ge(sem("e_gu"), k + 1)
                act.activation(sg[:, j, :], bank[2 + j][:, 0:I], ACT.Silu).then_inc(sem("e_sg"), 1)

            with act.Fori(0, SLOT_TILES // 2) as i:
                gated(2 * i, 0)
                gated(2 * i + 1, 1)
            gated(SLOT_TILES - 1, 0)

        def dve_experts(dve):
            def feature_major(k, j):
                dve.wait_ge(sem("tx_used"), k + 1)
                dve.tensor_copy(txT[:, j, :], bank[j][:]).then_inc(sem("e_te"), 1)

            def product(k, j):
                dve.wait_ge(sem("e_sg"), k + 1)
                dve.tensor_tensor(hh[:, j, :], sg[:, j, :], bank[2 + j][:, I:2 * I], ALU.mult).then_inc(sem("e_hh"), 1)

            def product_turned(k, j):
                dve.wait_ge(sem("e_th"), k + 1)
                dve.tensor_copy(hT[:, j, :], bank[4 + j][:, 0:I]).then_inc(sem("e_hT"), 1)

            def outputs(k, j):
                dve.wait_ge(sem("e_dn"), k + 1)
                dve.wait_ge(sem(f"ys_out{j}"), ys_value(k, j))
                dve.tensor_copy(yo[:, j, :], bank[6 + j][:]).then_inc(sem("e_yo"), 1)

            def step(k, j):
                product_turned(k, j)
                product(k + 1, 1 - j)
                feature_major(k + 2, j)
                outputs(k, j)

            feature_major(0, 0)
            product(0, 0)
            feature_major(1, 1)
            with dve.Fori(0, (SLOT_TILES - 3) // 2) as i:
                step(2 * i, 0)
                step(2 * i + 1, 1)
            last = SLOT_TILES - 1
            step(last - 2, 0)
            product_turned(last - 1, 1)
            product(last, 0)
            outputs(last - 1, 1)
            product_turned(last, 0)
            outputs(last, 0)

        def ys_value(k, j):
            return (k - j) * 8 + 16

        def pool_gather(pool):
            pool.wait_ge(sem("ys_out0"), 16 + 16 * ((SLOT_TILES + 1) // 2))
            pool.wait_ge(sem("ys_out1"), 16 + 16 * (SLOT_TILES // 2))
            pool.wait_ge(sem("tx_used"), SLOT_TILES)
            for t in range(TILES):
                if t >= 3:
                    pool.wait_ge(sem("final"), t - 2)
                pool.indirect_dma_start(yg[:, t % 3, :], None, ys_dram, bass.IndirectOffsetOnAxis(posi[:, t:t + 1], 0))\
                    .then_inc(sem(f"gathered{t % 3}"), 16)

        def dve_final(dve):
            for t in range(TILES):
                dve.wait_ge(sem(f"gathered{t % 3}"), 16 * (t // 3 + 1))
                dve.tensor_tensor(xr[:, t, :], xr[:, t, :], yg[:, t % 3, :], ALU.add).then_inc(sem("final"), 1)

        @block.sync
        def _(sp):
            def load_kv(layer):
                w = (wk0, wv0) if layer == 0 else (wk1, wv1)
                sp.dma_start(ctx_sb[:], ctxT.rearrange("b (p c) k -> p b c k", c=C)).then_inc(sem("k_in"), 16)
                sp.dma_start(wk[:], w[0].rearrange("(p c) n -> p c n", c=C)).then_inc(sem("k_in"), 16)
                sp.dma_start(wv[:], w[1].rearrange("(p c) n -> p c n", c=C)).then_inc(sem("v_in"), 16)
                for c in range(C):
                    for j in range(4):
                        sp.dma_start(ctx_b[:, :, c, KB * j:KB * j + KB],
                                     ctxT.rearrange("b (p c) k -> p b c k", c=C)[:, :, c, KB0:]).then_inc(sem("v_in"), 16)
                if layer == 1:
                    sp.dma_start(bk[:], bk1).then_inc(sem("kv_bias_in"), 16)
                    sp.dma_start(bv[:], bv1.partition_broadcast(P)).then_inc(sem("kv_bias_in"), 16)

            def load_qo(layer):
                w = (wq0, wo0) if layer == 0 else (wq1, wo1)
                sp.dma_start(wq[:], w[0].rearrange("(p c) n -> p c n", c=C)).then_inc(sem("qo_in"), 16)
                sp.dma_start(wo[:], w[1].rearrange("(c p) n -> p c n", c=C)).then_inc(sem("qo_in"), 16)
                if layer == 1:
                    sp.dma_start(bq[:], bq1).then_inc(sem("qo_bias_in"), 16)
                    sp.dma_start(bo[:], bo1.partition_broadcast(P)).then_inc(sem("qo_bias_in"), 16)

            load_kv(0)
            sp.dma_start(xr[:, 0:GT, :], x_tiles[:, 0:GT, :]).then_inc(sem("x_in"), 16)
            load_qo(0)
            sp.wait_ge(sem("const"), 5)
            sp.dma_start(xs_dram.rearrange("(t p) d -> p t d", p=P),
                         zero_row[:].unsqueeze(1).broadcast_to([P, SLOT_TILES, D])).then_inc(sem("slots_zeroed"), 16)
            sp.wait_ge(sem("kv_over"), 4)
            def load_x(g):
                sp.wait_ge(sem("x_in"), 16 * g)
                sp.dma_start(xr[:, bass.ds(GT * g, GT), :], x_tiles[:, bass.ds(GT * g, GT), :])\
                    .then_inc(sem("x_in"), 16)

            def load_masks(b, i):
                g = b * GPB + i
                sp.wait_ge(sem("mask_t_free"), g + 1)
                sp.dma_start(mk_t[:], mask[b, 0].rearrange("(t p) k -> p t k", p=P)[:, bass.ds(GT * i, GT), :])\
                    .then_inc(sem("mask_t_in"), 16)
                sp.wait_ge(sem("mask_free"), g + 1)
                sp.dma_start(mk_a[:], maskT[b, 0:KA, bass.ds(GW * i, GW)]).then_inc(sem("mask_in"), 16)
                for j in range(4):
                    sp.dma_start(mk_b[KB * j:KB * j + KB, :], maskT[b, KB0:KEYS, bass.ds(GW * i, GW)])\
                        .then_inc(sem("mask_in"), 16)

            load_masks(0, 0)
            load_x(1)
            with sp.Fori(1, GPB) as i:
                load_x(i + 1)
                load_masks(0, i)
            with sp.Fori(0, GPB - 1) as i:
                load_x(GPB + 1 + i)
                load_masks(1, i)
            load_masks(1, GPB - 1)
            sp.sem_inc(sem("att0_over"), 1)
            sp.wait_ge(sem("att0_over"), 5)
            for n, (a, b_, g_, be_, l_, lb_) in enumerate([(so_cw, so_cb, so_g, so_be, so_lw, so_lb),
                                                           (si_cw, si_cb, si_g, si_be, si_lw, si_lb)]):
                sp.dma_start(cw[:, n, :], a).then_inc(sem("ffn_in"), 16)
                sp.dma_start(cb[:, n:n + 1], b_.rearrange("(p a) -> p a", a=1)).then_inc(sem("ffn_in"), 16)
                sp.dma_start(gam[:, n:n + 1], g_.rearrange("(p a) -> p a", a=1)).then_inc(sem("ffn_in"), 16)
                sp.dma_start(bet[:, n:n + 1], be_.rearrange("(p a) -> p a", a=1)).then_inc(sem("ffn_in"), 16)
                sp.dma_start(lw[:, n, :], l_).then_inc(sem("ffn_in"), 16)
                sp.dma_start(lb[:, n, :], lb_.partition_broadcast(P)).then_inc(sem("ffn_in"), 16)
            sp.dma_start(wf[:], w_ffn.rearrange("(p c) n -> p c n", c=C)).then_inc(sem("ffn_in"), 16)
            sp.dma_start(bf[:], b_ffn.partition_broadcast(P)).then_inc(sem("ffn_in"), 16)
            load_kv(1)
            sp.sem_inc(sem("ffn_over"), 1)
            sp.wait_ge(sem("ffn_over"), 5)
            load_qo(1)
            sp.sem_inc(sem("att1_over"), 1)
            sp_experts(sp)

        @block.gpsimd
        def _(pool):
            pool_constants(pool)
            pool_att_setup(pool, 0)
            enter_groups(pool, 0)
            pool_att(pool, 0)
            leave(pool, "att0_over", "a_rl", GROUPS)
            pool_all_rstd(pool, 0)
            pool_batch_norm(pool)
            with pool.Fori(0, GROUPS) as g:
                pool_ffn_group(pool, g)
            leave(pool, "ffn_over", "f_x", 2 + 8 * 4)
            pool_att_setup(pool, 1)
            enter_groups(pool, 1)
            pool_att(pool, 1)
            leave(pool, "att1_over", "a_xb", 8)
            pool_all_rstd(pool, 1)
            pool.wait_ge(sem("att1_over"), 5)
            pool_sort(pool)
            pool_scatter(pool)
            pool_gather(pool)

        @block.tensor
        def _(pe):
            pe_kv(pe, 0)
            pe_att_start(pe, 0)
            pe_att(pe, 0)
            leave(pe, "att0_over", "o_done", GROUPS * GT)
            pe.sem_inc(sem("t_tp"), 4)
            pe.wait_ge(sem("att0_over"), 5)
            pe.wait_ge(sem("ffn_in"), 14 * 16)
            with pe.Fori(0, GROUPS) as g:
                pe_stats_group(pe, g)
            pe.wait_ge(sem("bias_lo"), 1)
            pe_logits(pe, 0, 0)
            with pe.Fori(0, GROUPS - 1) as g:
                pe_ffn_group(pe, g, g + 1)
            pe_ffn_group(pe, GROUPS - 1, None)
            leave(pe, "ffn_over", "in_done", 8 * 4)
            pe.wait_ge(sem("ffn_over"), 5)
            pe_kv(pe, 1)
            pe_att_start(pe, 1)
            pe_att(pe, 1)
            leave(pe, "att1_over", "o_done", 2 * GROUPS * GT)
            pe.wait_ge(sem("att1_over"), 5)
            pe.sem_inc(sem("g_tp"), 4)
            pe.sem_inc(sem("g_lg"), 1)
            pe.wait_ge(sem("gate_in"), 16)
            with pe.Fori(0, GROUPS) as g:
                pe_gate_group(pe, g)
            pe_sort(pe)
            pe_experts(pe)

        @block.scalar
        def _(act):
            act.sem_inc(sem("kT_free"), 2)
            act.sem_inc(sem("a_te"), 2)
            act_kv(act, 0)
            enter_groups(act, 0)
            act_att(act, 0)
            leave(act, "att0_over", "a_rh", GROUPS)
            act.sem_inc(sem("t_te"), 4)
            act.sem_inc(sem("t_cp"), 2)
            act.sem_inc(sem("f_te"), 2)
            act.wait_ge(sem("att0_over"), 5)
            act.wait_ge(sem("ffn_in"), 14 * 16)
            act_bias_rows(act)
            act_stats(act)
            act.wait_ge(sem("b_sc"), 3)
            act.wait_ge(sem("t_cp"), 2 + 2 * GROUPS)
            act_gelu(act, 0)
            with act.Fori(0, GROUPS - 1) as g:
                act_ffn_group(act, g, g + 1)
            act_ffn_group(act, GROUPS - 1, None)
            leave(act, "ffn_over", "f_te", 2 + 8 * 8)
            act.wait_ge(sem("ffn_over"), 5)
            act_kv(act, 1)
            enter_groups(act, 1)
            act_att(act, 1)
            leave(act, "att1_over", "a_rh", 2 * GROUPS)
            act.sem_inc(sem("g_te"), 4)
            act.wait_ge(sem("att1_over"), 5)
            with act.Fori(0, GROUPS) as g:
                act_gate_group(act, g)
            act.wait_ge(sem("s_top"), 1)
            act.activation(rwe[:], top_v[:], ACT.Exp, scale=-1.0).then_inc(sem("s_exp"), 1)
            act_experts(act)

        @block.vector
        def _(dve):
            dve.sem_inc(sem("k_split"), 2)
            dve.sem_inc(sem("v_free"), 2)
            dve.sem_inc(sem("qm_free"), 4)
            dve.sem_inc(sem("o_free"), 6)
            dve.sem_inc(sem("a_raw"), 1)
            dve.sem_inc(sem("mask_t_free"), 1)
            dve.sem_inc(sem("a_sm"), 2)
            dve.sem_inc(sem("a_red"), 2)
            dve.sem_inc(sem("a_at"), 1)
            dve.sem_inc(sem("mask_free"), 1)
            dve_kv(dve, 0)
            enter_groups(dve, 0)
            dve_att(dve, 0)
            leave(dve, "att0_over", "kept", GROUPS)
            dve.sem_inc(sem("t_gs"), 2)
            dve.sem_inc(sem("f_top"), 16)
            dve.sem_inc(sem("f_ex"), 2)
            dve.sem_inc(sem("full_free"), 2)
            dve.sem_inc(sem("f_x"), 2)
            dve.sem_inc(sem("f_xs"), 4)
            dve.sem_inc(sem("f_sum"), 2)
            dve.wait_ge(sem("att0_over"), 5)
            dve.wait_ge(sem("ffn_in"), 14 * 16)
            dve_bias_rows(dve)
            dve_stats(dve)
            dve_batch_norm(dve)
            dve_ffn(dve)
            leave(dve, "ffn_over", "f_sum", 2 + 8 * 4)
            dve.wait_ge(sem("ffn_over"), 5)
            dve_kv(dve, 1)
            enter_groups(dve, 1)
            dve_att(dve, 1)
            leave(dve, "att1_over", "kept", 2 * GROUPS)
            dve.sem_inc(sem("ys_out0"), 16)
            dve.sem_inc(sem("ys_out1"), 16)
            dve.sem_inc(sem("g_cp"), 1)
            dve.sem_inc(sem("e_te"), 2)
            dve.sem_inc(sem("e_hh"), 2)
            dve.sem_inc(sem("e_hT"), 2)
            dve.sem_inc(sem("e_yo"), 2)
            dve.wait_ge(sem("att1_over"), 5)
            dve_gate(dve)
            dve_sort(dve)
            dve_experts(dve)
            dve_final(dve)


_INS = ["x", "ctxT", "mask", "maskT", "wq0", "wk0", "wv0", "wo0", "w_ffn", "b_ffn", "so_cw", "so_cb", "so_g", "so_be",
        "so_lw", "so_lb", "si_cw", "si_cb", "si_g", "si_be", "si_lw", "si_lb", "wq1", "bq1", "wk1", "bk1", "wv1", "bv1",
        "wo1", "bo1", "gate_w", "w_in", "w_down"]


def kernel(**inputs):
    import numpy as _np
    import concourse.bacc as _bacc
    from concourse import mybir as _mybir
    from concourse.bass_utils import run_bass_kernel_spmd as _run

    a = {k: _np.asarray(v) for k, v in inputs.items()}
    f, t = "L0_ffn_", "L1_xattn_"
    given = dict(
        x=a["x"], ctxT=a["ctx_1024"].transpose(0, 2, 1), mask=a["mask_Bx1xSxS2_ff0"],
        maskT=a["mask_Bx1xSxS2_ff0"][:, 0].transpose(0, 2, 1),
        wq0=a["L0_xattn_wq"].reshape(D, D), wk0=a["L0_xattn_wk"].reshape(D, D), wv0=a["L0_xattn_wv"].reshape(D, D),
        wo0=a["L0_xattn_wo"].reshape(D, D), w_ffn=a[f + "weight"], b_ffn=a[f + "bias"],
        so_cw=a[f + "so_conv_w"], so_cb=a[f + "so_conv_b"], so_g=a[f + "so_gamma"], so_be=a[f + "so_beta"],
        so_lw=a[f + "so_lin_w"].T, so_lb=a[f + "so_lin_b"], si_cw=a[f + "si_conv_w"], si_cb=a[f + "si_conv_b"],
        si_g=a[f + "si_gamma"], si_be=a[f + "si_beta"], si_lw=a[f + "si_lin_w"].T, si_lb=a[f + "si_lin_b"],
        wq1=a[t + "W_Q"].T, bq1=a[t + "b_Q"].reshape(C, P).T, wk1=a[t + "W_K"].T, bk1=a[t + "b_K"].reshape(C, P).T, wv1=a[t + "W_V"].T,
        bv1=a[t + "b_V"], wo1=a[t + "W_O"].T, bo1=a[t + "b_O"], gate_w=a["L1_ffn_gate_w"].T,
        w_in=_np.concatenate([a["L1_ffn_w_gate"], a["L1_ffn_w_up"]], axis=1).transpose(0, 2, 1),
        w_down=a["L1_ffn_w_down"].transpose(0, 2, 1))
    nc = _bacc.Bacc("TRN2", target_bir_lowering=False, num_devices=1)
    arrays, args = {}, []
    for name in _INS:
        v = _np.ascontiguousarray(given[name])
        arrays[f"in_{name}"] = v
        args.append(nc.dram_tensor(f"in_{name}", v.shape, _mybir.dt.from_np(v.dtype), kind="ExternalInput").ap())
    args.append(nc.dram_tensor("out_x", (B, S, D), F32, kind="ExternalOutput").ap())
    program(nc, *args)
    r = _run(nc, [arrays], core_ids=[0])
    return r.results[0]["out_x"]
```
